# Optimizing a Trainium2 kernel written in Bass

```python
import numpy as np
import jax
import jax.numpy as jnp

def _softmax(x, axis=-1):
    return jax.nn.softmax(x, axis=axis)

def _gelu(x):
    return jax.nn.gelu(x, approximate=True)

def _silu(x):
    return jax.nn.silu(x)

def _sigmoid(x):
    return jax.nn.sigmoid(x)

def _layernorm(x, axis=-1, eps=1e-05):
    m = jnp.mean(x, axis=axis, keepdims=True)
    v = jnp.var(x, axis=axis, keepdims=True)
    return (x - m) / jnp.sqrt(v + eps)

def _scatter_add(tgt, idx, src, axis=0):
    return tgt.at[idx].add(src)

def _segment_sum(src, seg, n):
    return jax.ops.segment_sum(src, seg, n)
kernel_name = 'mk_gps_d1_gnn_r8_fda3bc'

def setup_inputs(seed: int=0):
    np.random.seed(seed)
    _w = jnp.asarray

    def _rec_inputs():
        import jax
        import jax.numpy as jnp
        _gk = jax.random.key(seed)
        x = -0.000124 + 1 * jax.random.normal(jax.random.fold_in(_gk, 1), (6250, 256), jnp.float32)
        src = jax.random.randint(jax.random.fold_in(_gk, 2), (200000,), 0, 6250, jnp.int32)
        dst = jax.random.randint(jax.random.fold_in(_gk, 3), (200000,), 0, 6250, jnp.int32)
        _o = jnp.argsort(dst, stable=True)
        src = src[_o]
        dst = dst[_o]
        edge_weight = jax.random.uniform(jax.random.fold_in(_gk, 12), (200000,), jnp.float32, 0.0, 0.999999)
        return (x, src, dst, edge_weight)
    x, src, dst, edge_weight = _rec_inputs()

    def _L0_gnn_setup():
        import jax, jax.numpy as jnp
        import numpy as np
        N_NODES = 18870
        N_EDGES = 150000
        DIM = 256
        EPS = 1e-05

        def _layer_norm(x, g, b):
            mu = jnp.mean(x, axis=-1, keepdims=True)
            var = jnp.mean(jnp.square(x - mu), axis=-1, keepdims=True)
            return (x - mu) * jax.lax.rsqrt(var + EPS) * g + b

        def _gcn_conv(x, edge_index, edge_weight, W, b):
            n = x.shape[0]
            row, col = (edge_index[0], edge_index[1])
            loop = jnp.arange(n, dtype=row.dtype)
            row = jnp.concatenate([row, loop])
            col = jnp.concatenate([col, loop])
            ew = jnp.concatenate([edge_weight, jnp.ones((n,), dtype=x.dtype)])
            deg = jax.ops.segment_sum(ew, col, num_segments=n)
            dis = jnp.where(deg > 0, jax.lax.rsqrt(jnp.where(deg > 0, deg, 1.0)), 0.0)
            norm = dis[row] * ew * dis[col]
            h = x @ W.T
            msg = h[row] * norm[:, None]
            out = jax.ops.segment_sum(msg, col, num_segments=n)
            return out + b

        def _block(x, edge_index, edge_weight, g, bln, W, b):
            h = _layer_norm(x, g, bln)
            h = _gcn_conv(h, edge_index, edge_weight, W, b)
            h = jax.nn.relu(h)
            return x + h
        key = jax.random.key(seed)
        ks = jax.random.split(key, 8)
        s = 0.05
        return {'x': jax.random.normal(ks[0], (N_NODES, DIM), dtype=jnp.float32), 'edge_index': jax.random.randint(ks[1], (2, N_EDGES), 0, N_NODES, dtype=jnp.int64) if jax.config.jax_enable_x64 else jax.random.randint(ks[1], (2, N_EDGES), 0, N_NODES).astype(jnp.int32), 'edge_weight': jax.random.uniform(ks[2], (N_EDGES,), dtype=jnp.float32), 'ln6_g': jnp.ones((DIM,), jnp.float32), 'ln6_b': jnp.zeros((DIM,), jnp.float32), 'W6': jax.random.normal(ks[3], (DIM, DIM), jnp.float32) * s, 'b6': jnp.zeros((DIM,), jnp.float32), 'ln7_g': jnp.ones((DIM,), jnp.float32), 'ln7_b': jnp.zeros((DIM,), jnp.float32), 'W7': jax.random.normal(ks[4], (DIM, DIM), jnp.float32) * s, 'b7': jnp.zeros((DIM,), jnp.float32), 'Wp': jax.random.normal(ks[5], (DIM, DIM), jnp.float32) * s, 'bp': jnp.zeros((DIM,), jnp.float32)}
    _L0_gnn_all = _L0_gnn_setup()
    _L0_gnn_in = {k: v for k, v in _L0_gnn_all.items() if k in ('ln6_g', 'ln6_b', 'W6', 'b6', 'ln7_g', 'ln7_b', 'W7', 'b7', 'Wp', 'bp')}
    del _L0_gnn_all

    def _L0_mix_setup():
        import jax, jax.numpy as jnp
        import numpy as np
        NHEAD = 8
        ATT_EPS = 1e-06
        LN_EPS = 1e-05

        def _layernorm(x, g, b):
            mu = jnp.mean(x, axis=-1, keepdims=True)
            var = jnp.mean(jnp.square(x - mu), axis=-1, keepdims=True)
            return (x - mu) * jax.lax.rsqrt(var + LN_EPS) * g + b
        key = jax.random.key(seed)
        ks = jax.random.split(key, 7)
        N, L, C = (4, 2048, 256)
        s = 1.0 / np.sqrt(C)
        return {'x': jax.random.normal(ks[0], (N, L, C), jnp.float32), 'Wq': jax.random.normal(ks[1], (C, C), jnp.float32) * s, 'Wk': jax.random.normal(ks[2], (C, C), jnp.float32) * s, 'Wv': jax.random.normal(ks[3], (C, C), jnp.float32) * s, 'Wm': jax.random.normal(ks[4], (C, C), jnp.float32) * s, 'W1': jax.random.normal(ks[5], (2 * C, 2 * C), jnp.float32) * (1.0 / np.sqrt(2 * C)), 'W2': jax.random.normal(ks[6], (2 * C, C), jnp.float32) * (1.0 / np.sqrt(2 * C)), 'g1': jnp.ones((C,), jnp.float32), 'b1': jnp.zeros((C,), jnp.float32), 'g2': jnp.ones((C,), jnp.float32), 'b2': jnp.zeros((C,), jnp.float32)}
    _L0_mix_all = _L0_mix_setup()
    _L0_mix_in = {k: v for k, v in _L0_mix_all.items() if k in ('Wq', 'Wk', 'Wv', 'Wm', 'W1', 'W2', 'g1', 'b1', 'g2', 'b2')}
    del _L0_mix_all

    def _L0_ffn_setup():
        import jax, jax.numpy as jnp
        import numpy as np
        B, S, D, E, H, K = (4, 512, 256, 8, 512, 2)
        key = jax.random.key(seed)
        ks = jax.random.split(key, 6)
        x = jax.random.normal(ks[0], (B, S, D), jnp.float32)
        Wg = jax.random.normal(ks[1], (D, E), jnp.float32) * 0.02
        bg = jnp.zeros((E,), jnp.float32)
        W1 = jax.random.normal(ks[2], (E, D, H), jnp.float32) * 0.02
        b1 = jnp.zeros((E, H), jnp.float32)
        W2 = jax.random.normal(ks[3], (E, H, D), jnp.float32) * 0.02
        b2 = jnp.zeros((E, D), jnp.float32)
        return {'x': x, 'Wg': Wg, 'bg': bg, 'W1': W1, 'b1': b1, 'W2': W2, 'b2': b2}
    _L0_ffn_all = _L0_ffn_setup()
    _L0_ffn_in = {k: v for k, v in _L0_ffn_all.items() if k in ('Wg', 'bg', 'W1', 'b1', 'W2', 'b2')}
    del _L0_ffn_all
    return {'x': x, 'src': src, 'dst': dst, 'edge_weight': edge_weight, 'L0_gnn_ln6_g': _L0_gnn_in['ln6_g'], 'L0_gnn_ln6_b': _L0_gnn_in['ln6_b'], 'L0_gnn_W6': _L0_gnn_in['W6'], 'L0_gnn_b6': _L0_gnn_in['b6'], 'L0_gnn_ln7_g': _L0_gnn_in['ln7_g'], 'L0_gnn_ln7_b': _L0_gnn_in['ln7_b'], 'L0_gnn_W7': _L0_gnn_in['W7'], 'L0_gnn_b7': _L0_gnn_in['b7'], 'L0_gnn_Wp': _L0_gnn_in['Wp'], 'L0_gnn_bp': _L0_gnn_in['bp'], 'L0_mix_Wq': _L0_mix_in['Wq'], 'L0_mix_Wk': _L0_mix_in['Wk'], 'L0_mix_Wv': _L0_mix_in['Wv'], 'L0_mix_Wm': _L0_mix_in['Wm'], 'L0_mix_W1': _L0_mix_in['W1'], 'L0_mix_W2': _L0_mix_in['W2'], 'L0_mix_g1': _L0_mix_in['g1'], 'L0_mix_b1': _L0_mix_in['b1'], 'L0_mix_g2': _L0_mix_in['g2'], 'L0_mix_b2': _L0_mix_in['b2'], 'L0_ffn_Wg': _L0_ffn_in['Wg'], 'L0_ffn_bg': _L0_ffn_in['bg'], 'L0_ffn_W1': _L0_ffn_in['W1'], 'L0_ffn_b1': _L0_ffn_in['b1'], 'L0_ffn_W2': _L0_ffn_in['W2'], 'L0_ffn_b2': _L0_ffn_in['b2']}

def reference(x, src, dst, edge_weight, L0_gnn_ln6_g, L0_gnn_ln6_b, L0_gnn_W6, L0_gnn_b6, L0_gnn_ln7_g, L0_gnn_ln7_b, L0_gnn_W7, L0_gnn_b7, L0_gnn_Wp, L0_gnn_bp, L0_mix_Wq, L0_mix_Wk, L0_mix_Wv, L0_mix_Wm, L0_mix_W1, L0_mix_W2, L0_mix_g1, L0_mix_b1, L0_mix_g2, L0_mix_b2, L0_ffn_Wg, L0_ffn_bg, L0_ffn_W1, L0_ffn_b1, L0_ffn_W2, L0_ffn_b2):
    import jax
    import jax.numpy as jnp

    def _L0_gnn_ref(x, edge_index, edge_weight, ln6_g, ln6_b, W6, b6, ln7_g, ln7_b, W7, b7, Wp, bp):
        import jax, jax.numpy as jnp
        import numpy as np
        N_NODES = 18870
        N_EDGES = 150000
        DIM = 256
        EPS = 1e-05

        def _layer_norm(x, g, b):
            mu = jnp.mean(x, axis=-1, keepdims=True)
            var = jnp.mean(jnp.square(x - mu), axis=-1, keepdims=True)
            return (x - mu) * jax.lax.rsqrt(var + EPS) * g + b

        def _gcn_conv(x, edge_index, edge_weight, W, b):
            n = x.shape[0]
            row, col = (edge_index[0], edge_index[1])
            loop = jnp.arange(n, dtype=row.dtype)
            row = jnp.concatenate([row, loop])
            col = jnp.concatenate([col, loop])
            ew = jnp.concatenate([edge_weight, jnp.ones((n,), dtype=x.dtype)])
            deg = jax.ops.segment_sum(ew, col, num_segments=n)
            dis = jnp.where(deg > 0, jax.lax.rsqrt(jnp.where(deg > 0, deg, 1.0)), 0.0)
            norm = dis[row] * ew * dis[col]
            h = x @ W.T
            msg = h[row] * norm[:, None]
            out = jax.ops.segment_sum(msg, col, num_segments=n)
            return out + b

        def _block(x, edge_index, edge_weight, g, bln, W, b):
            h = _layer_norm(x, g, bln)
            h = _gcn_conv(h, edge_index, edge_weight, W, b)
            h = jax.nn.relu(h)
            return x + h
        x = _block(x, edge_index, edge_weight, ln6_g, ln6_b, W6, b6)
        x = _block(x, edge_index, edge_weight, ln7_g, ln7_b, W7, b7)
        return x @ Wp.T + bp

    def _L0_mix_ref(x, Wq, Wk, Wv, Wm, W1, W2, g1, b1, g2, b2):
        import jax, jax.numpy as jnp
        import numpy as np
        NHEAD = 8
        ATT_EPS = 1e-06
        LN_EPS = 1e-05

        def _layernorm(x, g, b):
            mu = jnp.mean(x, axis=-1, keepdims=True)
            var = jnp.mean(jnp.square(x - mu), axis=-1, keepdims=True)
            return (x - mu) * jax.lax.rsqrt(var + LN_EPS) * g + b
        N, L, C = x.shape
        H = NHEAD
        D = C // H
        q = (x @ Wq).reshape(N, L, H, D)
        k = (x @ Wk).reshape(N, L, H, D)
        v = (x @ Wv).reshape(N, L, H, D)
        Q = jax.nn.elu(q) + 1.0
        K = jax.nn.elu(k) + 1.0
        v = v / L
        KV = jnp.einsum('nshd,nshv->nhdv', K, v)
        Z = 1.0 / (jnp.einsum('nlhd,nhd->nlh', Q, K.sum(axis=1)) + ATT_EPS)
        msg = jnp.einsum('nlhd,nhdv,nlh->nlhv', Q, KV, Z) * L
        msg = msg.reshape(N, L, C) @ Wm
        msg = _layernorm(msg, g1, b1)
        h = jnp.concatenate([x, msg], axis=-1) @ W1
        h = jax.nn.relu(h) @ W2
        msg = _layernorm(h, g2, b2)
        return x + msg

    def _L0_ffn_ref(x, Wg, bg, W1, b1, W2, b2):
        import jax, jax.numpy as jnp
        import numpy as np
        B, S, D, E, H, K = (4, 512, 256, 8, 512, 2)
        Bv, Sv, Dv = x.shape
        gate_scores = x @ Wg + bg
        _, idx = jax.lax.top_k(gate_scores, K)
        mask = jax.nn.one_hot(idx, E, dtype=x.dtype).sum(axis=-2)
        xf = x.reshape(-1, Dv)
        mf = mask.reshape(-1, E)
        h = jax.nn.gelu(jnp.einsum('td,edh->teh', xf, W1) + b1[None], approximate=False)
        y = jnp.einsum('teh,ehd->ted', h, W2) + b2[None]
        out = jnp.einsum('ted,te->td', y, mf)
        return out.reshape(Bv, Sv, Dv)
    edge_index = jnp.stack([src, dst])
    xn = _layernorm(x, axis=-1)
    x = x + _L0_gnn_ref(xn, edge_index, edge_weight, L0_gnn_ln6_g, L0_gnn_ln6_b, L0_gnn_W6, L0_gnn_b6, L0_gnn_ln7_g, L0_gnn_ln7_b, L0_gnn_W7, L0_gnn_b7, L0_gnn_Wp, L0_gnn_bp) + _L0_mix_ref(xn[None], L0_mix_Wq, L0_mix_Wk, L0_mix_Wv, L0_mix_Wm, L0_mix_W1, L0_mix_W2, L0_mix_g1, L0_mix_b1, L0_mix_g2, L0_mix_b2)[0]
    x = x + _L0_ffn_ref(_layernorm(x, axis=-1)[None], L0_ffn_Wg, L0_ffn_bg, L0_ffn_W1, L0_ffn_b1, L0_ffn_W2, L0_ffn_b2)[0]
    return x

_drawn_inputs = setup_inputs


def setup_inputs(seed=0):
    import zlib

    import numpy as np

    out = dict(_drawn_inputs(seed))
    spreads = {'L0_gnn_ln6_g': (1.0, 0.6),
     'L0_gnn_ln6_b': (0.0, 0.32),
     'L0_gnn_b6': (0.0, 0.314),
     'L0_gnn_ln7_g': (1.0, 0.6),
     'L0_gnn_ln7_b': (0.0, 0.38),
     'L0_gnn_b7': (0.0, 0.321),
     'L0_gnn_bp': (0.0, 0.1),
     'L0_mix_g1': (1.0, 0.2),
     'L0_mix_b1': (0.0, 0.1),
     'L0_mix_g2': (1.0, 0.2),
     'L0_mix_b2': (0.0, 0.1),
     'L0_ffn_bg': (0.0, 0.1),
     'L0_ffn_b1': (0.0, 0.548),
     'L0_ffn_b2': (0.0, 0.1)}
    factors = {}
    for name, (base, spread) in spreads.items():
        noise = np.random.default_rng([zlib.crc32(name.encode()), seed]).standard_normal(out[name].shape)
        drawn = base * np.exp(spread * noise) if base else spread * noise
        out[name] = jnp.asarray(drawn.astype(out[name].dtype))
    for name, factor in factors.items():
        out[name] = (out[name] * factor).astype(out[name].dtype)
    return out
```

```python
from contextlib import ExitStack

import numpy as np

import concourse.bass as bass
from concourse import mybir

ALU = mybir.AluOpType
ACT = mybir.ActivationFunctionType
AX = mybir.AxisListType
F32 = mybir.dt.float32
I32 = mybir.dt.int32

P = 128
N_NODES, N_EDGES, D = 6250, 200000, 256
KB = D // P
W = -(-N_NODES // P)
NCH = -(-N_EDGES // P)
U = 4
PIECES = 8
STATIC = U * PIECES
GSLOTS = 16
SSLOTS = 8
NCOL = -(-(NCH + STATIC + 2 * U) // 8) * 8
RB = -(-NCH // P)
REST_FROM = NCOL
HEADS, HD = 8, 32
HPB = P // HD
NE, HID = 8, 512
HBLK = HID // P
EPS = 1e-5
ATT_EPS = 1e-6
DEGU = 8
DEG_STEPS = -(-NCH // DEGU)
DEG_STEPS += DEG_STEPS % 2
RSQRT_BITS = 0x5F3759DF
NEWTON = 3
LN_LINKS = 5 + 3 * NEWTON
WEIGHT_LOADS = 20
N_CONSTS = 15
assert W % 2 == 1 and DEG_STEPS * DEGU <= NCOL


class Chain:

    def __init__(self, eng, sem, per, turn):
        self.eng, self.sem, self.per, self.turn, self.n = eng, sem, per, turn, 0

    def link(self, ins):
        self.n += 1
        ins.then_inc(self.sem, 1)
        self.eng.wait_ge(self.sem, self.turn * self.per + self.n)


def gps_kernel(nc, x, src_cols, dst_cols, ew_cols, dst_rows, vecs, W6T, W7T, WpT, Wq, Wk, Wv, Wm, W1, W2,
               ln_cols, mix_cols, Wg, bg, eW1, eb1, eW2, eb2, out):
    with ExitStack() as ctx:
        def sb(name, shape, dt=F32):
            return ctx.enter_context(nc.sbuf_tensor(name, shape, dt))

        sems = {}

        class Sems:
            def __getitem__(self, name):
                if name not in sems:
                    sems[name] = ctx.enter_context(nc.semaphore(name))
                return sems[name]

        s = Sems()
        dve_, act_, pe_, pool_, sp_ = nc.vector, nc.scalar, nc.tensor, nc.gpsimd, nc.sync

        xn_d = nc.dram_tensor("xn_d", [(W + 1) * P, D], F32).ap()
        h1_d = nc.dram_tensor("h1_d", [(W + 1) * P, D], F32).ap()
        h2_d = nc.dram_tensor("h2_d", [(W + 2) * P, D], F32).ap()
        x1_d = nc.dram_tensor("x1_d", [(W + 1) * P, D], F32).ap()
        r_d = nc.dram_tensor("r_d", [(W + 1) * P, D], F32).ap()

        def rows(table, block):
            return table[bass.ds(block * P, P), :]

        ident = sb("ident", [P, P])
        ones_row = sb("ones_row", [1, P])
        zero_tile = sb("zero_tile", [P, D])
        iota_p = sb("iota_p", [P, P])
        iota_w = sb("iota_w", [P, W])
        win_first = sb("win_first", [P, W])
        chunk_id = sb("chunk_id", [P, RB])
        headmask = sb("headmask", [P, HPB])
        lowtri = sb("lowtri", [P, NE, NE])
        valid = sb("valid", [P, W])
        src1 = sb("src1", [P, NCOL], I32)
        src2 = sb("src2", [P, NCOL], I32)
        dst_f = sb("dst_f", [P, NCOL])
        ew = sb("ew", [P, NCOL])
        w6 = sb("w6", [P, KB, D]); w7 = sb("w7", [P, KB, D]); wp = sb("wp", [P, KB, D])
        wq = sb("wq", [P, KB, D]); wk = sb("wk", [P, KB, D]); wv = sb("wv", [P, KB, D]); wm = sb("wm", [P, KB, D])
        w1 = sb("w1", [P, 2 * KB, HID]); w2 = sb("w2", [P, HBLK, D])
        lncol = sb("lncol", [P, 4, KB])
        mixcol = sb("mixcol", [P, 2, KB])
        vec = sb("vec", [P, 6, D])
        hb = sb("hb", [1, 2, D])
        w1bias = sb("w1bias", [P, HBLK])
        wg = sb("wg", [P, KB, NE]); bgr = sb("bgr", [P, NE])
        ew1 = sb("ew1", [P, NE, KB, HID]); ew2 = sb("ew2", [P, NE, HBLK, D])
        eb1c = sb("eb1c", [P, NE, HBLK]); eb2r = sb("eb2r", [NE, D])
        tab = sb("tab", [1, 7, W], I32)
        dis = sb("dis", [P, W + 1])
        idx_s = sb("idx_s", [P, GSLOTS], I32); idx_r = sb("idx_r", [P, U], I32)
        gs = sb("gs", [P, GSLOTS, D]); gr = sb("gr", [P, U, D])
        ss = sb("ss", [P, SSLOTS, P]); sr = sb("sr", [P, U, P])
        iw = sb("iw", [P, P])
        hself = sb("hself", [P, D])
        kvx = sb("kvx", [P, KB, P + HPB])
        t_a = [sb(f"t_a{i}", [P, D]) for i in range(2)]
        t_b = [sb(f"t_b{i}", [P, D]) for i in range(2)]
        t_c = [sb(f"t_c{i}", [P, D]) for i in range(2)]
        xT = sb("xT", [P, KB, P]); zT = sb("zT", [P, KB, P]); mT = sb("mT", [P, KB, P]); nT = sb("nT", [P, KB, P])
        u1 = sb("u1", [P, D]); u2 = sb("u2", [P, D]); u3 = sb("u3", [P, D]); u4 = sb("u4", [P, D]); u5 = sb("u5", [P, D])
        u6 = sb("u6", [P, D]); u7 = sb("u7", [P, D]); u8 = sb("u8", [P, D])
        vx = sb("vx", [P, KB, P + 1])
        hT = [sb(f"hT{i}", [P, HBLK, P]) for i in range(2)]
        st = sb("st", [P, 6]); mv = sb("mv", [P, 2]); rstd = sb("rstd", [P, 4])
        st2 = sb("st2", [P, 6]); mv2 = sb("mv2", [P, 2]); rstd2 = sb("rstd2", [P, 4])
        zden = sb("zden", [P, KB, HPB]); zrec = sb("zrec", [P, KB, HPB])
        lg = sb("lg", [P, NE]); cmp1 = sb("cmp1", [P, NE, NE]); cmp2 = sb("cmp2", [P, NE, NE]); rank = sb("rank", [P, NE])
        mask_n = sb("mask_n", [P, NE]); mask_c = sb("mask_c", [P, NE]); maskT = sb("maskT", [NE, P])

        bank = [ctx.enter_context(nc.psum_tensor(f"bank{i}", [P, 512], F32)) for i in range(8)]

        def half(b, n=P):
            return bank[b][:, 0:KB * n].rearrange("p (k n) -> p k n", k=KB)

        acc = bank[0][:, 0:D]

        def wide(b):
            return bank[b][:, 0:D]

        def col(ap, shape):
            return ap.to_broadcast(shape)

        flat_gs = gs[:, :, :].rearrange("p a b -> p (a b)")
        drow_i = flat_gs[:, 0:RB * P].bitcast(I32).rearrange("p (b e) -> p b e", b=RB)
        drow_f = flat_gs[:, RB * P:2 * RB * P].rearrange("p (b e) -> p b e", b=RB)
        flat_e1 = ew1[:, :, :, :].rearrange("p a b c -> p (a b c)")
        flat_e2 = ew2[:, :, :, :].rearrange("p a b c -> p (a b c)")
        dst_hi = flat_e2[:, 0:NCOL]
        dst_lo = flat_e2[:, NCOL:2 * NCOL]
        dst_i = flat_e2[:, 2 * NCOL:3 * NCOL].bitcast(I32)
        tmp_i = flat_e2[:, 3 * NCOL:4 * NCOL].bitcast(I32)
        touch = [flat_e1[:, i * W * RB:(i + 1) * W * RB].rearrange("p (w b) -> p w b", w=W) for i in range(3)]
        at = 3 * W * RB
        oh_node = [flat_e1[:, at + b * DEGU * P:at + (b + 1) * DEGU * P].rearrange("p (c n) -> p c n", c=DEGU)
                   for b in range(2)]
        at += 2 * DEGU * P
        oh_win = [flat_e1[:, at + b * DEGU * W:at + (b + 1) * DEGU * W].rearrange("p (c n) -> p c n", c=DEGU)
                  for b in range(2)]
        at += 2 * DEGU * W
        range_part = flat_e1[:, at:at + 2 * W]
        range_all = flat_e1[:, at + 2 * W:at + 4 * W]
        rg = flat_e1[0:1, at + 4 * W:at + 10 * W].rearrange("p (a w) -> p a w", w=W)
        rg_i = flat_e1[0:1, at + 10 * W:at + 12 * W].bitcast(I32).rearrange("p (a w) -> p a w", w=W)
        cmin = flat_e1[:, at + 12 * W:at + 12 * W + RB]
        cmax = flat_e1[:, at + 12 * W + RB:at + 12 * W + 2 * RB]
        assert at + 12 * W + 2 * RB <= NE * KB * HID and 4 * NCOL <= NE * HBLK * D
        assert 2 * RB * P <= GSLOTS * D

        block = ctx.enter_context(nc.Block())

        def window_table(eng, layer, w):
            lo = eng.value_load(tab[0:1, 0, bass.ds(w, 1)], min_val=0, max_val=NCH)
            end = eng.value_load(tab[0:1, 1, bass.ds(w, 1)], min_val=STATIC + 1, max_val=NCOL - U + 1)
            off = eng.value_load(tab[0:1, 2 + layer, bass.ds(w, 1)], min_val=0, max_val=(2 * W + 1) * NCOL)
            return lo, end, off

        def rest_table(eng, layer, w):
            n = eng.value_load(tab[0:1, 4, bass.ds(w, 1)], min_val=U, max_val=NCOL)
            base = eng.value_load(tab[0:1, 5 + layer, bass.ds(w, 1)], min_val=0, max_val=2 * W * NCOL)
            return n, base

        def rest_first(eng, lo):
            return lo + STATIC

        @block.sync
        def _(sp):
            for dst_t, src_t in ((dst_i, dst_cols), (ew[:, :], ew_cols), (src1[:, :], src_cols)):
                sp.dma_start(dst_t, src_t).then_inc(s["edges_in"], 16)
            sp.dma_start(drow_i, dst_rows).then_inc(s["rows_in"], 16)
            for i in range(2):
                sp.dma_start(t_a[i][:, :], x[i * P:(i + 1) * P, :]).then_inc(s[f"x_in{i}"], 16)
            n = 0
            for t, a in ((w6, W6T), (w7, W7T), (wp, WpT), (wq, Wq), (wk, Wk), (wv, Wv), (wm, Wm), (w1, W1), (w2, W2)):
                sp.dma_start(t[:, :, :], a.rearrange("(k p) n -> p k n", p=P)).then_inc(s["weights_in"], 16)
                n += 1
            for i in range(5):
                sp.dma_start(vec[:, i, :], vecs[i:i + 1, :].to_broadcast([P, D])).then_inc(s["weights_in"], 16)
                n += 1
            with nc.allow_non_contiguous_dma(reason="a few columns"):
                sp.dma_start(lncol[:, :, :], ln_cols).then_inc(s["weights_in"], 16)
                sp.dma_start(mixcol[:, :, :], mix_cols).then_inc(s["weights_in"], 16)
                sp.dma_start(wg[:, :, :], Wg.rearrange("(k p) n -> p k n", p=P)).then_inc(s["weights_in"], 16)
                sp.dma_start(bgr[:, :], bg.to_broadcast([P, NE])).then_inc(s["weights_in"], 16)
                sp.dma_start(eb1c[:, :, :], eb1).then_inc(s["weights_in"], 16)
                sp.dma_start(eb2r[:, :], eb2).then_inc(s["weights_in"], 16)
                n += 6
            assert n == WEIGHT_LOADS
            sp.wait_ge(s["consts"], N_CONSTS)
            for table, b in ((xn_d, W), (h1_d, W), (h2_d, W + 1), (x1_d, W), (r_d, 0)):
                sp.dma_start(rows(table, b), zero_tile[:, :]).then_inc(s["blank_out"], 16)

            def tile(t, b, p):
                r0 = sp.snap(t * P) if not isinstance(t, int) else t * P
                r1 = sp.snap((t + 2) * P) if not isinstance(t, int) else (t + 2) * P
                sp.wait_ge(s["xn_done"], t + 1)
                sp.dma_start(xn_d[bass.ds(r0, P), :], t_b[b][:, :]).then_inc(s[f"xn_out{b}"], 16)
                sp.dma_start(t_a[b][:, :], x[bass.ds(r1, P), :]).then_inc(s[f"x_in{b}"], 16)
                sp.wait_ge(s["h1_done"], t + 1)
                sp.dma_start(h1_d[bass.ds(r0, P), :], u4[:, :]).then_inc(s["h1_out"], 16)

            tile(0, 0, 0)
            with sp.Fori(0, (W - 1) // 2) as p:
                tile(2 * p + 1, 1, p)
                tile(2 * p + 2, 0, p + 1)

            sp.wait_ge(s["blank_out"], 16 * 5)
            sp.wait_ge(s["kv_acc"], W)
            sp.wait_ge(s["h1_out"], 16 * W)
            for b in range(2):
                sp.wait_ge(s[f"xn_out{b}"], 16 * ((W + 1 - b) // 2))
            sp.sem_inc(s["table1"], 1)
            sp.dma_start(hself[:, :], rows(h1_d, 0)).then_inc(s["self_in"], 16)
            sp.dma_start(u1[:, :], rows(xn_d, 0)).then_inc(s["xn_in"], 16)
            for e in range(NE):
                sp.dma_start(ew1[:, e, :, :], eW1[e].rearrange("(k p) n -> p k n", p=P)).then_inc(s["experts_in"], 16)
                sp.dma_start(ew2[:, e, :, :], eW2[e].rearrange("(k p) n -> p k n", p=P)).then_inc(s["experts_in"], 16)
            with sp.Fori(0, W) as w:
                here, after = sp.snap(w * P), sp.snap((w + 1) * P)
                sp.wait_ge(s["self_used"], w + 1)
                sp.dma_start(hself[:, :], h1_d[bass.ds(after, P), :]).then_inc(s["self_in"], 16)
                sp.wait_ge(s["r_done"], w)
                sp.dma_start(u2[:, :], x[bass.ds(here, P), :]).then_inc(s["x_again"], 16)
                sp.wait_ge(s["h2_done"], w + 1)
                sp.dma_start(h2_d[bass.ds(here, P), :], u4[:, :]).then_inc(s["h2_out"], 16)
                sp.wait_ge(s["x1_done"], w + 1)
                sp.dma_start(x1_d[bass.ds(here, P), :], u5[:, :]).then_inc(s["x1_out"], 16)
                sp.wait_ge(s["r_done"], w + 1)
                sp.dma_start(r_d[bass.ds(after, P), :], u6[:, :]).then_inc(s["r_out"], 16)
                sp.dma_start(u1[:, :], xn_d[bass.ds(after, P), :]).then_inc(s["xn_in"], 16)
            sp.wait_ge(s["h2_done"], W + 1)
            sp.dma_start(rows(h2_d, W), u4[:, :]).then_inc(s["h2_out"], 16)

            sp.wait_ge(s["h2_out"], 16 * (W + 1))
            sp.wait_ge(s["x1_out"], 16 * W)
            sp.wait_ge(s["r_out"], 16 * W)
            sp.wait_ge(s["self_in"], 16 * (W + 1))
            sp.wait_ge(s["xn_in"], 16 * (W + 1))
            sp.sem_inc(s["table2"], 1)
            sp.dma_start(hself[:, :], rows(h2_d, 1)).then_inc(s["self2_in"], 16)
            sp.dma_start(u1[:, :], rows(x1_d, 0)).then_inc(s["x1_in"], 16)

            def out_tile(w):
                sp.wait_ge(s["facc"], (NE + 1) * (w + 1))
                sp.dma_start(rows(out, w), u8[:, :]).then_inc(s["out_stored"], 16)

            def r_tile(w):
                sp.wait_ge(s["x3_done"], w)
                sp.dma_start(u2[:, :], rows(r_d, w)).then_inc(s["r_in"], 16)

            with sp.Fori(0, W) as w:
                here, nxt, nxt2 = sp.snap(w * P), sp.snap((w + 1) * P), sp.snap((w + 2) * P)
                sp.wait_ge(s["x3_done"], w)
                sp.dma_start(u2[:, :], r_d[bass.ds(here, P), :]).then_inc(s["r_in"], 16)
                sp.wait_ge(s["self2_used"], w + 1)
                sp.dma_start(hself[:, :], h2_d[bass.ds(nxt2, P), :]).then_inc(s["self2_in"], 16)
                sp.wait_ge(s["x2_done"], w + 2)
                sp.dma_start(u1[:, :], x1_d[bass.ds(nxt, P), :]).then_inc(s["x1_in"], 16)
                sp.wait_ge(s["facc"], (NE + 1) * (w + 1))
                sp.dma_start(out[bass.ds(here, P), :], u8[:, :]).then_inc(s["out_stored"], 16)
            r_tile(W)
            out_tile(W)
            out_tile(W + 1)
            sp.wait_ge(s["out_stored"], 16 * (W + 2))
            sp.wait_ge(s["self2_in"], 16 * (W + 1))
            sp.wait_ge(s["x1_in"], 16 * (W + 1))

        @block.gpsimd
        def _(pool):
            c = s["consts"]
            n = 0

            def const(ins):
                nonlocal n
                n += 1
                ins.then_inc(c, 1)

            const(pool.memset(ident[:, :], 0.0))
            const(pool.memset(ones_row[:, :], 1.0))
            const(pool.memset(zero_tile[:, :], 0.0))
            const(pool.memset(headmask[:, :], 1.0))
            const(pool.memset(valid[:, :], 1.0))
            const(pool.memset(lowtri[:, :, :], 1.0))
            const(pool.iota(iota_p[:, :], [[1, P]], channel_multiplier=0, allow_small_or_imprecise_dtypes=True))
            const(pool.iota(iota_w[:, :], [[1, W]], channel_multiplier=0, allow_small_or_imprecise_dtypes=True))
            const(pool.iota(win_first[:, :], [[P, W]], channel_multiplier=0, allow_small_or_imprecise_dtypes=True))
            const(pool.iota(chunk_id[:, :], [[P, RB]], channel_multiplier=1, allow_small_or_imprecise_dtypes=True))
            pool.wait_ge(c, n)
            const(pool.affine_select(out=ident[:, :], in_=ident[:, :], compare_op=ALU.not_equal, fill=1.0, base=0,
                                     pattern=[[-1, P]], channel_multiplier=1))
            const(pool.affine_select(out=valid[:, :], in_=valid[:, :], compare_op=ALU.is_ge, fill=0.0,
                                     base=N_NODES - 1, pattern=[[-P, W]], channel_multiplier=-1))
            const(pool.affine_select(out=headmask[:, :], in_=headmask[:, :], compare_op=ALU.is_ge, fill=0.0,
                                     base=0, pattern=[[-HD, HPB]], channel_multiplier=1))
            const(pool.affine_select(out=lowtri[:, :, :], in_=lowtri[:, :, :], compare_op=ALU.is_ge, fill=0.0,
                                     base=-1, pattern=[[1, NE], [-1, NE]], channel_multiplier=0))
            pool.wait_ge(c, n)
            const(pool.affine_select(out=headmask[:, :], in_=headmask[:, :], compare_op=ALU.is_ge, fill=0.0,
                                     base=HD - 1, pattern=[[HD, HPB]], channel_multiplier=-1))
            assert n == N_CONSTS
            pool.wait_ge(s["range_parts"], 2)
            pool.partition_all_reduce(range_all, range_part, P, bass.bass_isa.ReduceOp.max).then_inc(s["range_max"], 1)
            pool.wait_ge(s["consts"], N_CONSTS)
            pool.wait_ge(s["dst_parts"], 2)

            def deg_step(t, b):
                wts = ew[:, bass.ds(t * DEGU, DEGU)].unsqueeze(2).to_broadcast([P, DEGU, W])
                pool.wait_ge(s["oh_win_eq"], t + 1)
                pool.sem_inc(s["pool_gate"], 1)
                pool.tensor_tensor(oh_win[b], oh_win[b], wts, ALU.mult).then_inc(s["oh_win"], 1)

            with pool.Fori(0, DEG_STEPS // 2) as p:
                deg_step(2 * p, 0)
                deg_step(2 * p + 1, 1)

            def gathers(layer, table, src):
                pool.wait_ge(s[f"table{layer + 1}"], 1)
                pool.wait_ge(s["tab_set"], 7)
                with pool.Fori(0, W) as w:
                    lo, end, off = window_table(pool, layer, w)
                    v = layer * W * STATIC + w * STATIC
                    for n in range(STATIC):
                        slot = n % GSLOTS
                        if n % U == 0:
                            pool.wait_ge(s["main_used"], v + n + U)
                            pool.sem_inc(s["pool_gate"], 1)
                            pool.tensor_copy(idx_s[:, slot:slot + U], src[:, bass.ds(lo + n, U)]).then_inc(s["idx_set"], U)
                            pool.wait_ge(s["idx_set"], v + n + U)
                            pool.sem_inc(s["pool_gate"], 1)
                        pool.indirect_dma_start(
                            gs[:, slot, :], None, table[:, :],
                            bass.IndirectOffsetOnAxis(ap=idx_s[:, slot:slot + 1], axis=0)).then_inc(s[f"main_in{slot}"], 16)
                    with pool.Fori(rest_first(pool, lo), end, U) as col0:
                        pool.wait_ge(s["rest_used"], col0 + off + U)
                        pool.sem_inc(s["pool_gate"], 1)
                        pool.tensor_copy(idx_r[:, :], src[:, bass.ds(col0, U)]).then_inc(s["idx_rest_set"], U)
                        pool.wait_ge(s["idx_rest_set"], col0 + off + U)
                        pool.sem_inc(s["pool_gate"], 1)
                        for j in range(U):
                            pool.indirect_dma_start(
                                gr[:, j, :], None, table[:, :],
                                bass.IndirectOffsetOnAxis(ap=idx_r[:, j:j + 1], axis=0)).then_inc(s[f"rest_in{j}"], 16)

            gathers(0, h1_d, src1)
            gathers(1, h2_d, src2)

        @block.scalar
        def _(act):
            act.wait_ge(s["consts"], N_CONSTS)

            def tile(t, b):
                act.wait_ge(s["xn_tp"], t + 1)
                act.wait_ge(s["v_ps"], t)
                act.copy(xT[:, :, :], half(1)).then_inc(s["xT_set"], 1)
                act.wait_ge(s["z_tp"], t + 1)
                act.wait_ge(s["h_ps"], t)
                act.copy(zT[:, :, :], half(2)).then_inc(s["zT_set"], 1)
                act.wait_ge(s["k_min"], t + 1)
                act.activation(u3[:, :], u2[:, :], ACT.Exp).then_inc(s["k_exp"], 1)
                act.wait_ge(s["v_ps"], t + 1)
                act.wait_ge(s["kv_acc"], t)
                act.activation(vx[:, :, 0:P], half(4), ACT.Copy, scale=valid[:, bass.ds(t, 1)])
                act.copy(vx[:, :, P:P + 1], valid[:, bass.ds(t, 1)].unsqueeze(1).to_broadcast([P, KB, 1])
                         ).then_inc(s["v_set"], 1)
                act.wait_ge(s["h_ps"], t + 1)
                act.wait_ge(s["dis_set"], 1)
                act.wait_ge(s["h1_out"], 16 * t)
                act.activation(u4[:, :], wide(7), ACT.Copy, scale=dis[:, bass.ds(t + 1, 1)]).then_inc(s["h1_done"], 1)

            tile(0, 0)
            with act.Fori(0, (W - 1) // 2) as p:
                tile(2 * p + 1, 1)
                tile(2 * p + 2, 0)

            act.wait_ge(s["h1_out"], 16 * W)

            def next_h(w):
                act.wait_ge(s["z1_tp"], w + 1)
                act.wait_ge(s["h7_ps"], w)
                act.copy(zT[:, :, :], half(1)).then_inc(s["z1T_set"], 1)

            def next_h_scaled(w):
                act.wait_ge(s["h7_ps"], w + 1)
                act.wait_ge(s["h2_out"], 16 * w)
                act.activation(u4[:, :], wide(7), ACT.Copy, scale=dis[:, bass.ds(w, 1)]).then_inc(s["h2_done"], 1)

            with act.Fori(0, W) as w:
                next_h(w)
                act.wait_ge(s["xn1_tp"], w + 1)
                act.wait_ge(s["hh_ps"], w)
                act.copy(xT[:, :, :], half(5)).then_inc(s["xn1T_set"], 1)
                next_h_scaled(w)
                act.wait_ge(s["q_min"], w + 1)
                act.activation(t_a[1][:, :], t_a[0][:, :], ACT.Exp).then_inc(s["q_exp"], 1)
                act.wait_ge(s["msg_tp"], w + 1)
                act.wait_ge(s["m_ps"], w)
                act.copy(mT[:, :, :], half(5)).then_inc(s["msgT_set"], 1)
                act.wait_ge(s["mn_tp"], w + 1)
                act.copy(nT[:, :, :], half(5)).then_inc(s["mnT_set"], 1)
                act.wait_ge(s["hh_ps"], w + 1)
                act.wait_ge(s["y1_ps"], w)
                for j in range(HBLK):
                    act.activation(hT[0][:, j, :], bank[6][:, j * P:(j + 1) * P], ACT.Relu,
                                   bias=w1bias[:, j:j + 1]).then_inc(s["hr_done"], 1)
            next_h(W)
            next_h_scaled(W)

            act.wait_ge(s["zn_blank"], 1)
            act.wait_ge(s["y1_ps"], W)

            def window2(w, epilogue=True):
                act.wait_ge(s["zn_set"], w)
                act.wait_ge(s["hid_ps"], NE * w)
                act.copy(nT[:, :, :], zT[:, :, :]).then_inc(s["zc_set"], 1)
                if epilogue:
                    act.wait_ge(s["x2_tp"], w + 1)
                    act.wait_ge(s["p_ps"], w)
                    act.copy(xT[:, :, :], half(1)).then_inc(s["x2T_set"], 1)
                for e in range(NE):
                    if epilogue and e == 3:
                        act.wait_ge(s["z3_tp"], w + 1)
                        act.wait_ge(s["zc_set"], w + 1)
                        act.copy(zT[:, :, :], half(1)).then_inc(s["zn_set"], 1)
                    if epilogue and e == 5:
                        act.wait_ge(s["mt_ps"], w + 1)
                        act.wait_ge(s["b2_ps"], w)
                        act.copy(maskT[:, :], bank[3][0:NE, P // 2:P // 2 + P]).then_inc(s["maskT_set"], 1)
                    act.wait_ge(s["hid_ps"], NE * w + e + 1)
                    act.wait_ge(s["y_ps"], NE * w + e + 1)
                    for j in range(HBLK):
                        act.activation(hT[e % 2][:, j, :], bank[(6, 2)[e % 2]][:, j * P:(j + 1) * P], ACT.Gelu,
                                       bias=eb1c[:, e, j:j + 1]).then_inc(s["gelu_done"], 1)

            with act.Fori(0, W) as w:
                window2(w)
            window2(W)
            window2(W + 1, epilogue=False)

        def inv_sqrt(dve, ch, v, minus_half, y, t):
            dve.tensor_scalar(minus_half, v, -0.5, None, ALU.mult)
            ch.link(dve.tensor_scalar(y.bitcast(I32), v.bitcast(I32), 1, None, ALU.arith_shift_right))
            ch.link(dve.tensor_scalar(y.bitcast(I32), y.bitcast(I32), -1.0, float(RSQRT_BITS), ALU.mult, ALU.add))
            for _ in range(NEWTON):
                ch.link(dve.tensor_tensor(t, y, y, ALU.mult))
                ch.link(dve.tensor_tensor(t, t, minus_half, ALU.mult))
                ch.link(dve.scalar_tensor_tensor(out=y, in0=t, scalar=1.5, in1=y, op0=ALU.add, op1=ALU.mult))

        def layer_norm(dve, ch, xin, xout, stats, mean_var, sc):
            ch.link(dve.bn_stats(stats[:, :], xin))
            dve.sem_inc(s["dve_gate"], 1)
            ch.link(dve.bn_aggr(mean_var[:, :], stats[:, :]))
            ch.link(dve.tensor_scalar(sc[:, 0:1], mean_var[:, 1:2], EPS, None, ALU.add))
            inv_sqrt(dve, ch, sc[:, 0:1], sc[:, 1:2], sc[:, 2:3], sc[:, 3:4])
            return dve.tensor_scalar(xout, xin, mean_var[:, 0:1], sc[:, 2:3], ALU.subtract, ALU.mult)

        @block.vector
        def _(dve):
            ch = Chain(dve, s["dve_setup"], 0, 0)
            dve.wait_ge(s["consts"], N_CONSTS)
            dve.wait_ge(s["rows_in"], 16)
            ch.link(dve.tensor_copy(drow_f, drow_i))
            dve.tensor_reduce(cmin, drow_f, AX.X, ALU.min)
            ch.link(dve.tensor_reduce(cmax, drow_f, AX.X, ALU.max))
            wins = win_first[:, :].unsqueeze(2).to_broadcast([P, W, RB])
            ch.link(dve.tensor_scalar(cmin, cmin, float(1 - P), None, ALU.add))
            dve.tensor_tensor(touch[0], wins, cmin.unsqueeze(1).to_broadcast([P, W, RB]), ALU.is_ge)
            ch.link(dve.tensor_tensor(touch[1], wins, cmax.unsqueeze(1).to_broadcast([P, W, RB]), ALU.is_le))
            ch.link(dve.tensor_tensor(touch[0], touch[0], touch[1], ALU.mult))
            ids = chunk_id[:, :].unsqueeze(1).to_broadcast([P, W, RB])
            ch.link(dve.tensor_tensor(touch[1], touch[0], ids, ALU.mult))
            ch.link(dve.tensor_tensor(touch[2], touch[1], touch[0], ALU.add))
            dve.tensor_reduce(range_part[:, W:2 * W], touch[2], AX.X, ALU.max).then_inc(s["range_parts"], 1)
            ch.link(dve.tensor_scalar(touch[0], touch[0], float(NCH), None, ALU.mult))
            ch.link(dve.tensor_tensor(touch[0], touch[0], touch[1], ALU.subtract))
            dve.tensor_reduce(range_part[:, 0:W], touch[0], AX.X, ALU.max).then_inc(s["range_parts"], 1)
            dve.wait_ge(s["edges_in"], 16 * 3)
            dve.tensor_copy(dst_f[:, :], dst_i)
            ch.link(dve.tensor_scalar(tmp_i, dst_i, 7, None, ALU.arith_shift_right))
            ch.link(dve.tensor_copy(dst_hi, tmp_i))
            ch.link(dve.tensor_scalar(tmp_i, dst_i, P - 1, None, ALU.bitwise_and))
            ch.link(dve.tensor_copy(dst_lo, tmp_i))
            dve.tensor_scalar(src2[:, :], src1[:, :], P, None, ALU.add).then_inc(s["dst_parts"], 2)
            dve.wait_ge(s["range_max"], 1)
            first, ngr, rest, cum = rg[:, 0, :], rg[:, 1, :], rg[:, 2, :], rg[:, 3, :]
            ch.link(dve.tensor_scalar(first, range_all[0:1, 0:W], -1.0, float(NCH), ALU.mult, ALU.add))
            ch.link(dve.tensor_tensor(ngr, range_all[0:1, W:2 * W], first, ALU.subtract))
            ch.link(dve.tensor_scalar(rg_i[:, 0, :], ngr, float(U - 1), 0.0, ALU.add, ALU.max))
            ch.link(dve.tensor_scalar(rg_i[:, 1, :], rg_i[:, 0, :], 2, None, ALU.arith_shift_right))
            ch.link(dve.tensor_scalar(rest, rg_i[:, 1, :], float(PIECES + 1), float(-PIECES), ALU.max, ALU.add))
            step, a, b = 1, 2, 3
            while step < W:
                dve.tensor_copy(rg[:, b, 0:step], rg[:, a, 0:step])
                ch.link(dve.tensor_tensor(rg[:, b, step:W], rg[:, a, step:W], rg[:, a, 0:W - step], ALU.add))
                a, b, step = b, (4 if b == 3 else 3), 2 * step
            total = rg[:, a, :]
            dve.tensor_scalar(tab[:, 4, :], rest, float(U), None, ALU.mult).then_inc(s["tab_set"], 1)
            ch.link(dve.tensor_scalar(rg[:, 1, :], rest, float(U), float(STATIC), ALU.mult, ALU.add))
            dve.tensor_copy(tab[:, 0, :], first).then_inc(s["tab_set"], 1)
            dve.tensor_tensor(tab[:, 1, :], first, rg[:, 1, :], ALU.add).then_inc(s["tab_set"], 1)
            ch.link(dve.tensor_tensor(rg[:, 5, :], total, rest, ALU.subtract))
            dve.tensor_scalar(tab[:, 5, :], rg[:, 5, :], float(U), None, ALU.mult).then_inc(s["tab_set"], 1)
            ch.link(dve.tensor_scalar(rg[:, 1, 0:1], total[:, W - 1:W], float(U), None, ALU.mult))
            dve.tensor_scalar(tab[:, 6, :], rg[:, 5, :], float(U), rg[:, 1, 0:1], ALU.mult, ALU.add).then_inc(s["tab_set"], 1)
            ch.link(dve.tensor_scalar(rg[:, 5, :], rg[:, 5, :], float(U), float(REST_FROM - STATIC), ALU.mult, ALU.add))
            ch.link(dve.tensor_tensor(rg[:, 5, :], rg[:, 5, :], first, ALU.subtract))
            dve.tensor_copy(tab[:, 2, :], rg[:, 5, :]).then_inc(s["tab_set"], 1)
            dve.tensor_scalar(tab[:, 3, :], rg[:, 5, :], rg[:, 1, 0:1], None, ALU.add).then_inc(s["tab_set"], 1)
            dve.wait_ge(s["weights_in"], 16 * WEIGHT_LOADS)
            dve.tensor_tensor(vec[:, 5, :], vec[:, 4, :], vec[:, 2, :], ALU.add)
            dve.wait_ge(s["shift_ps"], 3)
            dve.tensor_copy(hb[:, 0, :], bank[1][0:1, 0:D])
            dve.tensor_copy(hb[:, 1, :], bank[2][0:1, 0:D])
            dve.tensor_copy(w1bias[:, :], bank[3][:, 0:HBLK])
            for k in range(KB):
                dve.tensor_scalar(w6[:, k, :], w6[:, k, :], lncol[:, 0, k:k + 1], None, ALU.mult)
                dve.tensor_scalar(w7[:, k, :], w7[:, k, :], lncol[:, 2, k:k + 1], None, ALU.mult)
                last = dve.tensor_scalar(w1[:, KB + k, :], w1[:, KB + k, :], mixcol[:, 0, k:k + 1], None, ALU.mult)
            ch.link(last)
            dve.sem_inc(s["weights_set"], 1)

            def deg_step(t, b):
                dve.wait_ge(s["deg_used"], t + 1)
                dve.tensor_tensor(oh_node[b], iota_p[:, :].unsqueeze(1).to_broadcast([P, DEGU, P]),
                                  dst_lo[:, bass.ds(t * DEGU, DEGU)].unsqueeze(2).to_broadcast([P, DEGU, P]),
                                  ALU.is_equal).then_inc(s["oh_node"], 1)
                dve.tensor_tensor(oh_win[b], iota_w[:, :].unsqueeze(1).to_broadcast([P, DEGU, W]),
                                  dst_hi[:, bass.ds(t * DEGU, DEGU)].unsqueeze(2).to_broadcast([P, DEGU, W]),
                                  ALU.is_equal).then_inc(s["oh_win_eq"], 1)

            with dve.Fori(0, DEG_STEPS // 2) as p:
                deg_step(2 * p, 0)
                deg_step(2 * p + 1, 1)
            dve.wait_ge(s["deg_used"], DEG_STEPS + 2)
            deg, pos = u5[:, 0:W], u6[:, 0:W]
            ch.link(dve.tensor_scalar(deg, bank[0][:, 0:W], 1.0, None, ALU.add))
            ch.link(dve.tensor_scalar(pos, deg, 0.0, None, ALU.is_gt))
            ch.link(dve.tensor_scalar(deg, deg, float(np.finfo(np.float32).tiny), None, ALU.max))
            inv_sqrt(dve, ch, deg, u7[:, 0:W], u8[:, 0:W], u3[:, 0:W])
            dve.memset(dis[:, 0:1], 0.0)
            dve.tensor_tensor(dis[:, 1:W + 1], u8[:, 0:W], pos, ALU.mult).then_inc(s["dis_set"], 1)

            def norms(t, b, p):
                tc = Chain(dve, s["dve_norms"], 2 * LN_LINKS, t)
                dve.wait_ge(s[f"x_in{b}"], 16 * (p + 1))
                dve.wait_ge(s[f"xn_out{b}"], 16 * p)
                dve.wait_ge(s["z_tp"], t)
                layer_norm(dve, tc, t_a[b][:, :], t_b[b][:, :], st, mv, rstd).then_inc(s["xn_done"], 1)
                dve.wait_ge(s["xn_done"], t + 1)
                layer_norm(dve, tc, t_b[b][:, :], t_c[b][:, :], st2, mv2, rstd2).then_inc(s["z_done"], 1)
                assert tc.n == tc.per

            def keys(t):
                dve.wait_ge(s["k_ps"], t + 1)
                dve.tensor_scalar(u2[:, :], wide(3), 0.0, None, ALU.min).then_inc(s["k_min"], 1)
                dve.wait_ge(s["k_exp"], t + 1)
                dve.wait_ge(s["kv_acc"], t)
                dve.scalar_tensor_tensor(out=u1[:, :], in0=wide(3), scalar=0.0, in1=u3[:, :], op0=ALU.max,
                                         op1=ALU.add).then_inc(s["k_done"], 1)

            norms(0, 0, 0)
            with dve.Fori(0, (W - 1) // 2) as p:
                norms(2 * p + 1, 1, p)
                keys(2 * p)
                norms(2 * p + 2, 0, p + 1)
                keys(2 * p + 1)
            keys(W - 1)
            dve.wait_ge(s["kv_acc"], W)
            for k in range(KB):
                dve.tensor_tensor(kvx[:, k, 0:P].rearrange("p (h d) -> p h d", h=HPB),
                                  bank[5 + k][:, 0:P].rearrange("p (h d) -> p h d", h=HPB),
                                  headmask[:, :].unsqueeze(2).to_broadcast([P, HPB, HD]), ALU.mult)
                last = dve.tensor_scalar(kvx[:, k, P:P + HPB], headmask[:, :], bank[5 + k][:, P:P + 1], None, ALU.mult)
            last.then_inc(s["kvx_set"], 1)
            dve.wait_ge(s["x_in0"], 16 * ((W + 1) // 2 + 1))
            dve.wait_ge(s["x_in1"], 16 * ((W + 1) // 2))
            dve.wait_ge(s["z_tp"], W)
            dve.memset(u3[:, :], 0.0).then_inc(s["z1_done"], 1)

            def scatter_group(layer, v, k, first):
                dve.wait_ge(s["main_used"], v + k * U + U + GSLOTS - SSLOTS)
                for j in range(U):
                    c = first + (k * U + j)
                    m = dve.tensor_scalar(ss[:, (k * U + j) % SSLOTS, :], iw[:, :], dst_f[:, bass.ds(c, 1)],
                                          ew[:, bass.ds(c, 1)], ALU.is_equal, ALU.mult)
                m.then_inc(s["main_set"], U)

            def scatter_rest(lo, end, off):
                with dve.Fori(lo + STATIC, end, U) as col0:
                    dve.wait_ge(s["rest_used"], col0 + off + U)
                    for j in range(U):
                        m = dve.tensor_scalar(sr[:, j, :], iw[:, :], dst_f[:, bass.ds(col0 + j, 1)],
                                              ew[:, bass.ds(col0 + j, 1)], ALU.is_equal, ALU.mult)
                    m.then_inc(s["rest_set"], U)

            def window_nodes(layer, w):
                dve.tensor_scalar(iw[:, :], iota_p[:, :], win_first[:, bass.ds(w, 1)], None,
                                  ALU.add).then_inc(s["iw_set"], 1)
                dve.wait_ge(s["iw_set"], layer * W + w + 1)

            dve.wait_ge(s["tab_set"], 7)
            with dve.Fori(0, W) as w:
                tc = Chain(dve, s["dve_l1"], 3 * LN_LINKS + 6, w)
                lo, end, off = window_table(dve, 0, w)
                v = w * STATIC
                window_nodes(0, w)
                scatter_group(0, v, 0, lo)
                for k in range(PIECES):
                    if k + 1 < PIECES:
                        scatter_group(0, v, k + 1, lo)
                    if k == 1:
                        dve.wait_ge(s["q_ps"], w + 1)
                        dve.tensor_scalar(t_a[0][:, :], wide(2), 0.0, None, ALU.min).then_inc(s["q_min"], 1)
                    if k == 2:
                        dve.wait_ge(s["q_exp"], w + 1)
                        dve.wait_ge(s["nd_ps"], w)
                        dve.scalar_tensor_tensor(out=t_b[0][:, :], in0=wide(2), scalar=0.0, in1=t_a[1][:, :],
                                                 op0=ALU.max, op1=ALU.add).then_inc(s["q_done"], 1)
                    if k == 3:
                        dve.wait_ge(s["nd_ps"], w + 1)
                        nd = half(3, P + HPB)
                        tc.link(dve.tensor_scalar(zden[:, :, :], nd[:, :, P:P + HPB], ATT_EPS, None, ALU.add))
                        tc.link(dve.reciprocal(zrec[:, :, :], zden[:, :, :]))
                        dve.wait_ge(s["msg_tp"], w)
                        for kb in range(KB):
                            m = dve.tensor_tensor(
                                u8[:, kb * P:(kb + 1) * P].rearrange("p (h d) -> p h d", h=HPB),
                                nd[:, kb, 0:P].rearrange("p (h d) -> p h d", h=HPB),
                                zrec[:, kb, :].unsqueeze(2).to_broadcast([P, HPB, HD]), ALU.mult)
                        m.then_inc(s["msg_done"], 1)
                    if k == 5:
                        dve.wait_ge(s["m_ps"], w + 1)
                        layer_norm(dve, tc, wide(4), u7[:, :], st, mv, rstd).then_inc(s["mn_done"], 1)
                scatter_rest(lo, end, off)
                dve.wait_ge(s["rest_used"], end + off + U)
                dve.scalar_tensor_tensor(out=t_b[1][:, :], in0=acc, scalar=dis[:, bass.ds(w + 1, 1)], in1=vec[:, 0, :],
                                         op0=ALU.mult, op1=ALU.add).then_inc(s["acc_read"], 1)
                dve.wait_ge(s["acc_read"], w + 1)
                dve.wait_ge(s["x1_out"], 16 * w)
                dve.wait_ge(s["xn_in"], 16 * (w + 1))
                dve.scalar_tensor_tensor(out=u5[:, :], in0=t_b[1][:, :], scalar=0.0, in1=u1[:, :], op0=ALU.max,
                                         op1=ALU.add).then_inc(s["x1_done"], 1)
                dve.wait_ge(s["x1_done"], w + 1)
                dve.wait_ge(s["z1_tp"], w + 1)
                layer_norm(dve, tc, u5[:, :], u3[:, :], st2, mv2, rstd2).then_inc(s["z1_done"], 1)
                dve.wait_ge(s["x_again"], 16 * (w + 1))
                tc.link(dve.tensor_tensor(t_c[0][:, :], u1[:, :], u2[:, :], ALU.add))
                tc.link(dve.tensor_tensor(t_c[0][:, :], t_c[0][:, :], vec[:, 5, :], ALU.add))
                dve.wait_ge(s["y1_ps"], w + 1)
                tc.link(layer_norm(dve, tc, wide(4), t_c[1][:, :], st, mv, rstd))
                tc.link(dve.tensor_tensor(t_c[1][:, :], t_c[1][:, :], vec[:, 3, :], ALU.mult))
                dve.wait_ge(s["r_out"], 16 * w)
                dve.tensor_tensor(u6[:, :], t_c[1][:, :], t_c[0][:, :], ALU.add).then_inc(s["r_done"], 1)
                assert tc.n == tc.per, tc.n

            dve.wait_ge(s["x1_out"], 16 * W)
            dve.wait_ge(s["r_out"], 16 * W)
            dve.wait_ge(s["h2_out"], 16 * (W + 1))
            dve.wait_ge(s["z1_tp"], W + 1)
            dve.wait_ge(s["h7_ps"], W + 1)
            dve.memset(u3[:, :], 0.0).then_inc(s["x2_done"], 1)
            dve.memset(u6[:, :], 0.0).then_inc(s["blank_set"], 1)
            dve.memset(mask_n[:, :], 0.0).then_inc(s["blank_set"], 1)
            dve.memset(zT[:, :, :], 0.0).then_inc(s["zn_blank"], 1)
            dve.wait_ge(s["blank_set"], 2)

            def add_expert(w, e):
                dve.wait_ge(s["y_ps"], NE * w + e + 1 + 2)
                dve.wait_ge(s["facc"], (NE + 1) * w + 1 + e)
                dve.scalar_tensor_tensor(out=u8[:, :], in0=wide((7, 5)[e % 2]), scalar=mask_c[:, e:e + 1], in1=u8[:, :],
                                         op0=ALU.mult, op1=ALU.add).then_inc(s["facc"], 1)

            def window2(w, msgs=True, epilogue=True):
                if msgs:
                    lo, end, off = window_table(dve, 1, w)
                    v = (W + w) * STATIC
                    window_nodes(1, w)
                    scatter_group(1, v, 0, lo)
                dve.wait_ge(s["out_stored"], 16 * w)
                dve.wait_ge(s["x3b_done"], w)
                dve.tensor_copy(mask_c[:, :], mask_n[:, :]).then_inc(s["mask_set"], 1)
                dve.tensor_copy(u8[:, :], u6[:, :]).then_inc(s["facc"], 1)
                dve.wait_ge(s["mask_set"], w + 1)
                tc = Chain(dve, s["dve_l2"], LN_LINKS + 5, w)
                for k in range(PIECES):
                    if msgs and k + 1 < PIECES:
                        scatter_group(1, v, k + 1, lo)
                    if epilogue and k == 1:
                        dve.wait_ge(s["p_ps"], w + 1)
                        dve.wait_ge(s["r_in"], 16 * (w + 1))
                        dve.tensor_tensor(u4[:, :], wide(4), u2[:, :], ALU.add).then_inc(s["x3_done"], 1)
                        dve.wait_ge(s["x3_done"], w + 1)
                        dve.wait_ge(s["z3_tp"], w)
                        layer_norm(dve, tc, u4[:, :], u5[:, :], st2, mv2, rstd2).then_inc(s["z3_done"], 1)
                    if epilogue and k == 4:
                        dve.wait_ge(s["g_ps"], w + 1)
                        tc.link(dve.tensor_tensor(lg[:, :], bank[3][:, 0:NE], bgr[:, :], ALU.add))
                        mine = lg[:, :].unsqueeze(2).to_broadcast([P, NE, NE])
                        other = lg[:, :].unsqueeze(1).to_broadcast([P, NE, NE])
                        dve.tensor_tensor(cmp1[:, :, :], other, mine, ALU.is_gt)
                        tc.link(dve.tensor_tensor(cmp2[:, :, :], other, mine, ALU.is_equal))
                        tc.link(dve.tensor_tensor(cmp2[:, :, :], cmp2[:, :, :], lowtri[:, :, :], ALU.mult))
                        tc.link(dve.tensor_tensor(cmp1[:, :, :], cmp1[:, :, :], cmp2[:, :, :], ALU.add))
                        tc.link(dve.tensor_reduce(rank[:, :], cmp1[:, :, :], AX.X, ALU.add))
                        dve.tensor_scalar(mask_n[:, :], rank[:, :], 2.0, None, ALU.is_lt).then_inc(s["mask_done"], 1)
                    if epilogue and k == 6:
                        dve.wait_ge(s["b2_ps"], w + 1)
                        dve.wait_ge(s["facc"], (NE + 1) * w + 1)
                        dve.tensor_tensor(u6[:, :], wide(4), u4[:, :], ALU.add).then_inc(s["x3b_done"], 1)
                    if k:
                        add_expert(w, k - 1)
                if epilogue:
                    assert tc.n == tc.per, tc.n
                if msgs:
                    scatter_rest(lo, end, off)
                    dve.wait_ge(s["rest_used"], end + off + U)
                    dve.scalar_tensor_tensor(out=u7[:, :], in0=acc, scalar=dis[:, bass.ds(w + 1, 1)], in1=vec[:, 1, :],
                                             op0=ALU.mult, op1=ALU.add).then_inc(s["acc2_read"], 1)
                    dve.wait_ge(s["acc2_read"], w + 1)
                    dve.wait_ge(s["x1_in"], 16 * (w + 1))
                    dve.wait_ge(s["x2_tp"], w + 1)
                    dve.scalar_tensor_tensor(out=u3[:, :], in0=u7[:, :], scalar=0.0, in1=u1[:, :], op0=ALU.max,
                                             op1=ALU.add).then_inc(s["x2_done"], 1)
                add_expert(w, NE - 1)

            with dve.Fori(0, W) as w:
                window2(w)
            window2(W, msgs=False)
            window2(W + 1, msgs=False, epilogue=False)

        @block.tensor
        def _(pe):
            pe.sem_inc(s["deg_used"], 2)
            pe.sem_inc(s["main_used"], GSLOTS)
            pe.sem_inc(s["rest_used"], REST_FROM + U)
            pe.sem_inc(s["rest_set"], REST_FROM)
            pe.sem_inc(s["idx_rest_set"], REST_FROM)
            pe.wait_ge(s["consts"], N_CONSTS)
            pe.wait_ge(s["weights_in"], 16 * WEIGHT_LOADS)

            def mm(out_ap, lhsT, rhs, first, last, **kw):
                return pe.matmul(out_ap, lhsT, rhs, start=first, stop=last, **kw)

            for i, wt in enumerate((w6, w7)):
                for k in range(KB):
                    m = mm(bank[1 + i][0:1, 0:D], lncol[:, 2 * i + 1, k:k + 1], wt[:, k, :], k == 0, k == KB - 1)
                m.then_inc(s["shift_ps"], 1)
            for j in range(HBLK):
                for k in range(KB):
                    m = mm(bank[3][:, j:j + 1], w1[:, KB + k, j * P:(j + 1) * P], mixcol[:, 1, k:k + 1], k == 0,
                           k == KB - 1)
            m.then_inc(s["shift_ps"], 1)

            mm(bank[0][:, 0:W], zero_tile[:, 0:P], zero_tile[:, 0:W], True, True)

            def deg_step(t, b):
                pe.wait_ge(s["oh_node"], t + 1)
                pe.wait_ge(s["oh_win"], t + 1)
                for c in range(DEGU):
                    m = mm(bank[0][:, 0:W], oh_node[b][:, c, :], oh_win[b][:, c, :], False, True, skip_group_check=True)
                m.then_inc(s["deg_used"], 1)

            with pe.Fori(0, DEG_STEPS // 2) as p:
                deg_step(2 * p, 0)
                deg_step(2 * p + 1, 1)

            for k in range(KB):
                mm(bank[5 + k][:, 0:P + 1], zero_tile[:, 0:P], zero_tile[:, 0:P + 1], True, True)
            pe.wait_ge(s["weights_set"], 1)

            def flip(b, src, done):
                for k in range(KB):
                    m = pe.transpose(half(b)[:, k, :], src[:, k * P:(k + 1) * P], ident[:, :])
                m.then_inc(done, 1)

            def by_rows(b, xt, wt, done, bias=None):
                if bias is not None:
                    mm(wide(b), ones_row[:, :], bias, True, False)
                for k in range(KB):
                    m = mm(wide(b), xt[:, k, :], wt[:, k, :], bias is None and k == 0, k == KB - 1)
                m.then_inc(done, 1)

            def tile(t, b):
                pe.wait_ge(s["xn_done"], t + 1)
                pe.wait_ge(s["xT_set"], t)
                flip(1, t_b[b], s["xn_tp"])
                pe.wait_ge(s["z_done"], t + 1)
                pe.wait_ge(s["zT_set"], t)
                flip(2, t_c[b], s["z_tp"])
                pe.wait_ge(s["xT_set"], t + 1)
                pe.wait_ge(s["k_done"], t)
                by_rows(3, xT, wk, s["k_ps"])
                pe.wait_ge(s["v_set"], t)
                by_rows(4, xT, wv, s["v_ps"])
                pe.wait_ge(s["zT_set"], t + 1)
                pe.wait_ge(s["h1_done"], t)
                by_rows(7, zT, w6, s["h_ps"], bias=hb[:, 0, :])

            def kv(t):
                pe.wait_ge(s["k_done"], t + 1)
                pe.wait_ge(s["v_set"], t + 1)
                for k in range(KB):
                    m = mm(bank[5 + k][:, 0:P + 1], u1[:, k * P:(k + 1) * P], vx[:, k, :], False, True,
                           skip_group_check=True)
                m.then_inc(s["kv_acc"], 1)

            tile(0, 0)
            with pe.Fori(0, (W - 1) // 2) as p:
                tile(2 * p + 1, 1)
                kv(2 * p)
                tile(2 * p + 2, 0)
                kv(2 * p + 1)
            kv(W - 1)

            def messages(turn, v, k):
                pe.wait_ge(s["main_set"], v + k * U + U)
                for n in range(k * U, k * U + U):
                    pe.wait_ge(s[f"main_in{n % GSLOTS}"], 16 * (turn * (STATIC // GSLOTS) + n // GSLOTS + 1))
                    mm(acc, ss[:, n % SSLOTS, :], gs[:, n % GSLOTS, :], False, True,
                       skip_group_check=True).then_inc(s["main_used"], 1)

            def rest_messages(n, base):
                with pe.Fori(0, n, U) as i:
                    pe.wait_ge(s["rest_set"], base + i + (REST_FROM + U))
                    for j in range(U):
                        pe.wait_ge(s[f"rest_in{j}"], (base + i) * (16 // U) + 16)
                        mm(acc, sr[:, j, :], gr[:, j, :], False, True, skip_group_check=True).then_inc(s["rest_used"], 1)

            pe.wait_ge(s["kvx_set"], 1)
            pe.wait_ge(s["tab_set"], 7)

            def next_h_turn(w):
                pe.wait_ge(s["z1_done"], w + 1)
                pe.wait_ge(s["z1T_set"], w)
                flip(1, u3, s["z1_tp"])

            def next_h(w):
                pe.wait_ge(s["z1T_set"], w + 1)
                pe.wait_ge(s["h2_done"], w)
                by_rows(7, zT, w7, s["h7_ps"], bias=hb[:, 1, :])

            with pe.Fori(0, W) as w:
                n_rest, base = rest_table(pe, 0, w)
                v = w * STATIC
                pe.wait_ge(s["acc_read"], w)
                pe.wait_ge(s["self_in"], 16 * (w + 1))
                mm(acc, ident[:, :], hself[:, :], True, True).then_inc(s["self_used"], 1)
                for k in range(PIECES):
                    messages(w, v, k)
                    if k == 0:
                        next_h_turn(w)
                        pe.wait_ge(s["xn_in"], 16 * (w + 1))
                        pe.wait_ge(s["mnT_set"], w)
                        flip(5, u1, s["xn1_tp"])
                    if k == 1:
                        next_h(w)
                        pe.wait_ge(s["xn1T_set"], w + 1)
                        pe.wait_ge(s["q_done"], w)
                        for j in range(KB):
                            for i in range(KB):
                                m = mm(half(2)[:, j, :], wq[:, i, j * P:(j + 1) * P], xT[:, i, :], i == 0, i == KB - 1)
                        m.then_inc(s["q_ps"], 1)
                    if k == 3:
                        pe.wait_ge(s["q_done"], w + 1)
                        pe.wait_ge(s["msg_done"], w)
                        for j in range(KB):
                            m = mm(half(3, P + HPB)[:, j, :], t_b[0][:, j * P:(j + 1) * P], kvx[:, j, :], True, True)
                        m.then_inc(s["nd_ps"], 1)
                    if k == 4:
                        pe.wait_ge(s["msg_done"], w + 1)
                        flip(5, u8, s["msg_tp"])
                    if k == 5:
                        pe.wait_ge(s["msgT_set"], w + 1)
                        pe.wait_ge(s["r_done"], w)
                        by_rows(4, mT, wm, s["m_ps"])
                    if k == 6:
                        pe.wait_ge(s["mn_done"], w + 1)
                        flip(5, u7, s["mn_tp"])
                    if k == 7:
                        pe.wait_ge(s["mnT_set"], w + 1)
                        pe.wait_ge(s["hr_done"], HBLK * w)
                        for j in range(HBLK):
                            for i in range(2 * KB):
                                m = mm(bank[6][:, j * P:(j + 1) * P], w1[:, i, j * P:(j + 1) * P],
                                       (xT if i < KB else nT)[:, i % KB, :], i == 0, i == 2 * KB - 1)
                        m.then_inc(s["hh_ps"], 1)
                rest_messages(n_rest, base)
                pe.wait_ge(s["hr_done"], HBLK * (w + 1))
                for i in range(HBLK):
                    m = mm(wide(4), hT[0][:, i, :], w2[:, i, :], i == 0, i == HBLK - 1)
                m.then_inc(s["y1_ps"], 1)
            next_h_turn(W)
            next_h(W)

            pe.sem_inc(s["y_ps"], 2)
            pe.wait_ge(s["experts_in"], 16 * 2 * NE)
            pe.wait_ge(s["h2_done"], W + 1)

            def hidden(w, e):
                pe.wait_ge(s["zc_set"], w + 1)
                pe.wait_ge(s["gelu_done"], HBLK * (NE * w + max(e - 1, 0)))
                for j in range(HBLK):
                    for i in range(KB):
                        m = mm(bank[(6, 2)[e % 2]][:, j * P:(j + 1) * P], ew1[:, e, i, j * P:(j + 1) * P], nT[:, i, :],
                               i == 0, i == KB - 1)
                m.then_inc(s["hid_ps"], 1)

            def expert_out(w, e):
                pe.wait_ge(s["gelu_done"], HBLK * (NE * w + e + 1))
                pe.wait_ge(s["facc"], (NE + 1) * w + (e if e >= 2 else 0))
                for i in range(HBLK):
                    m = mm(wide((7, 5)[e % 2]), hT[e % 2][:, i, :], ew2[:, e, i, :], i == 0, i == HBLK - 1)
                m.then_inc(s["y_ps"], 1)

            def window2(w, msgs=True, epilogue=True):
                if msgs:
                    n_rest, base = rest_table(pe, 1, w)
                    v = (W + w) * STATIC
                    pe.wait_ge(s["acc2_read"], w)
                    pe.wait_ge(s["self2_in"], 16 * (w + 1))
                    mm(acc, ident[:, :], hself[:, :], True, True).then_inc(s["self2_used"], 1)
                for k in range(PIECES):
                    if msgs:
                        messages(W + w, v, k)
                    if epilogue and k == 0:
                        pe.wait_ge(s["x2_done"], w + 1)
                        pe.wait_ge(s["zn_set"], w)
                        flip(1, u3, s["x2_tp"])
                    if epilogue and k == 1:
                        pe.wait_ge(s["x2T_set"], w + 1)
                        pe.wait_ge(s["x3b_done"], w)
                        by_rows(4, xT, wp, s["p_ps"])
                    if epilogue and k == 3:
                        pe.wait_ge(s["z3_done"], w + 1)
                        flip(1, u5, s["z3_tp"])
                    if epilogue and k == 4:
                        pe.wait_ge(s["zn_set"], w + 1)
                        pe.wait_ge(s["maskT_set"], w)
                        for i in range(KB):
                            m = mm(bank[3][:, 0:NE], zT[:, i, :], wg[:, i, :], i == 0, i == KB - 1)
                        m.then_inc(s["g_ps"], 1)
                    if epilogue and k == 5:
                        pe.wait_ge(s["mask_done"], w + 1)
                        pe.transpose(bank[3][0:NE, P // 2:P // 2 + P], mask_n[:, :], ident[:, :]).then_inc(s["mt_ps"], 1)
                    if epilogue and k == 6:
                        pe.wait_ge(s["maskT_set"], w + 1)
                        pe.wait_ge(s["x3_done"], w + 1)
                        mm(wide(4), maskT[:, :], eb2r[:, :], True, True).then_inc(s["b2_ps"], 1)
                    hidden(w, k)
                    if k:
                        expert_out(w, k - 1)
                if msgs:
                    rest_messages(n_rest, base)
                expert_out(w, NE - 1)

            with pe.Fori(0, W) as w:
                window2(w)
            window2(W, msgs=False)
            window2(W + 1, msgs=False, epilogue=False)


def kernel(**inputs):
    import concourse.bacc as bacc
    from concourse.bass_utils import run_bass_kernel_spmd

    a = {k: np.ascontiguousarray(v) for k, v in inputs.items()}
    src, dst, ew = a["src"].astype(np.int32), a["dst"].astype(np.int32), a["edge_weight"]

    def columns(e, **kw):
        return np.ascontiguousarray(np.pad(e, (0, NCOL * P - N_EDGES), **kw).reshape(NCOL, P).T)

    whole = np.pad(dst, (0, NCH * P - N_EDGES), mode="edge")
    dst_rows = np.pad(whole, (0, (RB - NCH // P) * P * P - NCH % P * P), constant_values=-1)
    dst_rows = np.ascontiguousarray(dst_rows.reshape(RB, P, P).transpose(1, 0, 2))

    def col(v):
        return np.ascontiguousarray(v.reshape(-1, P).T)

    g, m, f = "L0_gnn_", "L0_mix_", "L0_ffn_"
    arrays = {
        "x": np.pad(a["x"], ((0, (W + 2) * P - N_NODES), (0, 0))),
        "src_cols": columns(src), "dst_cols": columns(dst, mode="edge"), "ew_cols": columns(ew), "dst_rows": dst_rows,
        "vecs": np.stack([a[g + "b6"], a[g + "b7"], a[g + "bp"], a[m + "g2"], a[m + "b2"]]),
        "W6T": np.ascontiguousarray(a[g + "W6"].T), "W7T": np.ascontiguousarray(a[g + "W7"].T),
        "WpT": np.ascontiguousarray(a[g + "Wp"].T),
        "Wq": a[m + "Wq"], "Wk": a[m + "Wk"], "Wv": a[m + "Wv"], "Wm": a[m + "Wm"], "W1": a[m + "W1"], "W2": a[m + "W2"],
        "ln_cols": np.ascontiguousarray(np.stack([col(a[g + n]) for n in ("ln6_g", "ln6_b", "ln7_g", "ln7_b")], 1)),
        "mix_cols": np.ascontiguousarray(np.stack([col(a[m + n]) for n in ("g1", "b1")], 1)),
        "Wg": a[f + "Wg"], "bg": a[f + "bg"].reshape(1, NE), "eW1": a[f + "W1"],
        "eb1": np.ascontiguousarray(a[f + "b1"].reshape(NE, HBLK, P).transpose(2, 0, 1)),
        "eW2": a[f + "W2"], "eb2": a[f + "b2"],
    }
    nc = bacc.Bacc("TRN2", target_bir_lowering=False, num_devices=1)
    args = [nc.dram_tensor(f"in_{n}", v.shape, mybir.dt.from_np(v.dtype), kind="ExternalInput").ap()
            for n, v in arrays.items()]
    out = nc.dram_tensor("out", ((W + 2) * P, D), F32, kind="ExternalOutput").ap()
    gps_kernel(nc, *args, out)
    r = run_bass_kernel_spmd(nc, [{f"in_{n}": v for n, v in arrays.items()}], core_ids=[0])
    return r.results[0]["out"][2 * P:2 * P + N_NODES]
```

```python
from contextlib import ExitStack

import numpy as np

import concourse.bass as bass
from concourse import mybir

ALU = mybir.AluOpType
ACT = mybir.ActivationFunctionType
AX = mybir.AxisListType
F32 = mybir.dt.float32
I32 = mybir.dt.int32
BF16 = mybir.dt.bfloat16

P = 128
N_NODES, N_EDGES, D = 6250, 200000, 256
KB = D // P
W = -(-N_NODES // P)
NCH = -(-N_EDGES // P)
U = 4
PIECES = 8
STATIC = U * PIECES
SLOTS = 16
AHEAD = 5
RU = 2
NCOL = -(-(NCH + STATIC + 2 * U) // 8) * 8
RB = -(-NCH // P)
REST_FROM = NCOL
HEADS, HD = 8, 32
HPB = P // HD
NE, HID = 8, 512
HBLK = HID // P
EPS = 1e-5
ATT_EPS = 1e-6
Q, QN = 4, P // 4
PARTS = 3
XG = 7
H_ACT = 4 * XG
RSQRT_BITS = 0x5F3759DF
NEWTON = 3
LN_LINKS = 5 + 3 * NEWTON
WEIGHT_LOADS = 20
N_CONSTS = 16
assert W % 2 == 1 and W % XG == 0 and Q * W <= 256


class Chain:

    def __init__(self, eng, sem, per, turn):
        self.eng, self.sem, self.per, self.turn, self.n = eng, sem, per, turn, 0

    def link(self, ins):
        self.n += 1
        ins.then_inc(self.sem, 1)
        self.eng.wait_ge(self.sem, self.turn * self.per + self.n)


def gps_kernel(nc, x, src_cols, dst_cols, ew_cols, dst_rows, vecs, W6T, W7T, WpT, Wq, Wk, Wv, Wm, W1, W2,
               ln_cols, mix_cols, Wg, bg, eW1, eb1, eW2, eb2, out):
    with ExitStack() as ctx:
        def sb(name, shape, dt=F32):
            return ctx.enter_context(nc.sbuf_tensor(name, shape, dt))

        sems = {}

        class Sems:
            def __getitem__(self, name):
                if name not in sems:
                    sems[name] = ctx.enter_context(nc.semaphore(name))
                return sems[name]

        s = Sems()
        dve_, act_, pe_, pool_, sp_ = nc.vector, nc.scalar, nc.tensor, nc.gpsimd, nc.sync

        xn_d = nc.dram_tensor("xn_d", [(W + 1) * P, D], F32).ap()
        h1_d = nc.dram_tensor("h1_d", [(W + 2) * P, D], F32).ap()
        h2_d = nc.dram_tensor("h2_d", [(W + 2) * P, D], F32).ap()
        x1_d = nc.dram_tensor("x1_d", [(W + 1) * P, D], F32).ap()
        r_d = nc.dram_tensor("r_d", [(W + 1) * P, D], F32).ap()

        def rows(table, block):
            return table[bass.ds(block * P, P), :]

        ident = sb("ident", [P, P])
        ones_row = sb("ones_row", [1, P])
        zero_tile = sb("zero_tile", [P, D])
        iota_p = sb("iota_p", [P, P])
        iota_q = sb("iota_q", [P, Q * W])
        iota_qb = sb("iota_qb", [P, Q * W], BF16); iota_nb = sb("iota_nb", [P, QN], BF16)
        win_first = sb("win_first", [P, W + 1])
        chunk_id = sb("chunk_id", [P, RB])
        headmask = sb("headmask", [P, HPB])
        lowtri = sb("lowtri", [P, NE, NE])
        valid = sb("valid", [P, W])
        src_row = sb("src_row", [P, NCOL], I32)
        dst_f = sb("dst_f", [P, NCOL])
        ew = sb("ew", [P, NCOL])
        w6 = sb("w6", [P, KB, D]); w7 = sb("w7", [P, KB, D]); wp = sb("wp", [P, KB, D])
        wq = sb("wq", [P, KB, D]); wk = sb("wk", [P, KB, D]); wv = sb("wv", [P, KB, D]); wm = sb("wm", [P, KB, D])
        w1 = sb("w1", [P, 2 * KB, HID]); w2 = sb("w2", [P, HBLK, D])
        lncol = sb("lncol", [P, 4, KB])
        mixcol = sb("mixcol", [P, 2, KB])
        vec = sb("vec", [P, 6, D])
        hb = sb("hb", [1, 2, D])
        w1bias = sb("w1bias", [P, HBLK])
        wg = sb("wg", [P, KB, NE]); bgr = sb("bgr", [P, NE])
        experts = sb("experts", [P, NE * (KB * HID + HBLK * D)])
        ew1 = experts[:, 0:NE * KB * HID].rearrange("p (e k n) -> p e k n", e=NE, k=KB)
        ew2 = experts[:, NE * KB * HID:].rearrange("p (e k n) -> p e k n", e=NE, k=HBLK)
        eb1c = sb("eb1c", [P, NE, HBLK]); eb2r = sb("eb2r", [NE, D])
        tab = sb("tab", [1, 7, W + 1], I32)
        st_all = sb("st_all", [P, W, 6]); mean_all = sb("mean_all", [P, W]); var_all = sb("var_all", [P, W])
        rstd_all = sb("rstd_all", [P, W]); shift_all = sb("shift_all", [P, W]); rstd2_all = sb("rstd2_all", [P, W])
        w_s1 = sb("w_s1", [P, W]); w_s2 = sb("w_s2", [P, W]); w_s3 = sb("w_s3", [P, W])
        deg_q = sb("deg_q", [QN, Q * W]); dis_q = sb("dis_q", [QN, Q, W])
        dis = sb("dis", [P, W + 1])
        idx_s = sb("idx_s", [P, SLOTS], I32); idx_r = sb("idx_r", [P, RU], I32)
        gs = sb("gs", [P, SLOTS, D]); gr = sb("gr", [P, RU, D])
        ss = sb("ss", [P, SLOTS, P]); sr = sb("sr", [P, RU, P])
        iw = sb("iw", [P, P])
        hself = sb("hself", [P, D])
        kvx = sb("kvx", [P, KB, P + HPB])
        t_a = [sb(f"t_a{i}", [P, D]) for i in range(2)]
        t_b = [sb(f"t_b{i}", [P, D]) for i in range(2)]
        t_c = [sb(f"t_c{i}", [P, D]) for i in range(2)]
        xT = sb("xT", [P, KB, P]); zT = sb("zT", [P, KB, P]); mT = sb("mT", [P, KB, P]); nT = sb("nT", [P, KB, P])
        xn_keep = sb("xn_keep", [P, D])
        u1 = sb("u1", [P, D]); u2 = sb("u2", [P, D]); u3 = sb("u3", [P, D]); u4 = sb("u4", [P, D]); u5 = sb("u5", [P, D])
        u6 = sb("u6", [P, D]); u7 = sb("u7", [P, D]); u8 = sb("u8", [P, D])
        vx = sb("vx", [P, KB, P + 1])
        hT = [sb(f"hT{i}", [P, HBLK, P]) for i in range(2)]
        st = sb("st", [P, 6]); mv = sb("mv", [P, 2]); rstd = sb("rstd", [P, 4])
        st2 = sb("st2", [P, 6]); mv2 = sb("mv2", [P, 2]); rstd2 = sb("rstd2", [P, 4])
        zden = sb("zden", [P, KB, HPB]); zrec = sb("zrec", [P, KB, HPB])
        lg = sb("lg", [P, NE]); cmp1 = sb("cmp1", [P, NE, NE]); cmp2 = sb("cmp2", [P, NE, NE]); rank = sb("rank", [P, NE])
        mask_n = sb("mask_n", [P, NE]); mask_c = sb("mask_c", [P, NE]); maskT = sb("maskT", [NE, P])

        bank = [ctx.enter_context(nc.psum_tensor(f"bank{i}", [P, 512], F32)) for i in range(8)]

        def half(b, n=P):
            return bank[b][:, 0:KB * n].rearrange("p (k n) -> p k n", k=KB)

        acc = bank[0][:, 0:D]

        def wide(b):
            return bank[b][:, 0:D]

        def col(ap, shape):
            return ap.to_broadcast(shape)

        flat_gs = gs[:, :, :].rearrange("p a b -> p (a b)")
        drow_i = flat_gs[:, 0:RB * P].bitcast(I32).rearrange("p (b e) -> p b e", b=RB)
        drow_f = flat_gs[:, RB * P:2 * RB * P].rearrange("p (b e) -> p b e", b=RB)
        assert 2 * RB * P <= SLOTS * D
        flat_ss = ss[:, :, :].rearrange("p a b -> p (a b)")
        touch = [flat_ss[:, i * W * RB:(i + 1) * W * RB].rearrange("p (w b) -> p w b", w=W) for i in range(3)]
        assert 3 * W * RB <= SLOTS * P
        dst_i = dst_f[:, :].bitcast(I32)
        xh = experts[:, 0:W * D].rearrange("p (t d) -> p t d", t=W)

        class Carve:

            def __init__(self, flat, at, end):
                self.flat, self.at, self.end = flat, at, end

            def take(self, n, dt=F32):
                words = n if dt == F32 else -(-n // 2)
                piece = self.flat[:, self.at:self.at + words]
                self.at += words
                assert self.at <= self.end
                return piece if dt == F32 else piece.bitcast(dt)

        tail = Carve(experts, W * D, NE * (KB * HID + HBLK * D))
        ew_parts = tail.take(NCOL * PARTS, BF16).rearrange("p (c a) -> p c a", a=PARTS)
        dst_n = tail.take(NCOL, BF16)
        range_part, range_all = tail.take(2 * W), tail.take(2 * W)
        rg = tail.take(6 * W)[0:1, :].rearrange("p (a w) -> p a w", w=W)
        rg_i = tail.take(2 * W)[0:1, :].bitcast(I32).rearrange("p (a w) -> p a w", w=W)
        cmin, cmax = tail.take(RB), tail.take(RB)
        room = Carve(flat_gs, 0, SLOTS * D)
        wide_s = room.take(NCOL)
        dst_q = room.take(NCOL, BF16)
        oh_node = [room.take(STATIC * QN, BF16).rearrange("p (c n) -> p c n", n=QN) for _ in range(2)]
        oh_q = room.take(STATIC * Q, BF16).rearrange("p (c q) -> p c q", q=Q)
        oh_w = [room.take(STATIC * PARTS * Q, BF16).rearrange("p (c a q) -> p c a q", a=PARTS, q=Q) for _ in range(2)]
        ohr_node = room.take(RU * QN, BF16).rearrange("p (c n) -> p c n", n=QN)
        ohr_q = room.take(RU * Q, BF16).rearrange("p (c q) -> p c q", q=Q)
        ohr_w = room.take(RU * PARTS * Q, BF16).rearrange("p (c a q) -> p c a q", a=PARTS, q=Q)

        block = ctx.enter_context(nc.Block())

        def first_column(eng, w):
            return eng.value_load(tab[0:1, 0, bass.ds(w, 1)], min_val=0, max_val=NCH)

        def end_column(eng, layer, w):
            end = eng.value_load(tab[0:1, 1, bass.ds(w, 1)], min_val=STATIC + 1, max_val=NCOL - RU + 1)
            off = eng.value_load(tab[0:1, 2 + layer, bass.ds(w, 1)], min_val=0, max_val=(2 * W + 1) * NCOL)
            return end, off

        def rest_table(eng, layer, w):
            n = eng.value_load(tab[0:1, 4, bass.ds(w, 1)], min_val=RU, max_val=NCOL)
            base = eng.value_load(tab[0:1, 5 + layer, bass.ds(w, 1)], min_val=0, max_val=2 * W * NCOL)
            return n, base

        @block.sync
        def _(sp):
            for dst_t, src_t in ((dst_i, dst_cols), (ew[:, :], ew_cols), (src_row[:, :], src_cols)):
                sp.dma_start(dst_t, src_t).then_inc(s["edges_in"], 16)
            sp.dma_start(drow_i, dst_rows).then_inc(s["rows_in"], 16)
            for i in range(0, W, XG):
                sp.dma_start(xh[:, i:i + XG, :],
                             x[i * P:(i + XG) * P, :].rearrange("(t p) d -> p t d", p=P)).then_inc(s["x_in"], 16)
            n = 0
            for t, a in ((w6, W6T), (w7, W7T), (wp, WpT), (wq, Wq), (wk, Wk), (wv, Wv), (wm, Wm), (w1, W1), (w2, W2)):
                sp.dma_start(t[:, :, :], a.rearrange("(k p) n -> p k n", p=P)).then_inc(s["weights_in"], 16)
                n += 1
            for i in range(5):
                sp.dma_start(vec[:, i, :], vecs[i:i + 1, :].to_broadcast([P, D])).then_inc(s["weights_in"], 16)
                n += 1
            with nc.allow_non_contiguous_dma(reason="a few columns"):
                sp.dma_start(lncol[:, :, :], ln_cols).then_inc(s["weights_in"], 16)
                sp.dma_start(mixcol[:, :, :], mix_cols).then_inc(s["weights_in"], 16)
                sp.dma_start(wg[:, :, :], Wg.rearrange("(k p) n -> p k n", p=P)).then_inc(s["weights_in"], 16)
                sp.dma_start(bgr[:, :], bg.to_broadcast([P, NE])).then_inc(s["weights_in"], 16)
                sp.dma_start(eb1c[:, :, :], eb1).then_inc(s["weights_in"], 16)
                sp.dma_start(eb2r[:, :], eb2).then_inc(s["weights_in"], 16)
                n += 6
            assert n == WEIGHT_LOADS
            sp.wait_ge(s["consts"], N_CONSTS)
            for table, b in ((xn_d, W), (h1_d, 0), (h1_d, W + 1), (h2_d, W + 1), (x1_d, W), (r_d, 0)):
                sp.dma_start(rows(table, b), zero_tile[:, :]).then_inc(s["blank_out"], 16)

            def tile(t, b):
                r0 = sp.snap(t * P) if not isinstance(t, int) else t * P
                sp.wait_ge(s["xn_done"], t + 1)
                sp.dma_start(xn_d[bass.ds(r0, P), :], t_b[b][:, :]).then_inc(s[f"xn_out{b}"], 16)

            tile(0, 0)
            with sp.Fori(0, (W - 1) // 2) as p:
                tile(2 * p + 1, 1)
                tile(2 * p + 2, 0)
            sp.wait_ge(s["dis_set"], 1)
            for q in range(Q):
                sp.dma_start(dis[q * QN:(q + 1) * QN, 1:W + 1], dis_q[:, q, :]).then_inc(s["dis_in"], 16)
            for n in range(W // XG):
                mine = n % 2 == 0
                g = n // 2 if mine else H_ACT // XG + n // 2
                sp.wait_ge(s["h_dve" if mine else "h_act"], (n // 2 + 1) * XG)
                sp.dma_start(h1_d[(g * XG + 1) * P:((g + 1) * XG + 1) * P, :].rearrange("(t p) d -> p t d", p=P),
                             xh[:, g * XG:(g + 1) * XG, :]).then_inc(s["h1_out"], 16)

            sp.wait_ge(s["blank_out"], 16 * 6)
            sp.wait_ge(s["kv_acc"], W)
            sp.wait_ge(s["h1_out"], 16 * (W // XG))
            for b in range(2):
                sp.wait_ge(s[f"xn_out{b}"], 16 * ((W + 1 - b) // 2))
            sp.sem_inc(s["table1"], 1)
            sp.dma_start(hself[:, :], rows(h1_d, 1)).then_inc(s["self_in"], 16)
            sp.dma_start(u1[:, :], rows(xn_d, 0)).then_inc(s["xn_in"], 16)
            for e in range(NE):
                sp.dma_start(ew1[:, e, :, :], eW1[e].rearrange("(k p) n -> p k n", p=P)).then_inc(s["experts_in"], 16)
                sp.dma_start(ew2[:, e, :, :], eW2[e].rearrange("(k p) n -> p k n", p=P)).then_inc(s["experts_in"], 16)
            with sp.Fori(0, W) as w:
                here, after, after2 = sp.snap(w * P), sp.snap((w + 1) * P), sp.snap((w + 2) * P)
                sp.wait_ge(s["self_used"], w + 1)
                sp.dma_start(hself[:, :], h1_d[bass.ds(after2, P), :]).then_inc(s["self_in"], 16)
                sp.wait_ge(s["r_done"], w)
                sp.dma_start(u2[:, :], x[bass.ds(here, P), :]).then_inc(s["x_again"], 16)
                sp.wait_ge(s["xn1_tp"], w + 1)
                sp.wait_ge(s["xn_kept"], w + 1)
                sp.dma_start(u1[:, :], xn_d[bass.ds(after, P), :]).then_inc(s["xn_in"], 16)
                sp.wait_ge(s["h2_done"], w + 1)
                sp.dma_start(h2_d[bass.ds(here, P), :], u4[:, :]).then_inc(s["h2_out"], 16)
                sp.wait_ge(s["x1_done"], w + 1)
                sp.dma_start(x1_d[bass.ds(here, P), :], u5[:, :]).then_inc(s["x1_out"], 16)
                sp.wait_ge(s["r_done"], w + 1)
                sp.dma_start(r_d[bass.ds(after, P), :], u6[:, :]).then_inc(s["r_out"], 16)
            sp.wait_ge(s["h2_done"], W + 1)
            sp.dma_start(rows(h2_d, W), u4[:, :]).then_inc(s["h2_out"], 16)

            sp.wait_ge(s["h2_out"], 16 * (W + 1))
            sp.wait_ge(s["x1_out"], 16 * W)
            sp.wait_ge(s["r_out"], 16 * W)
            sp.wait_ge(s["self_in"], 16 * (W + 1))
            sp.wait_ge(s["xn_in"], 16 * (W + 1))
            sp.sem_inc(s["table2"], 1)
            sp.dma_start(hself[:, :], rows(h2_d, 1)).then_inc(s["self2_in"], 16)
            sp.dma_start(u1[:, :], rows(x1_d, 0)).then_inc(s["x1_in"], 16)

            def out_tile(w):
                sp.wait_ge(s["facc"], (NE + 1) * (w + 1))
                sp.dma_start(rows(out, w), u8[:, :]).then_inc(s["out_stored"], 16)

            def r_tile(w):
                sp.wait_ge(s["x3_done"], w)
                sp.dma_start(u2[:, :], rows(r_d, w)).then_inc(s["r_in"], 16)

            with sp.Fori(0, W) as w:
                here, nxt, nxt2 = sp.snap(w * P), sp.snap((w + 1) * P), sp.snap((w + 2) * P)
                sp.wait_ge(s["x3_done"], w)
                sp.dma_start(u2[:, :], r_d[bass.ds(here, P), :]).then_inc(s["r_in"], 16)
                sp.wait_ge(s["self2_used"], w + 1)
                sp.dma_start(hself[:, :], h2_d[bass.ds(nxt2, P), :]).then_inc(s["self2_in"], 16)
                sp.wait_ge(s["x2_done"], w + 2)
                sp.dma_start(u1[:, :], x1_d[bass.ds(nxt, P), :]).then_inc(s["x1_in"], 16)
                sp.wait_ge(s["facc"], (NE + 1) * (w + 1))
                sp.dma_start(out[bass.ds(here, P), :], u8[:, :]).then_inc(s["out_stored"], 16)
            r_tile(W)
            out_tile(W)
            out_tile(W + 1)
            sp.wait_ge(s["out_stored"], 16 * (W + 2))
            sp.wait_ge(s["self2_in"], 16 * (W + 1))
            sp.wait_ge(s["x1_in"], 16 * (W + 1))

        @block.gpsimd
        def _(pool):
            c = s["consts"]
            n = 0

            def const(ins):
                nonlocal n
                n += 1
                ins.then_inc(c, 1)

            const(pool.memset(ident[:, :], 0.0))
            const(pool.memset(ones_row[:, :], 1.0))
            const(pool.memset(zero_tile[:, :], 0.0))
            const(pool.memset(headmask[:, :], 1.0))
            const(pool.memset(valid[:, :], 1.0))
            const(pool.memset(lowtri[:, :, :], 1.0))
            const(pool.iota(iota_p[:, :], [[1, P]], channel_multiplier=0, allow_small_or_imprecise_dtypes=True))
            const(pool.iota(iota_q[:, :], [[1, Q * W]], channel_multiplier=0, allow_small_or_imprecise_dtypes=True))
            const(pool.memset(win_first[:, W:W + 1], 0.0))
            const(pool.iota(win_first[:, 0:W], [[P, W]], channel_multiplier=0, allow_small_or_imprecise_dtypes=True))
            const(pool.iota(chunk_id[:, :], [[P, RB]], channel_multiplier=1, allow_small_or_imprecise_dtypes=True))
            pool.wait_ge(c, n)
            const(pool.affine_select(out=ident[:, :], in_=ident[:, :], compare_op=ALU.not_equal, fill=1.0, base=0,
                                     pattern=[[-1, P]], channel_multiplier=1))
            const(pool.affine_select(out=valid[:, :], in_=valid[:, :], compare_op=ALU.is_ge, fill=0.0,
                                     base=N_NODES - 1, pattern=[[-P, W]], channel_multiplier=-1))
            const(pool.affine_select(out=headmask[:, :], in_=headmask[:, :], compare_op=ALU.is_ge, fill=0.0,
                                     base=0, pattern=[[-HD, HPB]], channel_multiplier=1))
            const(pool.affine_select(out=lowtri[:, :, :], in_=lowtri[:, :, :], compare_op=ALU.is_ge, fill=0.0,
                                     base=-1, pattern=[[1, NE], [-1, NE]], channel_multiplier=0))
            pool.wait_ge(c, n)
            const(pool.affine_select(out=headmask[:, :], in_=headmask[:, :], compare_op=ALU.is_ge, fill=0.0,
                                     base=HD - 1, pattern=[[HD, HPB]], channel_multiplier=-1))
            assert n == N_CONSTS
            pool.wait_ge(s["range_parts"], 2)
            pool.partition_all_reduce(range_all, range_part, P, bass.bass_isa.ReduceOp.max).then_inc(s["range_max"], 1)
            def gathers(layer, table):
                pool.wait_ge(s[f"table{layer + 1}"], 1)
                with pool.Fori(0, W) as w:
                    v = layer * W * STATIC + w * STATIC
                    for n in range(STATIC):
                        slot = n % SLOTS
                        if n % U == 0:
                            pool.wait_ge(s["idx_set"], v + n + U)
                            pool.sem_inc(s["pool_gate"], 1)
                        pool.indirect_dma_start(
                            gs[:, slot, :], None, table[:, :],
                            bass.IndirectOffsetOnAxis(ap=idx_s[:, slot:slot + 1], axis=0)).then_inc(s[f"main_in{slot}"], 16)
                        if n == STATIC // 2:
                            n_rest, base = rest_table(pool, layer, w)
                    with pool.Fori(0, n_rest, RU) as i:
                        pool.wait_ge(s["idx_rest_set"], base + i + RU)
                        pool.sem_inc(s["pool_gate"], 1)
                        for j in range(RU):
                            pool.indirect_dma_start(
                                gr[:, j, :], None, table[:, :],
                                bass.IndirectOffsetOnAxis(ap=idx_r[:, j:j + 1], axis=0)).then_inc(s[f"rest_in{j}"], 16)

            pool.wait_ge(s["tab_set"], 7)
            gathers(0, h1_d)
            gathers(1, h2_d)

        @block.scalar
        def _(act):
            act.wait_ge(s["consts"], N_CONSTS)

            def xn_tile(t, b, p):
                act.wait_ge(s[f"xn_out{b}"], 16 * p)
                act.wait_ge(s["xn_tp"], t)
                act.activation(t_b[b][:, :], xh[:, bass.ds(t, 1), :], ACT.Identity, scale=rstd_all[:, bass.ds(t, 1)],
                               bias=shift_all[:, bass.ds(t, 1)]).then_inc(s["xn_done"], 1)

            def turned(t):
                act.wait_ge(s["xn_tp"], t + 1)
                act.wait_ge(s["h_ps"], t)
                act.copy(xT[:, :, :], half(1)).then_inc(s["xT_set"], 1)

            def key_value(t):
                act.wait_ge(s["k_min"], t + 1)
                act.wait_ge(s["k_done"], t)
                act.activation(u3[:, :], u2[:, :], ACT.Exp).then_inc(s["k_exp"], 1)
                act.wait_ge(s["v_ps"], t + 1)
                act.wait_ge(s["kv_acc"], t)
                act.activation(vx[:, :, 0:P], half(4), ACT.Copy, scale=valid[:, bass.ds(t, 1)])
                act.copy(vx[:, :, P:P + 1], valid[:, bass.ds(t, 1)].unsqueeze(1).to_broadcast([P, KB, 1])
                         ).then_inc(s["v_set"], 1)

            act.wait_ge(s["stats_set"], 1)
            xn_tile(0, 0, 0)
            turned(0)
            with act.Fori(0, (W - 1) // 2) as p:
                xn_tile(2 * p + 1, 1, p)
                key_value(2 * p)
                turned(2 * p + 1)
                xn_tile(2 * p + 2, 0, p + 1)
                key_value(2 * p + 1)
                turned(2 * p + 2)
            key_value(W - 1)
            act.wait_ge(s["dis_in"], 16 * Q)
            act.wait_ge(s["h_set"], W)
            with act.Fori(H_ACT, W) as t:
                act.activation(xh[:, bass.ds(t, 1), :], xh[:, bass.ds(t, 1), :], ACT.Copy,
                               scale=dis[:, bass.ds(t + 1, 1)]).then_inc(s["h_act"], 1)

            def next_h(w):
                act.wait_ge(s["z1_tp"], w + 1)
                act.wait_ge(s["h7_ps"], w)
                act.copy(zT[:, :, :], half(1)).then_inc(s["z1T_set"], 1)

            def next_h_scaled(w):
                act.wait_ge(s["h7_ps"], w + 1)
                act.wait_ge(s["h2_out"], 16 * w)
                act.activation(u4[:, :], wide(7), ACT.Copy, scale=dis[:, bass.ds(w, 1)]).then_inc(s["h2_done"], 1)

            with act.Fori(0, W) as w:
                act.wait_ge(s["xn1_tp"], w + 1)
                act.wait_ge(s["hh_ps"], w)
                act.copy(xT[:, :, :], half(5)).then_inc(s["xn1T_set"], 1)
                act.wait_ge(s["q_min"], w + 1)
                act.activation(t_a[1][:, :], t_a[0][:, :], ACT.Exp).then_inc(s["q_exp"], 1)
                act.wait_ge(s["x1_done"], w)
                act.copy(xn_keep[:, :], u1[:, :]).then_inc(s["xn_kept"], 1)
                next_h(w)
                act.wait_ge(s["msg_tp"], w + 1)
                act.wait_ge(s["m_ps"], w)
                act.copy(mT[:, :, :], half(5)).then_inc(s["msgT_set"], 1)
                next_h_scaled(w)
                act.wait_ge(s["mn_tp"], w + 1)
                act.copy(nT[:, :, :], half(5)).then_inc(s["mnT_set"], 1)
                act.wait_ge(s["hh_ps"], w + 1)
                act.wait_ge(s["y1_ps"], w)
                for j in range(HBLK):
                    act.activation(hT[0][:, j, :], bank[6][:, j * P:(j + 1) * P], ACT.Relu,
                                   bias=w1bias[:, j:j + 1]).then_inc(s["hr_done"], 1)
            next_h(W)
            next_h_scaled(W)

            act.wait_ge(s["zn_blank"], 1)
            act.wait_ge(s["y1_ps"], W)

            def window2(w, epilogue=True):
                act.wait_ge(s["zn_set"], w)
                act.wait_ge(s["hid_ps"], NE * w)
                act.copy(nT[:, :, :], zT[:, :, :]).then_inc(s["zc_set"], 1)
                if epilogue:
                    act.wait_ge(s["x2_tp"], w + 1)
                    act.wait_ge(s["p_ps"], w)
                    act.copy(xT[:, :, :], half(1)).then_inc(s["x2T_set"], 1)
                for e in range(NE):
                    if epilogue and e == 3:
                        act.wait_ge(s["z3_tp"], w + 1)
                        act.wait_ge(s["zc_set"], w + 1)
                        act.copy(zT[:, :, :], half(1)).then_inc(s["zn_set"], 1)
                    if epilogue and e == 5:
                        act.wait_ge(s["mt_ps"], w + 1)
                        act.wait_ge(s["b2_ps"], w)
                        act.copy(maskT[:, :], bank[3][0:NE, P // 2:P // 2 + P]).then_inc(s["maskT_set"], 1)
                    act.wait_ge(s["hid_ps"], NE * w + e + 1)
                    act.wait_ge(s["y_ps"], NE * w + e + 1)
                    for j in range(HBLK):
                        act.activation(hT[e % 2][:, j, :], bank[(6, 2)[e % 2]][:, j * P:(j + 1) * P], ACT.Gelu,
                                       bias=eb1c[:, e, j:j + 1]).then_inc(s["gelu_done"], 1)

            with act.Fori(0, W) as w:
                window2(w)
            window2(W)
            window2(W + 1, epilogue=False)

        def inv_sqrt(dve, ch, v, minus_half, y, t):
            dve.tensor_scalar(minus_half, v, -0.5, None, ALU.mult)
            ch.link(dve.tensor_scalar(y.bitcast(I32), v.bitcast(I32), 1, None, ALU.arith_shift_right))
            ch.link(dve.tensor_scalar(y.bitcast(I32), y.bitcast(I32), -1.0, float(RSQRT_BITS), ALU.mult, ALU.add))
            for _ in range(NEWTON):
                ch.link(dve.tensor_tensor(t, y, y, ALU.mult))
                ch.link(dve.tensor_tensor(t, t, minus_half, ALU.mult))
                ch.link(dve.scalar_tensor_tensor(out=y, in0=t, scalar=1.5, in1=y, op0=ALU.add, op1=ALU.mult))

        def layer_norm(dve, ch, xin, xout, stats, mean_var, sc):
            ch.link(dve.bn_stats(stats[:, :], xin))
            dve.sem_inc(s["dve_gate"], 1)
            ch.link(dve.bn_aggr(mean_var[:, :], stats[:, :]))
            ch.link(dve.tensor_scalar(sc[:, 0:1], mean_var[:, 1:2], EPS, None, ALU.add))
            inv_sqrt(dve, ch, sc[:, 0:1], sc[:, 1:2], sc[:, 2:3], sc[:, 3:4])
            return dve.tensor_scalar(xout, xin, mean_var[:, 0:1], sc[:, 2:3], ALU.subtract, ALU.mult)

        @block.vector
        def _(dve):
            ch = Chain(dve, s["dve_setup"], 0, 0)
            dve.wait_ge(s["consts"], N_CONSTS)
            dve.wait_ge(s["rows_in"], 16)
            ch.link(dve.tensor_copy(drow_f, drow_i))
            dve.tensor_reduce(cmin, drow_f, AX.X, ALU.min)
            ch.link(dve.tensor_reduce(cmax, drow_f, AX.X, ALU.max))
            wins = win_first[:, 0:W].unsqueeze(2).to_broadcast([P, W, RB])
            ch.link(dve.tensor_scalar(cmin, cmin, float(1 - P), None, ALU.add))
            dve.tensor_tensor(touch[0], wins, cmin.unsqueeze(1).to_broadcast([P, W, RB]), ALU.is_ge)
            ch.link(dve.tensor_tensor(touch[1], wins, cmax.unsqueeze(1).to_broadcast([P, W, RB]), ALU.is_le))
            ch.link(dve.tensor_tensor(touch[0], touch[0], touch[1], ALU.mult))
            ids = chunk_id[:, :].unsqueeze(1).to_broadcast([P, W, RB])
            ch.link(dve.tensor_tensor(touch[1], touch[0], ids, ALU.mult))
            ch.link(dve.tensor_tensor(touch[2], touch[1], touch[0], ALU.add))
            dve.tensor_reduce(range_part[:, W:2 * W], touch[2], AX.X, ALU.max).then_inc(s["range_parts"], 1)
            ch.link(dve.tensor_scalar(touch[0], touch[0], float(NCH), None, ALU.mult))
            ch.link(dve.tensor_tensor(touch[0], touch[0], touch[1], ALU.subtract))
            dve.tensor_reduce(range_part[:, 0:W], touch[0], AX.X, ALU.max).then_inc(s["range_parts"], 1)
            dve.wait_ge(s["edges_in"], 16 * 3)
            ints = wide_s.bitcast(I32)
            ch.link(dve.tensor_scalar(ints, dst_i, QN.bit_length() - 1, None, ALU.arith_shift_right))
            ch.link(dve.tensor_copy(dst_q, ints))
            ch.link(dve.tensor_scalar(ints, dst_i, QN - 1, None, ALU.bitwise_and))
            ch.link(dve.tensor_copy(dst_n, ints))
            ch.link(dve.tensor_copy(dst_f[:, :], dst_i))
            dve.tensor_scalar(src_row[:, :], src_row[:, :], P, None, ALU.add)
            ch.link(dve.tensor_copy(ew_parts[:, :, 0], ew[:, :]))
            ch.link(dve.tensor_tensor(wide_s, ew[:, :], ew_parts[:, :, 0], ALU.subtract))
            ch.link(dve.tensor_copy(ew_parts[:, :, 1], wide_s))
            ch.link(dve.tensor_tensor(wide_s, wide_s, ew_parts[:, :, 1], ALU.subtract))
            dve.tensor_copy(ew_parts[:, :, 2], wide_s)
            dve.tensor_copy(iota_qb[:, :], iota_q[:, :])
            ch.link(dve.tensor_copy(iota_nb[:, :], iota_p[:, 0:QN]))
            dve.wait_ge(s["range_max"], 1)
            first, ngr, rest, cum = rg[:, 0, :], rg[:, 1, :], rg[:, 2, :], rg[:, 3, :]
            ch.link(dve.tensor_scalar(first, range_all[0:1, 0:W], -1.0, float(NCH), ALU.mult, ALU.add))
            ch.link(dve.tensor_tensor(ngr, range_all[0:1, W:2 * W], first, ALU.subtract))
            ch.link(dve.tensor_scalar(rg_i[:, 0, :], ngr, float(RU - 1), 0.0, ALU.add, ALU.max))
            ch.link(dve.tensor_scalar(rg_i[:, 1, :], rg_i[:, 0, :], RU.bit_length() - 1, None, ALU.arith_shift_right))
            ch.link(dve.tensor_scalar(rest, rg_i[:, 1, :], float(STATIC // RU + 1), float(-STATIC // RU), ALU.max, ALU.add))
            step, a, b = 1, 2, 3
            while step < W:
                dve.tensor_copy(rg[:, b, 0:step], rg[:, a, 0:step])
                ch.link(dve.tensor_tensor(rg[:, b, step:W], rg[:, a, step:W], rg[:, a, 0:W - step], ALU.add))
                a, b, step = b, (4 if b == 3 else 3), 2 * step
            total = rg[:, a, :]
            dve.tensor_scalar(tab[:, 4, 0:W], rest, float(RU), None, ALU.mult).then_inc(s["tab_set"], 1)
            ch.link(dve.tensor_scalar(rg[:, 1, :], rest, float(RU), float(STATIC), ALU.mult, ALU.add))
            dve.tensor_copy(tab[:, 0, W:W + 1], first[:, 0:1])
            dve.tensor_copy(tab[:, 0, 0:W], first).then_inc(s["tab_set"], 1)
            dve.tensor_tensor(tab[:, 1, 0:W], first, rg[:, 1, :], ALU.add).then_inc(s["tab_set"], 1)
            ch.link(dve.tensor_tensor(rg[:, 5, :], total, rest, ALU.subtract))
            dve.tensor_scalar(tab[:, 5, 0:W], rg[:, 5, :], float(RU), None, ALU.mult).then_inc(s["tab_set"], 1)
            ch.link(dve.tensor_scalar(rg[:, 1, 0:1], total[:, W - 1:W], float(RU), None, ALU.mult))
            dve.tensor_scalar(tab[:, 6, 0:W], rg[:, 5, :], float(RU), rg[:, 1, 0:1], ALU.mult, ALU.add).then_inc(s["tab_set"], 1)
            ch.link(dve.tensor_scalar(rg[:, 5, :], rg[:, 5, :], float(RU), float(REST_FROM - STATIC), ALU.mult, ALU.add))
            ch.link(dve.tensor_tensor(rg[:, 5, :], rg[:, 5, :], first, ALU.subtract))
            dve.tensor_copy(tab[:, 2, 0:W], rg[:, 5, :]).then_inc(s["tab_set"], 1)
            dve.tensor_scalar(tab[:, 3, 0:W], rg[:, 5, :], rg[:, 1, 0:1], None, ALU.add).then_inc(s["tab_set"], 1)
            dve.wait_ge(s["weights_in"], 16 * WEIGHT_LOADS)
            dve.tensor_tensor(vec[:, 5, :], vec[:, 4, :], vec[:, 2, :], ALU.add)
            dve.wait_ge(s["shift_ps"], 3)
            dve.tensor_copy(hb[:, 0, :], bank[1][0:1, 0:D])
            dve.tensor_copy(hb[:, 1, :], bank[2][0:1, 0:D])
            dve.tensor_copy(w1bias[:, :], bank[3][:, 0:HBLK])
            for k in range(KB):
                dve.tensor_scalar(w6[:, k, :], w6[:, k, :], lncol[:, 0, k:k + 1], None, ALU.mult)
                dve.tensor_scalar(w7[:, k, :], w7[:, k, :], lncol[:, 2, k:k + 1], None, ALU.mult)
                last = dve.tensor_scalar(w1[:, KB + k, :], w1[:, KB + k, :], mixcol[:, 0, k:k + 1], None, ALU.mult)
            ch.link(last)
            dve.sem_inc(s["weights_set"], 1)

            dve.wait_ge(s["hb_ps"], 1)
            dve.tensor_copy(u8[:, :], wide(2))
            dve.wait_ge(s["x_in"], 16 * (W // XG))
            with dve.Fori(0, W // XG) as g:
                for i in range(XG):
                    dve.bn_stats(st_all[:, bass.ds(g * XG + i, 1), :].rearrange("p a b -> p (a b)"),
                                 xh[:, bass.ds(g * XG + i, 1), :].rearrange("p a b -> p (a b)")).then_inc(s["bn_all"], 1)
            dve.wait_ge(s["bn_all"], W)

            def stat(i):
                return st_all[:, :, i]

            dve.tensor_tensor(w_s1[:, :], stat(1), stat(4), ALU.subtract)
            dve.tensor_tensor(w_s2[:, :], stat(2), stat(5), ALU.add)
            ch.link(dve.tensor_tensor(mean_all[:, :], stat(1), stat(4), ALU.add))
            dve.tensor_scalar(mean_all[:, :], mean_all[:, :], 0.5, None, ALU.mult)
            ch.link(dve.scalar_tensor_tensor(out=w_s1[:, :], in0=w_s1[:, :], scalar=0.25, in1=w_s1[:, :], op0=ALU.mult,
                                             op1=ALU.mult))
            ch.link(dve.scalar_tensor_tensor(out=var_all[:, :], in0=w_s2[:, :], scalar=1.0 / D, in1=w_s1[:, :],
                                             op0=ALU.mult, op1=ALU.add))
            ch.link(dve.tensor_scalar(w_s1[:, :], var_all[:, :], EPS, None, ALU.add))
            inv_sqrt(dve, ch, w_s1[:, :], w_s2[:, :], rstd_all[:, :], w_s3[:, :])
            ch.link(dve.scalar_tensor_tensor(out=shift_all[:, :], in0=mean_all[:, :], scalar=-1.0, in1=rstd_all[:, :],
                                             op0=ALU.mult, op1=ALU.mult))
            dve.sem_inc(s["stats_set"], 1)
            ch.link(dve.tensor_tensor(w_s1[:, :], rstd_all[:, :], rstd_all[:, :], ALU.mult))
            ch.link(dve.tensor_tensor(w_s1[:, :], w_s1[:, :], var_all[:, :], ALU.mult))
            ch.link(dve.tensor_scalar(w_s1[:, :], w_s1[:, :], EPS, None, ALU.add))
            inv_sqrt(dve, ch, w_s1[:, :], w_s2[:, :], rstd2_all[:, :], w_s3[:, :])
            dve.wait_ge(s["tab_set"], 7)

            def degrees(t, b, lo, next_first=False):
                mine = iota_qb[:, bass.ds(t * Q, Q)]
                if not isinstance(t, int):
                    dve.wait_ge(s["deg_ps"], t - 1)
                dve.tensor_tensor(oh_q, dst_q[:, bass.ds(lo, STATIC)].unsqueeze(2).to_broadcast([P, STATIC, Q]),
                                  mine.unsqueeze(1).to_broadcast([P, STATIC, Q]), ALU.is_equal)
                dve.tensor_tensor(
                    oh_node[b], iota_nb[:, :].unsqueeze(1).to_broadcast([P, STATIC, QN]),
                    dst_n[:, bass.ds(lo, STATIC)].unsqueeze(2).to_broadcast([P, STATIC, QN]),
                    ALU.is_equal).then_inc(s["dve_deg"], 1)
                end, off = end_column(dve, 0, t)
                if next_first:
                    first = first_column(dve, t + 1)
                dve.wait_ge(s["dve_deg"], t + 1)
                dve.tensor_tensor(oh_w[b], oh_q.unsqueeze(2).to_broadcast([P, STATIC, PARTS, Q]),
                                  ew_parts[:, bass.ds(lo, STATIC), :].unsqueeze(3).to_broadcast([P, STATIC, PARTS, Q]),
                                  ALU.mult).then_inc(s["deg_set"], 1)
                return (lo, mine, end, off), first if next_first else None

            def degrees_rest(lo, mine, end, off):
                with dve.Fori(lo + STATIC, end, RU) as col0:
                    dve.wait_ge(s["deg_rest_used"], col0 + off + RU)
                    dve.tensor_tensor(ohr_q, dst_q[:, bass.ds(col0, RU)].unsqueeze(2).to_broadcast([P, RU, Q]),
                                      mine.unsqueeze(1).to_broadcast([P, RU, Q]), ALU.is_equal)
                    dve.tensor_tensor(
                        ohr_node, iota_nb[:, :].unsqueeze(1).to_broadcast([P, RU, QN]),
                        dst_n[:, bass.ds(col0, RU)].unsqueeze(2).to_broadcast([P, RU, QN]),
                        ALU.is_equal).then_inc(s["dve_deg_rest"], RU)
                    dve.wait_ge(s["dve_deg_rest"], col0 + off + RU)
                    dve.tensor_tensor(ohr_w, ohr_q.unsqueeze(2).to_broadcast([P, RU, PARTS, Q]),
                                      ew_parts[:, bass.ds(col0, RU), :].unsqueeze(3).to_broadcast([P, RU, PARTS, Q]),
                                      ALU.mult).then_inc(s["deg_rest_set"], RU)

            def degrees_read(t):
                dve.wait_ge(s["deg_ps"], t + 1)
                dve.tensor_reduce(deg_q[:, bass.ds(t * Q, Q)],
                                  bank[0][0:QN, 0:PARTS * Q].rearrange("p (a q) -> p q a", a=PARTS), AX.X,
                                  ALU.add).then_inc(s["deg_read"], 1)

            def keys_low(t):
                dve.wait_ge(s["k_ps"], t + 1)
                dve.wait_ge(s["k_exp"], t)
                dve.tensor_scalar(u2[:, :], wide(3), 0.0, None, ALU.min).then_inc(s["k_min"], 1)

            def keys(t):
                dve.wait_ge(s["h_ps"], t + 1)
                dve.scalar_tensor_tensor(out=xh[:, bass.ds(t, 1), :].rearrange("p a b -> p (a b)"), in0=wide(7),
                                         scalar=rstd2_all[:, bass.ds(t, 1)], in1=u8[:, :], op0=ALU.mult,
                                         op1=ALU.add).then_inc(s["h_set"], 1)
                dve.wait_ge(s["k_exp"], t + 1)
                dve.wait_ge(s["kv_acc"], t)
                dve.scalar_tensor_tensor(out=u1[:, :], in0=wide(3), scalar=0.0, in1=u3[:, :], op0=ALU.max,
                                         op1=ALU.add).then_inc(s["k_done"], 1)

            degrees_rest(*degrees(0, 0, first_column(dve, 0))[0])
            degrees_read(0)
            with dve.Fori(0, (W - 1) // 2) as p:
                first = first_column(dve, 2 * p + 1)
                for b in (1, 0):
                    t = 2 * p + (1 - b)
                    following, first = degrees(t + 1, b, first, next_first=b == 1)
                    keys_low(t)
                    degrees_rest(*following)
                    keys(t)
                    degrees_read(t + 1)
            keys_low(W - 1)
            keys(W - 1)
            dve.wait_ge(s["deg_read"], W)
            n = Q * W
            deg, pos, y, t1, t2 = (v[0:QN, 0:n] for v in (u5, u6, u7, t_c[0], t_c[1]))
            ch.link(dve.tensor_scalar(deg, deg_q[:, :], 1.0, None, ALU.add))
            ch.link(dve.tensor_scalar(pos, deg, 0.0, None, ALU.is_gt))
            ch.link(dve.tensor_scalar(deg, deg, float(np.finfo(np.float32).tiny), None, ALU.max))
            inv_sqrt(dve, ch, deg, t1, y, t2)
            dve.memset(dis[:, 0:1], 0.0)
            dve.tensor_tensor(dis_q[:, :, :].rearrange("p q w -> p w q"), y.rearrange("p (w q) -> p w q", q=Q),
                              pos.rearrange("p (w q) -> p w q", q=Q), ALU.mult).then_inc(s["dis_set"], 1)
            dve.wait_ge(s["dis_in"], 16 * Q)
            dve.wait_ge(s["h_set"], W)
            with dve.Fori(0, H_ACT) as t:
                row = xh[:, bass.ds(t, 1), :].rearrange("p a b -> p (a b)")
                dve.tensor_scalar(row, row, dis[:, bass.ds(t + 1, 1)], None, ALU.mult).then_inc(s["h_dve"], 1)
            dve.wait_ge(s["kv_acc"], W)
            for k in range(KB):
                dve.tensor_tensor(kvx[:, k, 0:P].rearrange("p (h d) -> p h d", h=HPB),
                                  bank[5 + k][:, 0:P].rearrange("p (h d) -> p h d", h=HPB),
                                  headmask[:, :].unsqueeze(2).to_broadcast([P, HPB, HD]), ALU.mult)
                last = dve.tensor_scalar(kvx[:, k, P:P + HPB], headmask[:, :], bank[5 + k][:, P:P + 1], None, ALU.mult)
            last.then_inc(s["kvx_set"], 1)
            dve.memset(u3[:, :], 0.0).then_inc(s["z1_done"], 1)

            def scatter_group(v, k, first):
                dve.wait_ge(s["main_used"], v + k * U + U)
                slot = k * U % SLOTS
                dve.tensor_copy(idx_s[:, slot:slot + U], src_row[:, bass.ds(first + k * U, U)]).then_inc(s["idx_set"], U)
                for j in range(U):
                    c = first + (k * U + j)
                    m = dve.tensor_scalar(ss[:, slot + j, :], iw[:, :], dst_f[:, bass.ds(c, 1)],
                                          ew[:, bass.ds(c, 1)], ALU.is_equal, ALU.mult)
                m.then_inc(s["main_set"], U)

            def scatter_rest(lo, end, off):
                with dve.Fori(lo + STATIC, end, RU) as col0:
                    dve.wait_ge(s["rest_used"], col0 + off + RU)
                    dve.tensor_copy(idx_r[:, :], src_row[:, bass.ds(col0, RU)]).then_inc(s["idx_rest_set"], RU)
                    for j in range(RU):
                        m = dve.tensor_scalar(sr[:, j, :], iw[:, :], dst_f[:, bass.ds(col0 + j, 1)],
                                              ew[:, bass.ds(col0 + j, 1)], ALU.is_equal, ALU.mult)
                    m.then_inc(s["rest_set"], RU)

            def begin_window(layer, w, node_w):
                dve.tensor_scalar(iw[:, :], iota_p[:, :], win_first[:, bass.ds(node_w, 1)], None,
                                  ALU.add).then_inc(s["iw_set"], 1)
                dve.wait_ge(s["iw_set"], layer * W + w + 1)
                first = first_column(dve, node_w)
                v = (layer * W + w) * STATIC
                for k in range(AHEAD - 2):
                    scatter_group(v, k, first)
                return v, first

            dve.wait_ge(s["tab_set"], 7)
            v, first = begin_window(0, 0, 0)
            scatter_group(v, AHEAD - 2, first)
            scatter_group(v, AHEAD - 1, first)
            def window1(w, last=False):
                tc = Chain(dve, s["dve_l1"], 3 * LN_LINKS + 6, w)
                lo = first_column(dve, w)
                v = w * STATIC
                for k in range(PIECES):
                    if k == 3:
                        end, off = end_column(dve, 0, w)
                    if k == 5:
                        scatter_rest(lo, end, off)
                    if k == 1:
                        dve.wait_ge(s["q_ps"], w + 1)
                        dve.tensor_scalar(t_a[0][:, :], wide(2), 0.0, None, ALU.min).then_inc(s["q_min"], 1)
                        dve.wait_ge(s["q_exp"], w + 1)
                        dve.wait_ge(s["nd_ps"], w)
                        dve.scalar_tensor_tensor(out=t_b[0][:, :], in0=wide(2), scalar=0.0, in1=t_a[1][:, :],
                                                 op0=ALU.max, op1=ALU.add).then_inc(s["q_done"], 1)
                    if k == 2:
                        dve.wait_ge(s["nd_ps"], w + 1)
                        nd = half(3, P + HPB)
                        tc.link(dve.tensor_scalar(zden[:, :, :], nd[:, :, P:P + HPB], ATT_EPS, None, ALU.add))
                        tc.link(dve.reciprocal(zrec[:, :, :], zden[:, :, :]))
                        dve.wait_ge(s["msg_tp"], w)
                        for kb in range(KB):
                            m = dve.tensor_tensor(
                                u8[:, kb * P:(kb + 1) * P].rearrange("p (h d) -> p h d", h=HPB),
                                nd[:, kb, 0:P].rearrange("p (h d) -> p h d", h=HPB),
                                zrec[:, kb, :].unsqueeze(2).to_broadcast([P, HPB, HD]), ALU.mult)
                        m.then_inc(s["msg_done"], 1)
                    if k == 4:
                        dve.wait_ge(s["m_ps"], w + 1)
                        layer_norm(dve, tc, wide(4), u7[:, :], st, mv, rstd).then_inc(s["mn_done"], 1)
                    if k == 6:
                        dve.wait_ge(s["x_again"], 16 * (w + 1))
                        dve.wait_ge(s["xn_kept"], w + 1)
                        tc.link(dve.tensor_tensor(t_c[0][:, :], xn_keep[:, :], u2[:, :], ALU.add))
                        tc.link(dve.tensor_tensor(t_c[0][:, :], t_c[0][:, :], vec[:, 5, :], ALU.add))
                    if k + AHEAD < PIECES:
                        scatter_group(v, k + AHEAD, lo)
                dve.wait_ge(s["rest_set"], end + off)
                v_next, first = begin_window(0, w + 1, w + 1)
                dve.wait_ge(s["rest_used"], end + off + RU)
                dve.scalar_tensor_tensor(out=t_b[1][:, :], in0=acc, scalar=dis[:, bass.ds(w + 1, 1)], in1=vec[:, 0, :],
                                         op0=ALU.mult, op1=ALU.add).then_inc(s["acc_read"], 1)
                scatter_group(v_next, AHEAD - 2, first)
                dve.wait_ge(s["acc_read"], w + 1)
                dve.wait_ge(s["x1_out"], 16 * w)
                dve.scalar_tensor_tensor(out=u5[:, :], in0=t_b[1][:, :], scalar=0.0, in1=xn_keep[:, :], op0=ALU.max,
                                         op1=ALU.add).then_inc(s["x1_done"], 1)
                dve.wait_ge(s["x1_done"], w + 1)
                dve.wait_ge(s["z1_tp"], w + 1)
                layer_norm(dve, tc, u5[:, :], u3[:, :], st2, mv2, rstd2).then_inc(s["z1_done"], 1)
                if not last:
                    scatter_group(v_next, AHEAD - 1, first)
                dve.wait_ge(s["y1_ps"], w + 1)
                tc.link(layer_norm(dve, tc, wide(4), t_c[1][:, :], st, mv, rstd))
                tc.link(dve.tensor_tensor(t_c[1][:, :], t_c[1][:, :], vec[:, 3, :], ALU.mult))
                dve.wait_ge(s["r_out"], 16 * w)
                dve.tensor_tensor(u6[:, :], t_c[1][:, :], t_c[0][:, :], ALU.add).then_inc(s["r_done"], 1)
                assert tc.n == tc.per, tc.n

            with dve.Fori(0, W - 1) as w:
                window1(w)
            window1(W - 1, last=True)

            dve.wait_ge(s["x1_out"], 16 * W)
            dve.wait_ge(s["r_out"], 16 * W)
            dve.wait_ge(s["h2_out"], 16 * (W + 1))
            dve.wait_ge(s["z1_tp"], W + 1)
            dve.wait_ge(s["h7_ps"], W + 1)
            dve.memset(u3[:, :], 0.0).then_inc(s["x2_done"], 1)
            dve.memset(u6[:, :], 0.0).then_inc(s["blank_set"], 1)
            dve.memset(mask_n[:, :], 0.0).then_inc(s["blank_set"], 1)
            dve.memset(zT[:, :, :], 0.0).then_inc(s["zn_blank"], 1)
            dve.wait_ge(s["blank_set"], 2)

            def add_expert(w, e):
                dve.wait_ge(s["y_ps"], NE * w + e + 1 + 2)
                dve.wait_ge(s["facc"], (NE + 1) * w + 1 + e)
                dve.scalar_tensor_tensor(out=u8[:, :], in0=wide((7, 5)[e % 2]), scalar=mask_c[:, e:e + 1], in1=u8[:, :],
                                         op0=ALU.mult, op1=ALU.add).then_inc(s["facc"], 1)

            def window2(w, msgs=True, epilogue=True):
                if msgs:
                    lo = first_column(dve, w)
                    v = (W + w) * STATIC
                    scatter_group(v, AHEAD - 1, lo)
                dve.wait_ge(s["out_stored"], 16 * w)
                dve.wait_ge(s["x3b_done"], w)
                dve.tensor_copy(mask_c[:, :], mask_n[:, :]).then_inc(s["mask_set"], 1)
                dve.tensor_copy(u8[:, :], u6[:, :]).then_inc(s["facc"], 1)
                dve.wait_ge(s["mask_set"], w + 1)
                tc = Chain(dve, s["dve_l2"], LN_LINKS + 5, w)
                for k in range(PIECES):
                    if msgs and k == 7:
                        dve.wait_ge(s["rest_set"], end + off)
                        v_next, first = begin_window(1, w + 1, w + 1)
                    if msgs and k == 3:
                        end, off = end_column(dve, 1, w)
                    if msgs and k == 6:
                        scatter_rest(lo, end, off)
                    if epilogue and k == 1:
                        dve.wait_ge(s["p_ps"], w + 1)
                        dve.wait_ge(s["r_in"], 16 * (w + 1))
                        dve.tensor_tensor(u4[:, :], wide(4), u2[:, :], ALU.add).then_inc(s["x3_done"], 1)
                        dve.wait_ge(s["x3_done"], w + 1)
                        dve.wait_ge(s["z3_tp"], w)
                        layer_norm(dve, tc, u4[:, :], u5[:, :], st2, mv2, rstd2).then_inc(s["z3_done"], 1)
                    if epilogue and k == 4:
                        dve.wait_ge(s["g_ps"], w + 1)
                        tc.link(dve.tensor_tensor(lg[:, :], bank[3][:, 0:NE], bgr[:, :], ALU.add))
                        mine = lg[:, :].unsqueeze(2).to_broadcast([P, NE, NE])
                        other = lg[:, :].unsqueeze(1).to_broadcast([P, NE, NE])
                        dve.tensor_tensor(cmp1[:, :, :], other, mine, ALU.is_gt)
                        tc.link(dve.tensor_tensor(cmp2[:, :, :], other, mine, ALU.is_equal))
                        tc.link(dve.tensor_tensor(cmp2[:, :, :], cmp2[:, :, :], lowtri[:, :, :], ALU.mult))
                        tc.link(dve.tensor_tensor(cmp1[:, :, :], cmp1[:, :, :], cmp2[:, :, :], ALU.add))
                        tc.link(dve.tensor_reduce(rank[:, :], cmp1[:, :, :], AX.X, ALU.add))
                        dve.tensor_scalar(mask_n[:, :], rank[:, :], 2.0, None, ALU.is_lt).then_inc(s["mask_done"], 1)
                    if epilogue and k == 6:
                        dve.wait_ge(s["b2_ps"], w + 1)
                        dve.wait_ge(s["facc"], (NE + 1) * w + 1)
                        dve.tensor_tensor(u6[:, :], wide(4), u4[:, :], ALU.add).then_inc(s["x3b_done"], 1)
                    if k:
                        add_expert(w, k - 1)
                    if msgs and k + AHEAD < PIECES:
                        scatter_group(v, k + AHEAD, lo)
                if epilogue:
                    assert tc.n == tc.per, tc.n
                if msgs:
                    dve.wait_ge(s["rest_used"], end + off + RU)
                    dve.scalar_tensor_tensor(out=u7[:, :], in0=acc, scalar=dis[:, bass.ds(w + 1, 1)], in1=vec[:, 1, :],
                                             op0=ALU.mult, op1=ALU.add).then_inc(s["acc2_read"], 1)
                    scatter_group(v_next, AHEAD - 2, first)
                    dve.wait_ge(s["acc2_read"], w + 1)
                    dve.wait_ge(s["x1_in"], 16 * (w + 1))
                    dve.wait_ge(s["x2_tp"], w + 1)
                    dve.scalar_tensor_tensor(out=u3[:, :], in0=u7[:, :], scalar=0.0, in1=u1[:, :], op0=ALU.max,
                                             op1=ALU.add).then_inc(s["x2_done"], 1)
                add_expert(w, NE - 1)

            with dve.Fori(0, W) as w:
                window2(w)
            window2(W, msgs=False)
            window2(W + 1, msgs=False, epilogue=False)

        @block.tensor
        def _(pe):
            pe.sem_inc(s["main_used"], SLOTS)
            pe.sem_inc(s["rest_used"], REST_FROM + RU)
            pe.sem_inc(s["rest_set"], REST_FROM)
            pe.sem_inc(s["deg_rest_used"], REST_FROM + RU)
            pe.sem_inc(s["dve_deg_rest"], REST_FROM)
            pe.wait_ge(s["consts"], N_CONSTS)
            pe.wait_ge(s["weights_in"], 16 * WEIGHT_LOADS)

            def mm(out_ap, lhsT, rhs, first, last, **kw):
                return pe.matmul(out_ap, lhsT, rhs, start=first, stop=last, **kw)

            for i, wt in enumerate((w6, w7)):
                for k in range(KB):
                    m = mm(bank[1 + i][0:1, 0:D], lncol[:, 2 * i + 1, k:k + 1], wt[:, k, :], k == 0, k == KB - 1)
                m.then_inc(s["shift_ps"], 1)
            for j in range(HBLK):
                for k in range(KB):
                    m = mm(bank[3][:, j:j + 1], w1[:, KB + k, j * P:(j + 1) * P], mixcol[:, 1, k:k + 1], k == 0,
                           k == KB - 1)
            m.then_inc(s["shift_ps"], 1)

            for k in range(KB):
                mm(bank[5 + k][:, 0:P + 1], zero_tile[:, 0:P], zero_tile[:, 0:P + 1], True, True)
            pe.wait_ge(s["weights_set"], 1)
            mm(wide(2), ones_row[:, :], hb[:, 0, :], True, True).then_inc(s["hb_ps"], 1)

            def flip(b, src, done):
                for k in range(KB):
                    m = pe.transpose(half(b)[:, k, :], src[:, k * P:(k + 1) * P], ident[:, :])
                m.then_inc(done, 1)

            def by_rows(b, xt, wt, done, bias=None):
                if bias is not None:
                    mm(wide(b), ones_row[:, :], bias, True, False)
                for k in range(KB):
                    m = mm(wide(b), xt[:, k, :], wt[:, k, :], bias is None and k == 0, k == KB - 1)
                m.then_inc(done, 1)

            def turn(t, b):
                pe.wait_ge(s["xn_done"], t + 1)
                pe.wait_ge(s["xT_set"], t)
                flip(1, t_b[b], s["xn_tp"])

            def degrees(t, b):
                pe.wait_ge(s["deg_set"], t + 1)
                pe.wait_ge(s["deg_read"], t)
                for c in range(STATIC):
                    mm(bank[0][0:QN, 0:PARTS * Q], oh_node[b][:, c, :], oh_w[b][:, c, :, :].rearrange("p a q -> p (a q)"),
                       c == 0, True, skip_group_check=True)

            def degrees_rest(n, base):
                with pe.Fori(0, n, RU) as i:
                    pe.wait_ge(s["deg_rest_set"], base + i + RU)
                    for c in range(RU):
                        m = mm(bank[0][0:QN, 0:PARTS * Q], ohr_node[:, c, :],
                               ohr_w[:, c, :, :].rearrange("p a q -> p (a q)"), False, True, skip_group_check=True)
                    m.then_inc(s["deg_rest_used"], RU)
                mm(bank[2][0:1, 0:1], zero_tile[:, 0:1], zero_tile[:, 0:1], True, True).then_inc(s["deg_ps"], 1)

            def tile(t, following=True):
                pe.wait_ge(s["xT_set"], t + 1)
                pe.wait_ge(s["k_done"], t)
                by_rows(3, xT, wk, s["k_ps"])
                pe.wait_ge(s["v_set"], t)
                by_rows(4, xT, wv, s["v_ps"])
                ranges = rest_table(pe, 0, t + 1) if following else None
                pe.wait_ge(s["h_set"], t)
                by_rows(7, xT, w6, s["h_ps"])
                return ranges

            def kv(t):
                pe.wait_ge(s["k_done"], t + 1)
                pe.wait_ge(s["v_set"], t + 1)
                for k in range(KB):
                    m = mm(bank[5 + k][:, 0:P + 1], u1[:, k * P:(k + 1) * P], vx[:, k, :], False, True,
                           skip_group_check=True)
                m.then_inc(s["kv_acc"], 1)

            pe.wait_ge(s["tab_set"], 7)
            turn(0, 0)
            degrees(0, 0)
            degrees_rest(*rest_table(pe, 0, 0))
            with pe.Fori(0, (W - 1) // 2) as p:
                for b in (1, 0):
                    t = 2 * p + (1 - b)
                    ranges = tile(t)
                    turn(t + 1, b)
                    degrees(t + 1, b)
                    degrees_rest(*ranges)
                    kv(t)
            tile(W - 1, following=False)
            kv(W - 1)

            def messages(turn, v, k):
                pe.wait_ge(s["main_set"], v + k * U + U)
                for n in range(k * U, k * U + U):
                    pe.wait_ge(s[f"main_in{n % SLOTS}"], 16 * (turn * (STATIC // SLOTS) + n // SLOTS + 1))
                    mm(acc, ss[:, n % SLOTS, :], gs[:, n % SLOTS, :], False, True,
                       skip_group_check=True).then_inc(s["main_used"], 1)

            def rest_messages(n, base):
                with pe.Fori(0, n, RU) as i:
                    pe.wait_ge(s["rest_set"], base + i + (REST_FROM + RU))
                    for j in range(RU):
                        pe.wait_ge(s[f"rest_in{j}"], (base + i) * (16 // RU) + 16)
                        mm(acc, sr[:, j, :], gr[:, j, :], False, True, skip_group_check=True).then_inc(s["rest_used"], 1)

            pe.wait_ge(s["kvx_set"], 1)
            pe.wait_ge(s["tab_set"], 7)

            def next_h_turn(w):
                pe.wait_ge(s["z1_done"], w + 1)
                pe.wait_ge(s["z1T_set"], w)
                flip(1, u3, s["z1_tp"])

            def next_h(w):
                pe.wait_ge(s["z1T_set"], w + 1)
                pe.wait_ge(s["h2_done"], w)
                by_rows(7, zT, w7, s["h7_ps"], bias=hb[:, 1, :])

            with pe.Fori(0, W) as w:
                v = w * STATIC
                pe.wait_ge(s["acc_read"], w)
                pe.wait_ge(s["self_in"], 16 * (w + 1))
                mm(acc, ident[:, :], hself[:, :], True, True).then_inc(s["self_used"], 1)
                for k in range(PIECES):
                    messages(w, v, k)
                    if k == 0:
                        pe.wait_ge(s["xn_in"], 16 * (w + 1))
                        pe.wait_ge(s["mnT_set"], w)
                        flip(5, u1, s["xn1_tp"])
                    if k == 1:
                        pe.wait_ge(s["xn1T_set"], w + 1)
                        pe.wait_ge(s["q_done"], w)
                        for j in range(KB):
                            for i in range(KB):
                                m = mm(half(2)[:, j, :], wq[:, i, j * P:(j + 1) * P], xT[:, i, :], i == 0, i == KB - 1)
                        m.then_inc(s["q_ps"], 1)
                    if k == 2:
                        pe.wait_ge(s["q_done"], w + 1)
                        pe.wait_ge(s["msg_done"], w)
                        for j in range(KB):
                            m = mm(half(3, P + HPB)[:, j, :], t_b[0][:, j * P:(j + 1) * P], kvx[:, j, :], True, True)
                        m.then_inc(s["nd_ps"], 1)
                        next_h_turn(w)
                    if k == 3:
                        pe.wait_ge(s["msg_done"], w + 1)
                        flip(5, u8, s["msg_tp"])
                        next_h(w)
                    if k == 4:
                        pe.wait_ge(s["msgT_set"], w + 1)
                        pe.wait_ge(s["r_done"], w)
                        by_rows(4, mT, wm, s["m_ps"])
                    if k == 5:
                        pe.wait_ge(s["mn_done"], w + 1)
                        flip(5, u7, s["mn_tp"])
                    if k == 6:
                        pe.wait_ge(s["mnT_set"], w + 1)
                        pe.wait_ge(s["hr_done"], HBLK * w)
                        for j in range(HBLK):
                            for i in range(2 * KB):
                                m = mm(bank[6][:, j * P:(j + 1) * P], w1[:, i, j * P:(j + 1) * P],
                                       (xT if i < KB else nT)[:, i % KB, :], i == 0, i == 2 * KB - 1)
                        m.then_inc(s["hh_ps"], 1)
                        n_rest, base = rest_table(pe, 0, w)
                    if k == 7:
                        pe.wait_ge(s["hr_done"], HBLK * (w + 1))
                        for i in range(HBLK):
                            m = mm(wide(4), hT[0][:, i, :], w2[:, i, :], i == 0, i == HBLK - 1)
                        m.then_inc(s["y1_ps"], 1)
                rest_messages(n_rest, base)
            next_h_turn(W)
            next_h(W)

            pe.sem_inc(s["y_ps"], 2)
            pe.wait_ge(s["experts_in"], 16 * 2 * NE)
            pe.wait_ge(s["h2_done"], W + 1)

            def hidden(w, e):
                pe.wait_ge(s["zc_set"], w + 1)
                pe.wait_ge(s["gelu_done"], HBLK * (NE * w + max(e - 1, 0)))
                for j in range(HBLK):
                    for i in range(KB):
                        m = mm(bank[(6, 2)[e % 2]][:, j * P:(j + 1) * P], ew1[:, e, i, j * P:(j + 1) * P], nT[:, i, :],
                               i == 0, i == KB - 1)
                m.then_inc(s["hid_ps"], 1)

            def expert_out(w, e):
                pe.wait_ge(s["gelu_done"], HBLK * (NE * w + e + 1))
                pe.wait_ge(s["facc"], (NE + 1) * w + (e if e >= 2 else 0))
                for i in range(HBLK):
                    m = mm(wide((7, 5)[e % 2]), hT[e % 2][:, i, :], ew2[:, e, i, :], i == 0, i == HBLK - 1)
                m.then_inc(s["y_ps"], 1)

            def window2(w, msgs=True, epilogue=True):
                if msgs:
                    v = (W + w) * STATIC
                    pe.wait_ge(s["acc2_read"], w)
                    pe.wait_ge(s["self2_in"], 16 * (w + 1))
                    mm(acc, ident[:, :], hself[:, :], True, True).then_inc(s["self2_used"], 1)
                for k in range(PIECES):
                    if msgs:
                        messages(W + w, v, k)
                    if epilogue and k == 0:
                        pe.wait_ge(s["x2_done"], w + 1)
                        pe.wait_ge(s["zn_set"], w)
                        flip(1, u3, s["x2_tp"])
                    if epilogue and k == 1:
                        pe.wait_ge(s["x2T_set"], w + 1)
                        pe.wait_ge(s["x3b_done"], w)
                        by_rows(4, xT, wp, s["p_ps"])
                    if epilogue and k == 3:
                        pe.wait_ge(s["z3_done"], w + 1)
                        flip(1, u5, s["z3_tp"])
                    if epilogue and k == 4:
                        pe.wait_ge(s["zn_set"], w + 1)
                        pe.wait_ge(s["maskT_set"], w)
                        for i in range(KB):
                            m = mm(bank[3][:, 0:NE], zT[:, i, :], wg[:, i, :], i == 0, i == KB - 1)
                        m.then_inc(s["g_ps"], 1)
                    if epilogue and k == 5:
                        pe.wait_ge(s["mask_done"], w + 1)
                        pe.transpose(bank[3][0:NE, P // 2:P // 2 + P], mask_n[:, :], ident[:, :]).then_inc(s["mt_ps"], 1)
                    if epilogue and k == 6:
                        pe.wait_ge(s["maskT_set"], w + 1)
                        pe.wait_ge(s["x3_done"], w + 1)
                        mm(wide(4), maskT[:, :], eb2r[:, :], True, True).then_inc(s["b2_ps"], 1)
                    hidden(w, k)
                    if k:
                        expert_out(w, k - 1)
                    if msgs and k == 6:
                        n_rest, base = rest_table(pe, 1, w)
                if msgs:
                    rest_messages(n_rest, base)
                expert_out(w, NE - 1)

            with pe.Fori(0, W) as w:
                window2(w)
            window2(W, msgs=False)
            window2(W + 1, msgs=False, epilogue=False)


def kernel(**inputs):
    import concourse.bacc as bacc
    from concourse.bass_utils import run_bass_kernel_spmd

    a = {k: np.ascontiguousarray(v) for k, v in inputs.items()}
    src, dst, ew = a["src"].astype(np.int32), a["dst"].astype(np.int32), a["edge_weight"]

    def columns(e, **kw):
        return np.ascontiguousarray(np.pad(e, (0, NCOL * P - N_EDGES), **kw).reshape(NCOL, P).T)

    whole = np.pad(dst, (0, NCH * P - N_EDGES), mode="edge")
    dst_rows = np.pad(whole, (0, (RB - NCH // P) * P * P - NCH % P * P), constant_values=-1)
    dst_rows = np.ascontiguousarray(dst_rows.reshape(RB, P, P).transpose(1, 0, 2))

    def col(v):
        return np.ascontiguousarray(v.reshape(-1, P).T)

    g, m, f = "L0_gnn_", "L0_mix_", "L0_ffn_"
    arrays = {
        "x": np.pad(a["x"], ((0, (W + 2) * P - N_NODES), (0, 0))),
        "src_cols": columns(src), "dst_cols": columns(dst, mode="edge"), "ew_cols": columns(ew), "dst_rows": dst_rows,
        "vecs": np.stack([a[g + "b6"], a[g + "b7"], a[g + "bp"], a[m + "g2"], a[m + "b2"]]),
        "W6T": np.ascontiguousarray(a[g + "W6"].T), "W7T": np.ascontiguousarray(a[g + "W7"].T),
        "WpT": np.ascontiguousarray(a[g + "Wp"].T),
        "Wq": a[m + "Wq"], "Wk": a[m + "Wk"], "Wv": a[m + "Wv"], "Wm": a[m + "Wm"], "W1": a[m + "W1"], "W2": a[m + "W2"],
        "ln_cols": np.ascontiguousarray(np.stack([col(a[g + n]) for n in ("ln6_g", "ln6_b", "ln7_g", "ln7_b")], 1)),
        "mix_cols": np.ascontiguousarray(np.stack([col(a[m + n]) for n in ("g1", "b1")], 1)),
        "Wg": a[f + "Wg"], "bg": a[f + "bg"].reshape(1, NE), "eW1": a[f + "W1"],
        "eb1": np.ascontiguousarray(a[f + "b1"].reshape(NE, HBLK, P).transpose(2, 0, 1)),
        "eW2": a[f + "W2"], "eb2": a[f + "b2"],
    }
    nc = bacc.Bacc("TRN2", target_bir_lowering=False, num_devices=1)
    args = [nc.dram_tensor(f"in_{n}", v.shape, mybir.dt.from_np(v.dtype), kind="ExternalInput").ap()
            for n, v in arrays.items()]
    out = nc.dram_tensor("out", ((W + 2) * P, D), F32, kind="ExternalOutput").ap()
    gps_kernel(nc, *args, out)
    r = run_bass_kernel_spmd(nc, [{f"in_{n}": v for n, v in arrays.items()}], core_ids=[0])
    return r.results[0]["out"][2 * P:2 * P + N_NODES]
```

```python
from contextlib import ExitStack

import numpy as np

import concourse.bass as bass
from concourse import mybir

ALU = mybir.AluOpType
ACT = mybir.ActivationFunctionType
AX = mybir.AxisListType
F32 = mybir.dt.float32
I32 = mybir.dt.int32
BF16 = mybir.dt.bfloat16
F16 = mybir.dt.float16

P = 128
N_NODES, N_EDGES, D = 6250, 200000, 256
KB = D // P
W = -(-N_NODES // P)
NCH = -(-N_EDGES // P)
U = 4
PIECES = 8
STATIC = U * PIECES
SLOTS = 16
EARLY = 1
RU = 2
NCOL = -(-(NCH + STATIC + 2 * U) // 8) * 8
RB = -(-NCH // P)
REST_FROM = NCOL
HEADS, HD = 8, 32
HPB = P // HD
NE, HID = 8, 512
HBLK = HID // P
EW_COLS = NE * (KB * HID + HBLK * D)
EW_STEP = -(-EW_COLS // W // 8) * 8
Z_UP, W_UP, H_UP = 1024.0, 1024.0, 256.0
HALVES = ((0, 0), (0, 1), (1, 0))
EPS = 1e-5
ATT_EPS = 1e-6
Q, QN = 4, P // 4
PARTS = 3
XG = 7
H_ACT = 4 * XG
RSQRT_BITS = 0x5F3759DF
NEWTON = 3
LN_LINKS = 5 + 3 * NEWTON
WEIGHT_LOADS = 20
N_CONSTS = 16
assert W % 2 == 1 and W % XG == 0 and Q * W <= 256


class Chain:

    def __init__(self, eng, sem, per, turn):
        self.eng, self.sem, self.per, self.turn, self.n = eng, sem, per, turn, 0

    def link(self, ins):
        self.n += 1
        ins.then_inc(self.sem, 1)
        self.eng.wait_ge(self.sem, self.turn * self.per + self.n)


def gps_kernel(nc, x, src_cols, dst_cols, ew_cols, dst_rows, vecs, W6T, W7T, WpT, Wq, Wk, Wv, Wm, W1, W2,
               ln_cols, mix_cols, Wg, bg, eW, eb1, eb2, out):
    with ExitStack() as ctx:
        def sb(name, shape, dt=F32):
            return ctx.enter_context(nc.sbuf_tensor(name, shape, dt))

        sems = {}

        class Sems:
            def __getitem__(self, name):
                if name not in sems:
                    sems[name] = ctx.enter_context(nc.semaphore(name))
                return sems[name]

        s = Sems()
        dve_, act_, pe_, pool_, sp_ = nc.vector, nc.scalar, nc.tensor, nc.gpsimd, nc.sync

        xn_d = nc.dram_tensor("xn_d", [(W + 1) * P, D], F32).ap()
        h1_d = nc.dram_tensor("h1_d", [(W + 2) * P, D], F32).ap()
        h2_d = nc.dram_tensor("h2_d", [(W + 2) * P, D], F32).ap()
        x1_d = nc.dram_tensor("x1_d", [(W + 1) * P, D], F32).ap()
        r_d = nc.dram_tensor("r_d", [(W + 1) * P, D], F32).ap()

        def rows(table, block):
            return table[bass.ds(block * P, P), :]

        ident = sb("ident", [P, P])
        ones_row = sb("ones_row", [1, P])
        zero_tile = sb("zero_tile", [P, D])
        iota_p = sb("iota_p", [P, P])
        iota_q = sb("iota_q", [P, Q * W])
        iota_qb = sb("iota_qb", [P, Q * W], BF16); iota_nb = sb("iota_nb", [P, QN], BF16)
        win_first = sb("win_first", [P, W + 1])
        chunk_id = sb("chunk_id", [P, RB])
        headmask = sb("headmask", [P, HPB])
        lowtri = sb("lowtri", [P, NE, NE])
        valid = sb("valid", [P, W])
        src_row = sb("src_row", [P, NCOL], I32)
        dst_f = sb("dst_f", [P, NCOL])
        ew = sb("ew", [P, NCOL])
        w6 = sb("w6", [P, KB, D]); w7 = sb("w7", [P, KB, D]); wp = sb("wp", [P, KB, D])
        wq = sb("wq", [P, KB, D]); wk = sb("wk", [P, KB, D]); wv = sb("wv", [P, KB, D]); wm = sb("wm", [P, KB, D])
        w1 = sb("w1", [P, 2 * KB, HID]); w2 = sb("w2", [P, HBLK, D])
        lncol = sb("lncol", [P, 4, KB])
        mixcol = sb("mixcol", [P, 2, KB])
        vec = sb("vec", [P, 6, D])
        hb = sb("hb", [1, 2, D])
        w1bias = sb("w1bias", [P, HBLK])
        wg = sb("wg", [P, KB, NE]); bgr = sb("bgr", [P, NE])
        experts = sb("experts", [P, W * EW_STEP])
        ew_halves = experts[:, :].bitcast(F16)
        ew_part = [ew_halves[:, i * W * EW_STEP:(i + 1) * W * EW_STEP] for i in range(2)]
        ew1 = [a[:, 0:NE * KB * HID].rearrange("p (e k n) -> p e k n", e=NE, k=KB) for a in ew_part]
        ew2 = [a[:, NE * KB * HID:EW_COLS].rearrange("p (e k n) -> p e k n", e=NE, k=HBLK) for a in ew_part]
        ew_in = sb("ew_in", [P, EW_STEP])
        eb1c = sb("eb1c", [P, NE, HBLK]); eb2r = sb("eb2r", [NE, D])
        tab = sb("tab", [1, 7, W + 1], I32)
        st_all = sb("st_all", [P, W, 6]); mean_all = sb("mean_all", [P, W]); var_all = sb("var_all", [P, W])
        rstd_all = sb("rstd_all", [P, W]); shift_all = sb("shift_all", [P, W]); rstd2_all = sb("rstd2_all", [P, W])
        w_s1 = sb("w_s1", [P, W]); w_s2 = sb("w_s2", [P, W]); w_s3 = sb("w_s3", [P, W])
        deg_q = sb("deg_q", [QN, Q * W]); dis_q = sb("dis_q", [QN, Q, W])
        dis = sb("dis", [P, W + 1])
        idx_s = sb("idx_s", [P, SLOTS], I32); idx_r = sb("idx_r", [P, RU], I32)
        gs = sb("gs", [P, SLOTS, D]); gr = sb("gr", [P, RU, D])
        ss = sb("ss", [P, SLOTS, P]); sr = sb("sr", [P, RU, P])
        iw = sb("iw", [P, P]); iw_rest = sb("iw_rest", [P, P])
        hself = sb("hself", [P, D])
        kvx = sb("kvx", [P, KB, P + HPB])
        t_a = [sb(f"t_a{i}", [P, D]) for i in range(2)]
        t_b = [sb(f"t_b{i}", [P, D]) for i in range(2)]
        t_c = [sb(f"t_c{i}", [P, D]) for i in range(2)]
        xT = sb("xT", [P, KB, P]); zT = sb("zT", [P, KB, P]); mT = sb("mT", [P, KB, P]); nT = sb("nT", [P, KB, P])
        xn_keep = sb("xn_keep", [P, D])
        u1 = sb("u1", [P, D]); u2 = sb("u2", [P, D]); u3 = sb("u3", [P, D]); u4 = sb("u4", [P, D]); u5 = sb("u5", [P, D])
        u6 = sb("u6", [P, D]); u7 = sb("u7", [P, D]); u8 = sb("u8", [P, D])
        vx = sb("vx", [P, KB, P + 1])
        hT = [sb(f"hT{i}", [P, HBLK, P]) for i in range(2)]
        hT_part = [[sb(f"hT_{n}{i}", [P, HBLK, P], F16) for n in ("high", "low")] for i in range(2)]
        nT_part = [sb(f"nT_{n}", [P, KB, P], F16) for n in ("high", "low")]
        st = sb("st", [P, 12]); mv = sb("mv", [P, 4]); rstd = sb("rstd", [P, 8])
        zden = sb("zden", [P, KB, HPB]); zrec = sb("zrec", [P, KB, HPB])
        lg = sb("lg", [P, NE]); cmp1 = sb("cmp1", [P, NE, NE]); cmp2 = sb("cmp2", [P, NE, NE]); rank = sb("rank", [P, NE])
        mask_n = sb("mask_n", [P, NE]); mask_c = sb("mask_c", [P, NE]); maskT = sb("maskT", [NE, P])

        bank = [ctx.enter_context(nc.psum_tensor(f"bank{i}", [P, 512], F32)) for i in range(8)]

        def half(b, n=P):
            return bank[b][:, 0:KB * n].rearrange("p (k n) -> p k n", k=KB)

        acc = bank[0][:, 0:D]

        def wide(b):
            return bank[b][:, 0:D]

        def col(ap, shape):
            return ap.to_broadcast(shape)

        flat_gs = gs[:, :, :].rearrange("p a b -> p (a b)")
        drow_i = flat_gs[:, 0:RB * P].bitcast(I32).rearrange("p (b e) -> p b e", b=RB)
        drow_f = flat_gs[:, RB * P:2 * RB * P].rearrange("p (b e) -> p b e", b=RB)
        assert 2 * RB * P <= SLOTS * D
        flat_ss = ss[:, :, :].rearrange("p a b -> p (a b)")
        touch = [flat_ss[:, i * W * RB:(i + 1) * W * RB].rearrange("p (w b) -> p w b", w=W) for i in range(3)]
        assert 3 * W * RB <= SLOTS * P
        dst_i = dst_f[:, :].bitcast(I32)
        xh = experts[:, 0:W * D].rearrange("p (t d) -> p t d", t=W)

        class Carve:

            def __init__(self, flat, at, end):
                self.flat, self.at, self.end = flat, at, end

            def take(self, n, dt=F32):
                words = n if dt == F32 else -(-n // 2)
                piece = self.flat[:, self.at:self.at + words]
                self.at += words
                assert self.at <= self.end
                return piece if dt == F32 else piece.bitcast(dt)

        tail = Carve(experts, W * D, W * EW_STEP)
        ew_parts = tail.take(NCOL * PARTS, BF16).rearrange("p (c a) -> p c a", a=PARTS)
        dst_n = tail.take(NCOL, BF16)
        range_part, range_all = tail.take(2 * W), tail.take(2 * W)
        rg = tail.take(6 * W)[0:1, :].rearrange("p (a w) -> p a w", w=W)
        rg_i = tail.take(2 * W)[0:1, :].bitcast(I32).rearrange("p (a w) -> p a w", w=W)
        cmin, cmax = tail.take(RB), tail.take(RB)
        room = Carve(flat_gs, 0, SLOTS * D)
        wide_s = room.take(NCOL)
        dst_q = room.take(NCOL, BF16)
        oh_node = [room.take(STATIC * QN, BF16).rearrange("p (c n) -> p c n", n=QN) for _ in range(2)]
        oh_q = room.take(STATIC * Q, BF16).rearrange("p (c q) -> p c q", q=Q)
        oh_w = [room.take(STATIC * PARTS * Q, BF16).rearrange("p (c a q) -> p c a q", a=PARTS, q=Q) for _ in range(2)]
        ohr_node = room.take(RU * QN, BF16).rearrange("p (c n) -> p c n", n=QN)
        ohr_q = room.take(RU * Q, BF16).rearrange("p (c q) -> p c q", q=Q)
        ohr_w = room.take(RU * PARTS * Q, BF16).rearrange("p (c a q) -> p c a q", a=PARTS, q=Q)

        block = ctx.enter_context(nc.Block())

        def first_column(eng, w):
            return eng.value_load(tab[0:1, 0, bass.ds(w, 1)], min_val=0, max_val=NCH)

        def end_column(eng, layer, w):
            end = eng.value_load(tab[0:1, 1, bass.ds(w, 1)], min_val=STATIC + 1, max_val=NCOL - RU + 1)
            off = eng.value_load(tab[0:1, 2 + layer, bass.ds(w, 1)], min_val=0, max_val=(2 * W + 1) * NCOL)
            return end, off

        def rest_table(eng, layer, w):
            n = eng.value_load(tab[0:1, 4, bass.ds(w, 1)], min_val=RU, max_val=NCOL)
            base = eng.value_load(tab[0:1, 5 + layer, bass.ds(w, 1)], min_val=0, max_val=2 * W * NCOL)
            return n, base

        @block.sync
        def _(sp):
            for dst_t, src_t in ((dst_i, dst_cols), (ew[:, :], ew_cols), (src_row[:, :], src_cols)):
                sp.dma_start(dst_t, src_t).then_inc(s["edges_in"], 16)
            sp.dma_start(drow_i, dst_rows).then_inc(s["rows_in"], 16)
            for i in range(0, W, XG):
                sp.dma_start(xh[:, i:i + XG, :],
                             x[i * P:(i + XG) * P, :].rearrange("(t p) d -> p t d", p=P)).then_inc(s["x_in"], 16)
            n = 0
            for t, a in ((w6, W6T), (w7, W7T), (wp, WpT), (wq, Wq), (wk, Wk), (wv, Wv), (wm, Wm), (w1, W1), (w2, W2)):
                sp.dma_start(t[:, :, :], a.rearrange("(k p) n -> p k n", p=P)).then_inc(s["weights_in"], 16)
                n += 1
            for i in range(5):
                sp.dma_start(vec[:, i, :], vecs[i:i + 1, :].to_broadcast([P, D])).then_inc(s["weights_in"], 16)
                n += 1
            with nc.allow_non_contiguous_dma(reason="a few columns"):
                sp.dma_start(lncol[:, :, :], ln_cols).then_inc(s["weights_in"], 16)
                sp.dma_start(mixcol[:, :, :], mix_cols).then_inc(s["weights_in"], 16)
                sp.dma_start(wg[:, :, :], Wg.rearrange("(k p) n -> p k n", p=P)).then_inc(s["weights_in"], 16)
                sp.dma_start(bgr[:, :], bg.to_broadcast([P, NE])).then_inc(s["weights_in"], 16)
                sp.dma_start(eb1c[:, :, :], eb1).then_inc(s["weights_in"], 16)
                sp.dma_start(eb2r[:, :], eb2).then_inc(s["weights_in"], 16)
                n += 6
            assert n == WEIGHT_LOADS
            sp.wait_ge(s["consts"], N_CONSTS)
            for table, b in ((xn_d, W), (h1_d, 0), (h1_d, W + 1), (h2_d, W + 1), (x1_d, W), (r_d, 0)):
                sp.dma_start(rows(table, b), zero_tile[:, :]).then_inc(s["blank_out"], 16)

            def tile(t, b):
                r0 = sp.snap(t * P) if not isinstance(t, int) else t * P
                sp.wait_ge(s["xn_done"], t + 1)
                sp.dma_start(xn_d[bass.ds(r0, P), :], t_b[b][:, :]).then_inc(s[f"xn_out{b}"], 16)

            tile(0, 0)
            with sp.Fori(0, (W - 1) // 2) as p:
                tile(2 * p + 1, 1)
                tile(2 * p + 2, 0)
            sp.wait_ge(s["dis_set"], 1)
            for q in range(Q):
                sp.dma_start(dis[q * QN:(q + 1) * QN, 1:W + 1], dis_q[:, q, :]).then_inc(s["dis_in"], 16)
            for n in range(W // XG):
                mine = n % 2 == 0
                g = n // 2 if mine else H_ACT // XG + n // 2
                sp.wait_ge(s["h_dve" if mine else "h_act"], (n // 2 + 1) * XG)
                sp.dma_start(h1_d[(g * XG + 1) * P:((g + 1) * XG + 1) * P, :].rearrange("(t p) d -> p t d", p=P),
                             xh[:, g * XG:(g + 1) * XG, :]).then_inc(s["h1_out"], 16)

            sp.wait_ge(s["blank_out"], 16 * 6)
            sp.wait_ge(s["kv_acc"], W)
            sp.wait_ge(s["h1_out"], 16 * (W // XG))
            for b in range(2):
                sp.wait_ge(s[f"xn_out{b}"], 16 * ((W + 1 - b) // 2))
            sp.sem_inc(s["table1"], 1)
            sp.dma_start(hself[:, :], rows(h1_d, 1)).then_inc(s["self_in"], 16)
            sp.dma_start(u1[:, :], rows(xn_d, 0)).then_inc(s["xn_in"], 16)
            with sp.Fori(0, W) as w:
                here, after, after2 = sp.snap(w * P), sp.snap((w + 1) * P), sp.snap((w + 2) * P)
                piece = sp.snap(w * EW_STEP)
                sp.wait_ge(s["ew_low"], w)
                sp.dma_start(ew_in[:, :], eW[:, bass.ds(piece, EW_STEP)]).then_inc(s["experts_in"], 16)
                sp.wait_ge(s["self_used"], w + 1)
                sp.dma_start(hself[:, :], h1_d[bass.ds(after2, P), :]).then_inc(s["self_in"], 16)
                sp.wait_ge(s["r_done"], w)
                sp.dma_start(u2[:, :], x[bass.ds(here, P), :]).then_inc(s["x_again"], 16)
                sp.wait_ge(s["xn1_tp"], w + 1)
                sp.wait_ge(s["xn_kept"], w + 1)
                sp.dma_start(u1[:, :], xn_d[bass.ds(after, P), :]).then_inc(s["xn_in"], 16)
                sp.wait_ge(s["h2_done"], w + 1)
                sp.dma_start(h2_d[bass.ds(here, P), :], u4[:, :]).then_inc(s["h2_out"], 16)
                sp.wait_ge(s["x1_done"], w + 1)
                sp.dma_start(x1_d[bass.ds(here, P), :], u5[:, :]).then_inc(s["x1_out"], 16)
                sp.wait_ge(s["r_done"], w + 1)
                sp.dma_start(r_d[bass.ds(after, P), :], u6[:, :]).then_inc(s["r_out"], 16)
            sp.wait_ge(s["h2_done"], W + 1)
            sp.dma_start(rows(h2_d, W), u4[:, :]).then_inc(s["h2_out"], 16)

            sp.wait_ge(s["h2_out"], 16 * (W + 1))
            sp.wait_ge(s["x1_out"], 16 * W)
            sp.wait_ge(s["r_out"], 16 * W)
            sp.wait_ge(s["self_in"], 16 * (W + 1))
            sp.wait_ge(s["xn_in"], 16 * (W + 1))
            sp.wait_ge(s["xn1_tp"], W + 1)
            sp.sem_inc(s["table2"], 1)
            sp.dma_start(hself[:, :], rows(h2_d, 1)).then_inc(s["self2_in"], 16)
            sp.dma_start(u1[:, :], rows(x1_d, 0)).then_inc(s["x1_in"], 16)

            def out_tile(w):
                sp.wait_ge(s["facc"], (NE + 1) * (w + 1))
                sp.dma_start(rows(out, w), u8[:, :]).then_inc(s["out_stored"], 16)

            def r_tile(w):
                sp.wait_ge(s["x3_done"], w)
                sp.dma_start(u2[:, :], rows(r_d, w)).then_inc(s["r_in"], 16)

            with sp.Fori(0, W) as w:
                here, nxt, nxt2 = sp.snap(w * P), sp.snap((w + 1) * P), sp.snap((w + 2) * P)
                sp.wait_ge(s["x3_done"], w)
                sp.dma_start(u2[:, :], r_d[bass.ds(here, P), :]).then_inc(s["r_in"], 16)
                sp.wait_ge(s["acc2_read"], w + 1)
                sp.dma_start(hself[:, :], h2_d[bass.ds(nxt2, P), :]).then_inc(s["self2_in"], 16)
                sp.wait_ge(s["x2_done"], w + 2)
                sp.dma_start(u1[:, :], x1_d[bass.ds(nxt, P), :]).then_inc(s["x1_in"], 16)
                sp.wait_ge(s["facc"], (NE + 1) * (w + 1))
                sp.dma_start(out[bass.ds(here, P), :], u8[:, :]).then_inc(s["out_stored"], 16)
            r_tile(W)
            out_tile(W)
            out_tile(W + 1)
            sp.wait_ge(s["out_stored"], 16 * (W + 2))
            sp.wait_ge(s["self2_in"], 16 * (W + 1))
            sp.wait_ge(s["x1_in"], 16 * (W + 1))

        @block.gpsimd
        def _(pool):
            c = s["consts"]
            n = 0

            def const(ins):
                nonlocal n
                n += 1
                ins.then_inc(c, 1)

            const(pool.memset(ident[:, :], 0.0))
            const(pool.memset(ones_row[:, :], 1.0))
            const(pool.memset(zero_tile[:, :], 0.0))
            const(pool.memset(headmask[:, :], 1.0))
            const(pool.memset(valid[:, :], 1.0))
            const(pool.memset(lowtri[:, :, :], 1.0))
            const(pool.iota(iota_p[:, :], [[1, P]], channel_multiplier=0, allow_small_or_imprecise_dtypes=True))
            const(pool.iota(iota_q[:, :], [[1, Q * W]], channel_multiplier=0, allow_small_or_imprecise_dtypes=True))
            const(pool.memset(win_first[:, W:W + 1], 0.0))
            const(pool.iota(win_first[:, 0:W], [[P, W]], channel_multiplier=0, allow_small_or_imprecise_dtypes=True))
            const(pool.iota(chunk_id[:, :], [[P, RB]], channel_multiplier=1, allow_small_or_imprecise_dtypes=True))
            pool.wait_ge(c, n)
            const(pool.affine_select(out=ident[:, :], in_=ident[:, :], compare_op=ALU.not_equal, fill=1.0, base=0,
                                     pattern=[[-1, P]], channel_multiplier=1))
            const(pool.affine_select(out=valid[:, :], in_=valid[:, :], compare_op=ALU.is_ge, fill=0.0,
                                     base=N_NODES - 1, pattern=[[-P, W]], channel_multiplier=-1))
            const(pool.affine_select(out=headmask[:, :], in_=headmask[:, :], compare_op=ALU.is_ge, fill=0.0,
                                     base=0, pattern=[[-HD, HPB]], channel_multiplier=1))
            const(pool.affine_select(out=lowtri[:, :, :], in_=lowtri[:, :, :], compare_op=ALU.is_ge, fill=0.0,
                                     base=-1, pattern=[[1, NE], [-1, NE]], channel_multiplier=0))
            pool.wait_ge(c, n)
            const(pool.affine_select(out=headmask[:, :], in_=headmask[:, :], compare_op=ALU.is_ge, fill=0.0,
                                     base=HD - 1, pattern=[[HD, HPB]], channel_multiplier=-1))
            assert n == N_CONSTS
            pool.wait_ge(s["range_parts"], 2)
            pool.partition_all_reduce(range_all, range_part, P, bass.bass_isa.ReduceOp.max).then_inc(s["range_max"], 1)
            def gathers(layer, table):
                pool.wait_ge(s[f"table{layer + 1}"], 1)

                def groups(w, some):
                    for n in range(some.start * U, some.stop * U):
                        slot = n % SLOTS
                        if n % U == 0:
                            pool.wait_ge(s["idx_set"], layer * W * STATIC + w * STATIC + n + U)
                            pool.sem_inc(s["pool_gate"], 1)
                        pool.indirect_dma_start(
                            gs[:, slot, :], None, table[:, :],
                            bass.IndirectOffsetOnAxis(ap=idx_s[:, slot:slot + 1], axis=0)).then_inc(s[f"main_in{slot}"], 16)

                def rest(n_rest, base):
                    with pool.Fori(0, n_rest, RU) as i:
                        pool.wait_ge(s["idx_rest_set"], base + i + RU)
                        pool.sem_inc(s["pool_gate"], 1)
                        for j in range(RU):
                            pool.indirect_dma_start(
                                gr[:, j, :], None, table[:, :],
                                bass.IndirectOffsetOnAxis(ap=idx_r[:, j:j + 1], axis=0)).then_inc(s[f"rest_in{j}"], 16)

                groups(0, range(0, EARLY))
                with pool.Fori(0, W - 1) as w:
                    groups(w, range(EARLY, PIECES))
                    ranges = rest_table(pool, layer, w)
                    groups(w + 1, range(0, EARLY))
                    rest(*ranges)
                groups(W - 1, range(EARLY, PIECES))
                rest(*rest_table(pool, layer, W - 1))

            pool.wait_ge(s["tab_set"], 7)
            gathers(0, h1_d)
            gathers(1, h2_d)

        @block.scalar
        def _(act):
            act.wait_ge(s["consts"], N_CONSTS)

            def xn_tile(t, b, p):
                act.wait_ge(s[f"xn_out{b}"], 16 * p)
                act.wait_ge(s["xn_tp"], t)
                act.activation(t_b[b][:, :], xh[:, bass.ds(t, 1), :], ACT.Identity, scale=rstd_all[:, bass.ds(t, 1)],
                               bias=shift_all[:, bass.ds(t, 1)]).then_inc(s["xn_done"], 1)

            def turned(t):
                act.wait_ge(s["xn_tp"], t + 1)
                act.wait_ge(s["h_ps"], t)
                act.copy(xT[:, :, :], half(1)).then_inc(s["xT_set"], 1)

            def key_value(t):
                act.wait_ge(s["k_min"], t + 1)
                act.wait_ge(s["k_done"], t)
                act.activation(u3[:, :], u2[:, :], ACT.Exp).then_inc(s["k_exp"], 1)
                act.wait_ge(s["v_ps"], t + 1)
                act.wait_ge(s["kv_acc"], t)
                act.activation(vx[:, :, 0:P], half(4), ACT.Copy, scale=valid[:, bass.ds(t, 1)])
                act.copy(vx[:, :, P:P + 1], valid[:, bass.ds(t, 1)].unsqueeze(1).to_broadcast([P, KB, 1])
                         ).then_inc(s["v_set"], 1)

            act.wait_ge(s["stats_set"], 1)
            xn_tile(0, 0, 0)
            turned(0)
            with act.Fori(0, (W - 1) // 2) as p:
                xn_tile(2 * p + 1, 1, p)
                key_value(2 * p)
                turned(2 * p + 1)
                xn_tile(2 * p + 2, 0, p + 1)
                key_value(2 * p + 1)
                turned(2 * p + 2)
            key_value(W - 1)
            act.wait_ge(s["dis_in"], 16 * Q)
            act.wait_ge(s["h_set"], W)
            with act.Fori(H_ACT, W) as t:
                act.activation(xh[:, bass.ds(t, 1), :], xh[:, bass.ds(t, 1), :], ACT.Copy,
                               scale=dis[:, bass.ds(t + 1, 1)]).then_inc(s["h_act"], 1)

            def next_h(w):
                act.wait_ge(s["z1_tp"], w + 1)
                act.wait_ge(s["h7_ps"], w)
                act.copy(zT[:, :, :], half(1)).then_inc(s["z1T_set"], 1)

            def next_h_scaled(w):
                act.wait_ge(s["h7_ps"], w + 1)
                act.wait_ge(s["h2_out"], 16 * w)
                act.activation(u4[:, :], wide(7), ACT.Copy, scale=dis[:, bass.ds(w, 1)]).then_inc(s["h2_done"], 1)

            with act.Fori(0, W) as w:
                act.wait_ge(s["xn1_tp"], w + 1)
                act.wait_ge(s["hh_ps"], w)
                act.copy(xT[:, :, :], half(5)).then_inc(s["xn1T_set"], 1)
                act.wait_ge(s["q_min"], w + 1)
                act.activation(t_a[1][:, :], t_a[0][:, :], ACT.Exp).then_inc(s["q_exp"], 1)
                act.wait_ge(s["x1_done"], w)
                act.copy(xn_keep[:, :], u1[:, :]).then_inc(s["xn_kept"], 1)
                act.wait_ge(s["experts_in"], 16 * (w + 1))
                act.activation(ew_part[0][:, bass.ds(w * EW_STEP, EW_STEP)], ew_in[:, :], ACT.Copy,
                               scale=W_UP).then_inc(s["ew_high"], 1)
                next_h(w)
                act.wait_ge(s["msg_tp"], w + 1)
                act.wait_ge(s["m_ps"], w)
                act.copy(mT[:, :, :], half(5)).then_inc(s["msgT_set"], 1)
                next_h_scaled(w)
                act.wait_ge(s["mn_tp"], w + 1)
                act.copy(nT[:, :, :], half(5)).then_inc(s["mnT_set"], 1)
                act.wait_ge(s["hh_ps"], w + 1)
                act.wait_ge(s["y1_ps"], w)
                for j in range(HBLK):
                    act.activation(hT[0][:, j, :], bank[6][:, j * P:(j + 1) * P], ACT.Relu,
                                   bias=w1bias[:, j:j + 1]).then_inc(s["hr_done"], 1)
            next_h(W)
            next_h_scaled(W)

            act.wait_ge(s["zn_blank"], 1)
            act.wait_ge(s["y1_ps"], W)

            def window2(w, epilogue=True):
                act.wait_ge(s["zn_set"], w)
                act.wait_ge(s["hid_ps"], NE * w)
                act.activation(nT_part[0][:, :, :], zT[:, :, :], ACT.Copy, scale=Z_UP).then_inc(s["zc_high"], 1)
                if epilogue:
                    act.wait_ge(s["x2_tp"], w + 1)
                    act.wait_ge(s["p_ps"], w)
                    act.copy(xT[:, :, :], half(1)).then_inc(s["x2T_set"], 1)
                for e in range(NE):
                    if epilogue and e == 3:
                        act.wait_ge(s["z3_tp"], w + 1)
                        act.wait_ge(s["zc_set"], w + 1)
                        act.copy(zT[:, :, :], half(1)).then_inc(s["zn_set"], 1)
                    if epilogue and e == 5:
                        act.wait_ge(s["mt_ps"], w + 1)
                        act.wait_ge(s["b2_ps"], w)
                        act.copy(maskT[:, :], bank[3][0:NE, P // 2:P // 2 + P]).then_inc(s["maskT_set"], 1)
                    act.wait_ge(s["hid_ps"], NE * w + e + 1)
                    act.wait_ge(s["y_ps"], NE * w + e + 1)
                    for j in range(HBLK):
                        act.activation(hT[e % 2][:, j, :], bank[(6, 2)[e % 2]][:, j * P:(j + 1) * P], ACT.Gelu,
                                       scale=1.0 / (Z_UP * W_UP), bias=eb1c[:, e, j:j + 1]).then_inc(s["gelu_done"], 1)
                    act.wait_ge(s["gelu_done"], HBLK * (NE * w + e + 1))
                    act.activation(hT_part[e % 2][0][:, :, :], hT[e % 2][:, :, :], ACT.Copy,
                                   scale=H_UP).then_inc(s["h_high"], 1)

            with act.Fori(0, W) as w:
                window2(w)
            window2(W)
            window2(W + 1, epilogue=False)

        def inv_sqrt(dve, ch, v, minus_half, y, t):
            dve.tensor_scalar(minus_half, v, -0.5, None, ALU.mult)
            ch.link(dve.tensor_scalar(y.bitcast(I32), v.bitcast(I32), 1, None, ALU.arith_shift_right))
            ch.link(dve.tensor_scalar(y.bitcast(I32), y.bitcast(I32), -1.0, float(RSQRT_BITS), ALU.mult, ALU.add))
            for _ in range(NEWTON):
                ch.link(dve.tensor_tensor(t, y, y, ALU.mult))
                ch.link(dve.tensor_tensor(t, t, minus_half, ALU.mult))
                ch.link(dve.scalar_tensor_tensor(out=y, in0=t, scalar=1.5, in1=y, op0=ALU.add, op1=ALU.mult))

        def layer_norm(dve, ch, *tiles):
            n = len(tiles)
            for i, (xin, _) in enumerate(tiles):
                last = dve.bn_stats(st[:, 6 * i:6 * i + 6], xin)
            ch.link(last)
            dve.sem_inc(s["dve_gate"], 1)
            for i in range(n):
                last = dve.bn_aggr(mv[:, 2 * i:2 * i + 2], st[:, 6 * i:6 * i + 6])
            ch.link(last)
            var, minus_half, rs, tmp = (rstd[:, i * n:(i + 1) * n] for i in range(4))
            ch.link(dve.tensor_scalar(var, mv[:, 0:2 * n].rearrange("p (i a) -> p i a", a=2)[:, :, 1], EPS, None, ALU.add))
            inv_sqrt(dve, ch, var, minus_half, rs, tmp)
            return [dve.tensor_scalar(xout, xin, mv[:, 2 * i:2 * i + 1], rs[:, i:i + 1], ALU.subtract, ALU.mult)
                    for i, (xin, xout) in enumerate(tiles)]

        @block.vector
        def _(dve):
            ch = Chain(dve, s["dve_setup"], 0, 0)
            dve.wait_ge(s["consts"], N_CONSTS)
            dve.wait_ge(s["rows_in"], 16)
            ch.link(dve.tensor_copy(drow_f, drow_i))
            dve.tensor_reduce(cmin, drow_f, AX.X, ALU.min)
            ch.link(dve.tensor_reduce(cmax, drow_f, AX.X, ALU.max))
            wins = win_first[:, 0:W].unsqueeze(2).to_broadcast([P, W, RB])
            ch.link(dve.tensor_scalar(cmin, cmin, float(1 - P), None, ALU.add))
            dve.tensor_tensor(touch[0], wins, cmin.unsqueeze(1).to_broadcast([P, W, RB]), ALU.is_ge)
            ch.link(dve.tensor_tensor(touch[1], wins, cmax.unsqueeze(1).to_broadcast([P, W, RB]), ALU.is_le))
            ch.link(dve.tensor_tensor(touch[0], touch[0], touch[1], ALU.mult))
            ids = chunk_id[:, :].unsqueeze(1).to_broadcast([P, W, RB])
            ch.link(dve.tensor_tensor(touch[1], touch[0], ids, ALU.mult))
            ch.link(dve.tensor_tensor(touch[2], touch[1], touch[0], ALU.add))
            dve.tensor_reduce(range_part[:, W:2 * W], touch[2], AX.X, ALU.max).then_inc(s["range_parts"], 1)
            ch.link(dve.tensor_scalar(touch[0], touch[0], float(NCH), None, ALU.mult))
            ch.link(dve.tensor_tensor(touch[0], touch[0], touch[1], ALU.subtract))
            dve.tensor_reduce(range_part[:, 0:W], touch[0], AX.X, ALU.max).then_inc(s["range_parts"], 1)
            dve.wait_ge(s["edges_in"], 16 * 3)
            ints = wide_s.bitcast(I32)
            ch.link(dve.tensor_scalar(ints, dst_i, QN.bit_length() - 1, None, ALU.arith_shift_right))
            ch.link(dve.tensor_copy(dst_q, ints))
            ch.link(dve.tensor_scalar(ints, dst_i, QN - 1, None, ALU.bitwise_and))
            ch.link(dve.tensor_copy(dst_n, ints))
            ch.link(dve.tensor_copy(dst_f[:, :], dst_i))
            dve.tensor_scalar(src_row[:, :], src_row[:, :], P, None, ALU.add)
            ch.link(dve.tensor_copy(ew_parts[:, :, 0], ew[:, :]))
            ch.link(dve.tensor_tensor(wide_s, ew[:, :], ew_parts[:, :, 0], ALU.subtract))
            ch.link(dve.tensor_copy(ew_parts[:, :, 1], wide_s))
            ch.link(dve.tensor_tensor(wide_s, wide_s, ew_parts[:, :, 1], ALU.subtract))
            dve.tensor_copy(ew_parts[:, :, 2], wide_s)
            dve.tensor_copy(iota_qb[:, :], iota_q[:, :])
            ch.link(dve.tensor_copy(iota_nb[:, :], iota_p[:, 0:QN]))
            dve.wait_ge(s["range_max"], 1)
            first, ngr, rest, cum = rg[:, 0, :], rg[:, 1, :], rg[:, 2, :], rg[:, 3, :]
            ch.link(dve.tensor_scalar(first, range_all[0:1, 0:W], -1.0, float(NCH), ALU.mult, ALU.add))
            ch.link(dve.tensor_tensor(ngr, range_all[0:1, W:2 * W], first, ALU.subtract))
            ch.link(dve.tensor_scalar(rg_i[:, 0, :], ngr, float(RU - 1), 0.0, ALU.add, ALU.max))
            ch.link(dve.tensor_scalar(rg_i[:, 1, :], rg_i[:, 0, :], RU.bit_length() - 1, None, ALU.arith_shift_right))
            ch.link(dve.tensor_scalar(rest, rg_i[:, 1, :], float(STATIC // RU + 1), float(-STATIC // RU), ALU.max, ALU.add))
            step, a, b = 1, 2, 3
            while step < W:
                dve.tensor_copy(rg[:, b, 0:step], rg[:, a, 0:step])
                ch.link(dve.tensor_tensor(rg[:, b, step:W], rg[:, a, step:W], rg[:, a, 0:W - step], ALU.add))
                a, b, step = b, (4 if b == 3 else 3), 2 * step
            total = rg[:, a, :]
            dve.tensor_scalar(tab[:, 4, 0:W], rest, float(RU), None, ALU.mult).then_inc(s["tab_set"], 1)
            ch.link(dve.tensor_scalar(rg[:, 1, :], rest, float(RU), float(STATIC), ALU.mult, ALU.add))
            dve.tensor_copy(tab[:, 0, W:W + 1], first[:, 0:1])
            dve.tensor_copy(tab[:, 0, 0:W], first).then_inc(s["tab_set"], 1)
            dve.tensor_tensor(tab[:, 1, 0:W], first, rg[:, 1, :], ALU.add).then_inc(s["tab_set"], 1)
            ch.link(dve.tensor_tensor(rg[:, 5, :], total, rest, ALU.subtract))
            dve.tensor_scalar(tab[:, 5, 0:W], rg[:, 5, :], float(RU), None, ALU.mult).then_inc(s["tab_set"], 1)
            ch.link(dve.tensor_scalar(rg[:, 1, 0:1], total[:, W - 1:W], float(RU), None, ALU.mult))
            dve.tensor_scalar(tab[:, 6, 0:W], rg[:, 5, :], float(RU), rg[:, 1, 0:1], ALU.mult, ALU.add).then_inc(s["tab_set"], 1)
            ch.link(dve.tensor_scalar(rg[:, 5, :], rg[:, 5, :], float(RU), float(REST_FROM - STATIC), ALU.mult, ALU.add))
            ch.link(dve.tensor_tensor(rg[:, 5, :], rg[:, 5, :], first, ALU.subtract))
            dve.tensor_copy(tab[:, 2, 0:W], rg[:, 5, :]).then_inc(s["tab_set"], 1)
            dve.tensor_scalar(tab[:, 3, 0:W], rg[:, 5, :], rg[:, 1, 0:1], None, ALU.add).then_inc(s["tab_set"], 1)
            dve.wait_ge(s["weights_in"], 16 * WEIGHT_LOADS)
            dve.tensor_tensor(vec[:, 5, :], vec[:, 4, :], vec[:, 2, :], ALU.add)
            dve.wait_ge(s["shift_ps"], 3)
            dve.tensor_copy(hb[:, 0, :], bank[1][0:1, 0:D])
            dve.tensor_copy(hb[:, 1, :], bank[2][0:1, 0:D])
            dve.tensor_copy(w1bias[:, :], bank[3][:, 0:HBLK])
            for k in range(KB):
                dve.tensor_scalar(w6[:, k, :], w6[:, k, :], lncol[:, 0, k:k + 1], None, ALU.mult)
                dve.tensor_scalar(w7[:, k, :], w7[:, k, :], lncol[:, 2, k:k + 1], None, ALU.mult)
                last = dve.tensor_scalar(w1[:, KB + k, :], w1[:, KB + k, :], mixcol[:, 0, k:k + 1], None, ALU.mult)
            ch.link(last)
            dve.sem_inc(s["weights_set"], 1)

            dve.wait_ge(s["hb_ps"], 1)
            dve.tensor_copy(u8[:, :], wide(2))
            dve.wait_ge(s["x_in"], 16 * (W // XG))
            with dve.Fori(0, W // XG) as g:
                for i in range(XG):
                    dve.bn_stats(st_all[:, bass.ds(g * XG + i, 1), :].rearrange("p a b -> p (a b)"),
                                 xh[:, bass.ds(g * XG + i, 1), :].rearrange("p a b -> p (a b)")).then_inc(s["bn_all"], 1)
            dve.wait_ge(s["bn_all"], W)

            def stat(i):
                return st_all[:, :, i]

            dve.tensor_tensor(w_s1[:, :], stat(1), stat(4), ALU.subtract)
            dve.tensor_tensor(w_s2[:, :], stat(2), stat(5), ALU.add)
            ch.link(dve.tensor_tensor(mean_all[:, :], stat(1), stat(4), ALU.add))
            dve.tensor_scalar(mean_all[:, :], mean_all[:, :], 0.5, None, ALU.mult)
            ch.link(dve.scalar_tensor_tensor(out=w_s1[:, :], in0=w_s1[:, :], scalar=0.25, in1=w_s1[:, :], op0=ALU.mult,
                                             op1=ALU.mult))
            ch.link(dve.scalar_tensor_tensor(out=var_all[:, :], in0=w_s2[:, :], scalar=1.0 / D, in1=w_s1[:, :],
                                             op0=ALU.mult, op1=ALU.add))
            ch.link(dve.tensor_scalar(w_s1[:, :], var_all[:, :], EPS, None, ALU.add))
            inv_sqrt(dve, ch, w_s1[:, :], w_s2[:, :], rstd_all[:, :], w_s3[:, :])
            ch.link(dve.scalar_tensor_tensor(out=shift_all[:, :], in0=mean_all[:, :], scalar=-1.0, in1=rstd_all[:, :],
                                             op0=ALU.mult, op1=ALU.mult))
            dve.sem_inc(s["stats_set"], 1)
            ch.link(dve.tensor_tensor(w_s1[:, :], rstd_all[:, :], rstd_all[:, :], ALU.mult))
            ch.link(dve.tensor_tensor(w_s1[:, :], w_s1[:, :], var_all[:, :], ALU.mult))
            ch.link(dve.tensor_scalar(w_s1[:, :], w_s1[:, :], EPS, None, ALU.add))
            inv_sqrt(dve, ch, w_s1[:, :], w_s2[:, :], rstd2_all[:, :], w_s3[:, :])
            dve.wait_ge(s["tab_set"], 7)

            def degrees(t, b, lo, next_first=False):
                mine = iota_qb[:, bass.ds(t * Q, Q)]
                if not isinstance(t, int):
                    dve.wait_ge(s["deg_ps"], t - 1)
                dve.tensor_tensor(oh_q, dst_q[:, bass.ds(lo, STATIC)].unsqueeze(2).to_broadcast([P, STATIC, Q]),
                                  mine.unsqueeze(1).to_broadcast([P, STATIC, Q]), ALU.is_equal)
                dve.tensor_tensor(
                    oh_node[b], iota_nb[:, :].unsqueeze(1).to_broadcast([P, STATIC, QN]),
                    dst_n[:, bass.ds(lo, STATIC)].unsqueeze(2).to_broadcast([P, STATIC, QN]),
                    ALU.is_equal).then_inc(s["dve_deg"], 1)
                end, off = end_column(dve, 0, t)
                if next_first:
                    first = first_column(dve, t + 1)
                dve.wait_ge(s["dve_deg"], t + 1)
                dve.tensor_tensor(oh_w[b], oh_q.unsqueeze(2).to_broadcast([P, STATIC, PARTS, Q]),
                                  ew_parts[:, bass.ds(lo, STATIC), :].unsqueeze(3).to_broadcast([P, STATIC, PARTS, Q]),
                                  ALU.mult).then_inc(s["deg_set"], 1)
                return (lo, mine, end, off), first if next_first else None

            def degrees_rest(lo, mine, end, off):
                with dve.Fori(lo + STATIC, end, RU) as col0:
                    dve.wait_ge(s["deg_rest_used"], col0 + off + RU)
                    dve.tensor_tensor(ohr_q, dst_q[:, bass.ds(col0, RU)].unsqueeze(2).to_broadcast([P, RU, Q]),
                                      mine.unsqueeze(1).to_broadcast([P, RU, Q]), ALU.is_equal)
                    dve.tensor_tensor(
                        ohr_node, iota_nb[:, :].unsqueeze(1).to_broadcast([P, RU, QN]),
                        dst_n[:, bass.ds(col0, RU)].unsqueeze(2).to_broadcast([P, RU, QN]),
                        ALU.is_equal).then_inc(s["dve_deg_rest"], RU)
                    dve.wait_ge(s["dve_deg_rest"], col0 + off + RU)
                    dve.tensor_tensor(ohr_w, ohr_q.unsqueeze(2).to_broadcast([P, RU, PARTS, Q]),
                                      ew_parts[:, bass.ds(col0, RU), :].unsqueeze(3).to_broadcast([P, RU, PARTS, Q]),
                                      ALU.mult).then_inc(s["deg_rest_set"], RU)

            def degrees_read(t):
                dve.wait_ge(s["deg_ps"], t + 1)
                dve.tensor_reduce(deg_q[:, bass.ds(t * Q, Q)],
                                  bank[0][0:QN, 0:PARTS * Q].rearrange("p (a q) -> p q a", a=PARTS), AX.X,
                                  ALU.add).then_inc(s["deg_read"], 1)

            def keys_low(t):
                dve.wait_ge(s["k_ps"], t + 1)
                dve.wait_ge(s["k_exp"], t)
                dve.tensor_scalar(u2[:, :], wide(3), 0.0, None, ALU.min).then_inc(s["k_min"], 1)

            def keys(t):
                dve.wait_ge(s["h_ps"], t + 1)
                dve.scalar_tensor_tensor(out=xh[:, bass.ds(t, 1), :].rearrange("p a b -> p (a b)"), in0=wide(7),
                                         scalar=rstd2_all[:, bass.ds(t, 1)], in1=u8[:, :], op0=ALU.mult,
                                         op1=ALU.add).then_inc(s["h_set"], 1)
                dve.wait_ge(s["k_exp"], t + 1)
                dve.wait_ge(s["kv_acc"], t)
                dve.scalar_tensor_tensor(out=u1[:, :], in0=wide(3), scalar=0.0, in1=u3[:, :], op0=ALU.max,
                                         op1=ALU.add).then_inc(s["k_done"], 1)

            degrees_rest(*degrees(0, 0, first_column(dve, 0))[0])
            degrees_read(0)
            with dve.Fori(0, (W - 1) // 2) as p:
                first = first_column(dve, 2 * p + 1)
                for b in (1, 0):
                    t = 2 * p + (1 - b)
                    following, first = degrees(t + 1, b, first, next_first=b == 1)
                    keys_low(t)
                    degrees_rest(*following)
                    keys(t)
                    degrees_read(t + 1)
            keys_low(W - 1)
            keys(W - 1)
            dve.wait_ge(s["deg_read"], W)
            n = Q * W
            deg, pos, y, t1, t2 = (v[0:QN, 0:n] for v in (u5, u6, u7, t_c[0], t_c[1]))
            ch.link(dve.tensor_scalar(deg, deg_q[:, :], 1.0, None, ALU.add))
            ch.link(dve.tensor_scalar(pos, deg, 0.0, None, ALU.is_gt))
            ch.link(dve.tensor_scalar(deg, deg, float(np.finfo(np.float32).tiny), None, ALU.max))
            inv_sqrt(dve, ch, deg, t1, y, t2)
            dve.memset(dis[:, 0:1], 0.0)
            dve.tensor_tensor(dis_q[:, :, :].rearrange("p q w -> p w q"), y.rearrange("p (w q) -> p w q", q=Q),
                              pos.rearrange("p (w q) -> p w q", q=Q), ALU.mult).then_inc(s["dis_set"], 1)
            dve.wait_ge(s["dis_in"], 16 * Q)
            dve.wait_ge(s["h_set"], W)
            with dve.Fori(0, H_ACT) as t:
                row = xh[:, bass.ds(t, 1), :].rearrange("p a b -> p (a b)")
                dve.tensor_scalar(row, row, dis[:, bass.ds(t + 1, 1)], None, ALU.mult).then_inc(s["h_dve"], 1)
            dve.wait_ge(s["kv_acc"], W)
            for k in range(KB):
                dve.tensor_tensor(kvx[:, k, 0:P].rearrange("p (h d) -> p h d", h=HPB),
                                  bank[5 + k][:, 0:P].rearrange("p (h d) -> p h d", h=HPB),
                                  headmask[:, :].unsqueeze(2).to_broadcast([P, HPB, HD]), ALU.mult)
                last = dve.tensor_scalar(kvx[:, k, P:P + HPB], headmask[:, :], bank[5 + k][:, P:P + 1], None, ALU.mult)
            last.then_inc(s["kvx_set"], 1)
            dve.memset(u3[:, :], 0.0).then_inc(s["z1_done"], 1)

            def scatter_group(v, k, first):
                dve.wait_ge(s["main_used"], v + k * U + U)
                slot = k * U % SLOTS
                dve.tensor_copy(idx_s[:, slot:slot + U], src_row[:, bass.ds(first + k * U, U)]).then_inc(s["idx_set"], U)
                for j in range(U):
                    c = first + (k * U + j)
                    m = dve.tensor_scalar(ss[:, slot + j, :], iw[:, :], dst_f[:, bass.ds(c, 1)],
                                          ew[:, bass.ds(c, 1)], ALU.is_equal, ALU.mult)
                m.then_inc(s["main_set"], U)

            def scatter_rest(lo, end, off):
                with dve.Fori(lo + STATIC, end, RU) as col0:
                    dve.wait_ge(s["rest_used"], col0 + off + RU)
                    dve.tensor_copy(idx_r[:, :], src_row[:, bass.ds(col0, RU)]).then_inc(s["idx_rest_set"], RU)
                    for j in range(RU):
                        m = dve.tensor_scalar(sr[:, j, :], iw_rest[:, :], dst_f[:, bass.ds(col0 + j, 1)],
                                              ew[:, bass.ds(col0 + j, 1)], ALU.is_equal, ALU.mult)
                    m.then_inc(s["rest_set"], RU)

            def set_window(layer, w, node_w):
                dve.tensor_scalar(iw[:, :], iota_p[:, :], win_first[:, bass.ds(node_w, 1)], None,
                                  ALU.add).then_inc(s["iw_set"], 1)
                dve.wait_ge(s["iw_set"], layer * W + w + 1)

            def set_rest(layer, w):
                dve.tensor_scalar(iw_rest[:, :], iota_p[:, :], win_first[:, bass.ds(w, 1)], None,
                                  ALU.add).then_inc(s["iw_rest_set"], 1)
                dve.wait_ge(s["iw_rest_set"], layer * W + w + 1)

            dve.wait_ge(s["tab_set"], 7)
            set_window(0, 0, 0)
            first = first_column(dve, 0)
            for k in range(5):
                scatter_group(0, k, first)
            def window1(w, last=False):
                tc = Chain(dve, s["dve_l1"], 2 * LN_LINKS + 6, w)
                lo = first_column(dve, w)
                v = w * STATIC
                for k in range(PIECES):
                    if k == 3:
                        end, off = end_column(dve, 0, w)
                        first, v_next = first_column(dve, w + 1), (w + 1) * STATIC
                    if k == 5:
                        dve.wait_ge(s["main_set"], v + STATIC)
                        set_window(0, w + 1, w + 1)
                        scatter_group(v_next, 0, first)
                        set_rest(0, w)
                        scatter_rest(lo, end, off)
                    if k == 6:
                        scatter_group(v_next, 1, first)
                    if k == 0:
                        dve.wait_ge(s["q_ps"], w + 1)
                        dve.tensor_scalar(t_a[0][:, :], wide(2), 0.0, None, ALU.min).then_inc(s["q_min"], 1)
                        dve.wait_ge(s["q_exp"], w + 1)
                        dve.wait_ge(s["nd_ps"], w)
                        dve.scalar_tensor_tensor(out=t_b[0][:, :], in0=wide(2), scalar=0.0, in1=t_a[1][:, :],
                                                 op0=ALU.max, op1=ALU.add).then_inc(s["q_done"], 1)
                    if k == 2:
                        dve.wait_ge(s["nd_ps"], w + 1)
                        nd = half(3, P + HPB)
                        tc.link(dve.tensor_scalar(zden[:, :, :], nd[:, :, P:P + HPB], ATT_EPS, None, ALU.add))
                        tc.link(dve.reciprocal(zrec[:, :, :], zden[:, :, :]))
                        dve.wait_ge(s["msg_tp"], w)
                        for kb in range(KB):
                            m = dve.tensor_tensor(
                                u8[:, kb * P:(kb + 1) * P].rearrange("p (h d) -> p h d", h=HPB),
                                nd[:, kb, 0:P].rearrange("p (h d) -> p h d", h=HPB),
                                zrec[:, kb, :].unsqueeze(2).to_broadcast([P, HPB, HD]), ALU.mult)
                        m.then_inc(s["msg_done"], 1)
                    if k == 4:
                        dve.wait_ge(s["m_ps"], w + 1)
                        layer_norm(dve, tc, (wide(4), u7[:, :]))[0].then_inc(s["mn_done"], 1)
                    if k == 6:
                        dve.wait_ge(s["x_again"], 16 * (w + 1))
                        dve.wait_ge(s["xn_kept"], w + 1)
                        tc.link(dve.tensor_tensor(t_c[0][:, :], xn_keep[:, :], u2[:, :], ALU.add))
                        tc.link(dve.tensor_tensor(t_c[0][:, :], t_c[0][:, :], vec[:, 5, :], ALU.add))
                    if k == 5:
                        piece = bass.ds(w * EW_STEP, EW_STEP)
                        dve.wait_ge(s["ew_high"], w + 1)
                        dve.scalar_tensor_tensor(out=ew_part[1][:, piece], in0=ew_in[:, :], scalar=W_UP,
                                                 in1=ew_part[0][:, piece], op0=ALU.mult,
                                                 op1=ALU.subtract).then_inc(s["ew_low"], 1)
                    if k + 5 < PIECES:
                        scatter_group(v, k + 5, lo)
                scatter_group(v_next, 2, first)
                dve.wait_ge(s["rest_used"], end + off + RU)
                dve.scalar_tensor_tensor(out=t_b[1][:, :], in0=acc, scalar=dis[:, bass.ds(w + 1, 1)], in1=vec[:, 0, :],
                                         op0=ALU.mult, op1=ALU.add).then_inc(s["acc_read"], 1)
                scatter_group(v_next, 3, first)
                dve.wait_ge(s["acc_read"], w + 1)
                dve.wait_ge(s["x1_out"], 16 * w)
                dve.scalar_tensor_tensor(out=u5[:, :], in0=t_b[1][:, :], scalar=0.0, in1=xn_keep[:, :], op0=ALU.max,
                                         op1=ALU.add).then_inc(s["x1_done"], 1)
                dve.wait_ge(s["x1_done"], w + 1)
                dve.wait_ge(s["z1_tp"], w + 1)
                dve.wait_ge(s["y1_ps"], w + 1)
                z_ins, y_ins = layer_norm(dve, tc, (u5[:, :], u3[:, :]), (wide(4), t_c[1][:, :]))
                z_ins.then_inc(s["z1_done"], 1)
                tc.link(y_ins)
                if not last:
                    scatter_group(v_next, 4, first)
                tc.link(dve.tensor_tensor(t_c[1][:, :], t_c[1][:, :], vec[:, 3, :], ALU.mult))
                dve.wait_ge(s["r_out"], 16 * w)
                dve.tensor_tensor(u6[:, :], t_c[1][:, :], t_c[0][:, :], ALU.add).then_inc(s["r_done"], 1)
                assert tc.n == tc.per, tc.n

            with dve.Fori(0, W - 1) as w:
                window1(w)
            window1(W - 1, last=True)

            dve.wait_ge(s["x1_out"], 16 * W)
            dve.wait_ge(s["r_out"], 16 * W)
            dve.wait_ge(s["h2_out"], 16 * (W + 1))
            dve.wait_ge(s["z1_tp"], W + 1)
            dve.wait_ge(s["h7_ps"], W + 1)
            dve.memset(u3[:, :], 0.0).then_inc(s["x2_done"], 1)
            dve.memset(u6[:, :], 0.0).then_inc(s["blank_set"], 1)
            dve.memset(mask_n[:, :], 0.0).then_inc(s["blank_set"], 1)
            dve.memset(zT[:, :, :], 0.0).then_inc(s["zn_blank"], 1)
            dve.wait_ge(s["blank_set"], 2)

            def add_expert(w, e):
                dve.wait_ge(s["y_ps"], NE * w + e + 1 + 2)
                dve.wait_ge(s["facc"], (NE + 1) * w + 1 + e)
                dve.scalar_tensor_tensor(out=u8[:, :], in0=wide((7, 5)[e % 2]), scalar=mask_c[:, e:e + 1], in1=u8[:, :],
                                         op0=ALU.mult, op1=ALU.add).then_inc(s["facc"], 1)

            def hidden_low(w, e):
                dve.wait_ge(s["h_high"], NE * w + e + 1)
                dve.scalar_tensor_tensor(out=hT_part[e % 2][1][:, :, :], in0=hT[e % 2][:, :, :], scalar=H_UP,
                                         in1=hT_part[e % 2][0][:, :, :], op0=ALU.mult,
                                         op1=ALU.subtract).then_inc(s["h_low"], 1)

            def window2(w, msgs=True, epilogue=True):
                dve.wait_ge(s["zc_high"], w + 1)
                dve.scalar_tensor_tensor(out=nT_part[1][:, :, :], in0=zT[:, :, :], scalar=Z_UP, in1=nT_part[0][:, :, :],
                                         op0=ALU.mult, op1=ALU.subtract).then_inc(s["zc_set"], 1)
                if msgs:
                    lo = first_column(dve, w)
                    v = (W + w) * STATIC
                dve.wait_ge(s["out_stored"], 16 * w)
                dve.wait_ge(s["x3b_done"], w)
                dve.tensor_scalar(mask_c[:, :], mask_n[:, :], 1.0 / (H_UP * W_UP), None, ALU.mult).then_inc(s["mask_set"], 1)
                dve.tensor_copy(u8[:, :], u6[:, :]).then_inc(s["facc"], 1)
                dve.wait_ge(s["mask_set"], w + 1)
                tc = Chain(dve, s["dve_l2"], LN_LINKS + 5, w)
                for k in range(PIECES):
                    if k:
                        hidden_low(w, k - 1)
                    if msgs and k == 6:
                        set_rest(1, w)
                        scatter_rest(lo, end, off)
                    if k > 1:
                        add_expert(w, k - 2)
                    if msgs and k + 4 < PIECES:
                        scatter_group(v, k + 4, lo)
                    if msgs and k == 3:
                        end, off = end_column(dve, 1, w)
                        first, v_next = first_column(dve, w + 1), (W + w + 1) * STATIC
                    if msgs and k == 3:
                        dve.wait_ge(s["self2_in"], 16 * (w + 1))
                        dve.scalar_tensor_tensor(out=hself[:, :], in0=hself[:, :], scalar=dis[:, bass.ds(w + 1, 1)],
                                                 in1=vec[:, 1, :], op0=ALU.mult, op1=ALU.add).then_inc(s["self2_done"], 1)
                    if msgs and k == 5:
                        dve.wait_ge(s["main_set"], v + STATIC)
                        set_window(1, w + 1, w + 1)
                        scatter_group(v_next, 0, first)
                    if msgs and k == 6:
                        scatter_group(v_next, 1, first)
                    if msgs and k == 7:
                        scatter_group(v_next, 2, first)
                    if epilogue and k == 1:
                        dve.wait_ge(s["p_ps"], w + 1)
                        dve.wait_ge(s["r_in"], 16 * (w + 1))
                        dve.tensor_tensor(u4[:, :], wide(4), u2[:, :], ALU.add).then_inc(s["x3_done"], 1)
                        dve.wait_ge(s["x3_done"], w + 1)
                        dve.wait_ge(s["z3_tp"], w)
                        layer_norm(dve, tc, (u4[:, :], u5[:, :]))[0].then_inc(s["z3_done"], 1)
                    if epilogue and k == 4:
                        dve.wait_ge(s["g_ps"], w + 1)
                        tc.link(dve.tensor_tensor(lg[:, :], bank[3][:, 0:NE], bgr[:, :], ALU.add))
                        mine = lg[:, :].unsqueeze(2).to_broadcast([P, NE, NE])
                        other = lg[:, :].unsqueeze(1).to_broadcast([P, NE, NE])
                        dve.tensor_tensor(cmp1[:, :, :], other, mine, ALU.is_gt)
                        tc.link(dve.tensor_tensor(cmp2[:, :, :], other, mine, ALU.is_equal))
                        tc.link(dve.tensor_tensor(cmp2[:, :, :], cmp2[:, :, :], lowtri[:, :, :], ALU.mult))
                        tc.link(dve.tensor_tensor(cmp1[:, :, :], cmp1[:, :, :], cmp2[:, :, :], ALU.add))
                        tc.link(dve.tensor_reduce(rank[:, :], cmp1[:, :, :], AX.X, ALU.add))
                        dve.tensor_scalar(mask_n[:, :], rank[:, :], 2.0, None, ALU.is_lt).then_inc(s["mask_done"], 1)
                    if epilogue and k == 6:
                        dve.wait_ge(s["b2_ps"], w + 1)
                        dve.wait_ge(s["facc"], (NE + 1) * w + 1)
                        dve.tensor_tensor(u6[:, :], wide(4), u4[:, :], ALU.add).then_inc(s["x3b_done"], 1)
                if epilogue:
                    assert tc.n == tc.per, tc.n
                hidden_low(w, NE - 1)
                add_expert(w, NE - 2)
                if msgs:
                    dve.wait_ge(s["rest_used"], end + off + RU)
                    dve.wait_ge(s["self2_done"], w + 1)
                    dve.scalar_tensor_tensor(out=u7[:, :], in0=acc, scalar=dis[:, bass.ds(w + 1, 1)], in1=hself[:, :],
                                             op0=ALU.mult, op1=ALU.add).then_inc(s["acc2_read"], 1)
                    scatter_group(v_next, 3, first)
                    dve.wait_ge(s["acc2_read"], w + 1)
                    dve.wait_ge(s["x1_in"], 16 * (w + 1))
                    dve.wait_ge(s["x2_tp"], w + 1)
                    dve.scalar_tensor_tensor(out=u3[:, :], in0=u7[:, :], scalar=0.0, in1=u1[:, :], op0=ALU.max,
                                             op1=ALU.add).then_inc(s["x2_done"], 1)
                add_expert(w, NE - 1)

            with dve.Fori(0, W) as w:
                window2(w)
            window2(W, msgs=False)
            window2(W + 1, msgs=False, epilogue=False)

        @block.tensor
        def _(pe):
            pe.sem_inc(s["main_used"], SLOTS)
            pe.sem_inc(s["rest_used"], REST_FROM + RU)
            pe.sem_inc(s["rest_set"], REST_FROM)
            pe.sem_inc(s["deg_rest_used"], REST_FROM + RU)
            pe.sem_inc(s["dve_deg_rest"], REST_FROM)
            pe.wait_ge(s["consts"], N_CONSTS)
            pe.wait_ge(s["weights_in"], 16 * WEIGHT_LOADS)

            def mm(out_ap, lhsT, rhs, first, last, **kw):
                return pe.matmul(out_ap, lhsT, rhs, start=first, stop=last, **kw)

            for i, wt in enumerate((w6, w7)):
                for k in range(KB):
                    m = mm(bank[1 + i][0:1, 0:D], lncol[:, 2 * i + 1, k:k + 1], wt[:, k, :], k == 0, k == KB - 1)
                m.then_inc(s["shift_ps"], 1)
            for j in range(HBLK):
                for k in range(KB):
                    m = mm(bank[3][:, j:j + 1], w1[:, KB + k, j * P:(j + 1) * P], mixcol[:, 1, k:k + 1], k == 0,
                           k == KB - 1)
            m.then_inc(s["shift_ps"], 1)

            for k in range(KB):
                mm(bank[5 + k][:, 0:P + 1], zero_tile[:, 0:P], zero_tile[:, 0:P + 1], True, True)
            pe.wait_ge(s["weights_set"], 1)
            mm(wide(2), ones_row[:, :], hb[:, 0, :], True, True).then_inc(s["hb_ps"], 1)

            def flip(b, src, done):
                for k in range(KB):
                    m = pe.transpose(half(b)[:, k, :], src[:, k * P:(k + 1) * P], ident[:, :])
                m.then_inc(done, 1)

            def by_rows(b, xt, wt, done, bias=None):
                if bias is not None:
                    mm(wide(b), ones_row[:, :], bias, True, False)
                for k in range(KB):
                    m = mm(wide(b), xt[:, k, :], wt[:, k, :], bias is None and k == 0, k == KB - 1)
                m.then_inc(done, 1)

            def turn(t, b):
                pe.wait_ge(s["xn_done"], t + 1)
                pe.wait_ge(s["xT_set"], t)
                flip(1, t_b[b], s["xn_tp"])

            def degrees(t, b):
                pe.wait_ge(s["deg_set"], t + 1)
                pe.wait_ge(s["deg_read"], t)
                for c in range(STATIC):
                    mm(bank[0][0:QN, 0:PARTS * Q], oh_node[b][:, c, :], oh_w[b][:, c, :, :].rearrange("p a q -> p (a q)"),
                       c == 0, True, skip_group_check=True)

            def degrees_rest(n, base):
                with pe.Fori(0, n, RU) as i:
                    pe.wait_ge(s["deg_rest_set"], base + i + RU)
                    for c in range(RU):
                        m = mm(bank[0][0:QN, 0:PARTS * Q], ohr_node[:, c, :],
                               ohr_w[:, c, :, :].rearrange("p a q -> p (a q)"), False, True, skip_group_check=True)
                    m.then_inc(s["deg_rest_used"], RU)
                mm(bank[2][0:1, 0:1], zero_tile[:, 0:1], zero_tile[:, 0:1], True, True).then_inc(s["deg_ps"], 1)

            def tile(t, following=True):
                pe.wait_ge(s["xT_set"], t + 1)
                pe.wait_ge(s["k_done"], t)
                by_rows(3, xT, wk, s["k_ps"])
                pe.wait_ge(s["v_set"], t)
                by_rows(4, xT, wv, s["v_ps"])
                ranges = rest_table(pe, 0, t + 1) if following else None
                pe.wait_ge(s["h_set"], t)
                by_rows(7, xT, w6, s["h_ps"])
                return ranges

            def kv(t):
                pe.wait_ge(s["k_done"], t + 1)
                pe.wait_ge(s["v_set"], t + 1)
                for k in range(KB):
                    m = mm(bank[5 + k][:, 0:P + 1], u1[:, k * P:(k + 1) * P], vx[:, k, :], False, True,
                           skip_group_check=True)
                m.then_inc(s["kv_acc"], 1)

            pe.wait_ge(s["tab_set"], 7)
            turn(0, 0)
            degrees(0, 0)
            degrees_rest(*rest_table(pe, 0, 0))
            with pe.Fori(0, (W - 1) // 2) as p:
                for b in (1, 0):
                    t = 2 * p + (1 - b)
                    ranges = tile(t)
                    turn(t + 1, b)
                    degrees(t + 1, b)
                    degrees_rest(*ranges)
                    kv(t)
            tile(W - 1, following=False)
            kv(W - 1)

            def messages(turn, v, k, fresh=False):
                pe.wait_ge(s["main_set"], v + k * U + U)
                for n in range(k * U, k * U + U):
                    pe.wait_ge(s[f"main_in{n % SLOTS}"], 16 * (turn * (STATIC // SLOTS) + n // SLOTS + 1))
                    mm(acc, ss[:, n % SLOTS, :], gs[:, n % SLOTS, :], fresh and n == 0, True,
                       skip_group_check=True).then_inc(s["main_used"], 1)

            def rest_messages(n, base):
                with pe.Fori(0, n, RU) as i:
                    pe.wait_ge(s["rest_set"], base + i + (REST_FROM + RU))
                    for j in range(RU):
                        pe.wait_ge(s[f"rest_in{j}"], (base + i) * (16 // RU) + 16)
                        mm(acc, sr[:, j, :], gr[:, j, :], False, True, skip_group_check=True).then_inc(s["rest_used"], 1)

            pe.wait_ge(s["kvx_set"], 1)
            pe.wait_ge(s["tab_set"], 7)

            def next_h_turn(w):
                pe.wait_ge(s["z1_done"], w + 1)
                pe.wait_ge(s["z1T_set"], w)
                flip(1, u3, s["z1_tp"])

            def next_h(w):
                pe.wait_ge(s["z1T_set"], w + 1)
                pe.wait_ge(s["h2_done"], w)
                by_rows(7, zT, w7, s["h7_ps"], bias=hb[:, 1, :])

            pe.wait_ge(s["xn_in"], 16)
            flip(5, u1, s["xn1_tp"])
            with pe.Fori(0, W) as w:
                v = w * STATIC
                pe.wait_ge(s["acc_read"], w)
                pe.wait_ge(s["self_in"], 16 * (w + 1))
                mm(acc, ident[:, :], hself[:, :], True, True).then_inc(s["self_used"], 1)
                for k in range(PIECES):
                    messages(w, v, k)
                    if k == 0:
                        pe.wait_ge(s["xn1T_set"], w + 1)
                        pe.wait_ge(s["q_done"], w)
                        for j in range(KB):
                            for i in range(KB):
                                m = mm(half(2)[:, j, :], wq[:, i, j * P:(j + 1) * P], xT[:, i, :], i == 0, i == KB - 1)
                        m.then_inc(s["q_ps"], 1)
                    if k == 2:
                        pe.wait_ge(s["q_done"], w + 1)
                        pe.wait_ge(s["msg_done"], w)
                        for j in range(KB):
                            m = mm(half(3, P + HPB)[:, j, :], t_b[0][:, j * P:(j + 1) * P], kvx[:, j, :], True, True)
                        m.then_inc(s["nd_ps"], 1)
                        next_h_turn(w)
                    if k == 3:
                        pe.wait_ge(s["msg_done"], w + 1)
                        flip(5, u8, s["msg_tp"])
                        next_h(w)
                    if k == 4:
                        pe.wait_ge(s["msgT_set"], w + 1)
                        pe.wait_ge(s["r_done"], w)
                        by_rows(4, mT, wm, s["m_ps"])
                    if k == 5:
                        pe.wait_ge(s["mn_done"], w + 1)
                        flip(5, u7, s["mn_tp"])
                    if k == 6:
                        pe.wait_ge(s["mnT_set"], w + 1)
                        pe.wait_ge(s["hr_done"], HBLK * w)
                        for j in range(HBLK):
                            for i in range(2 * KB):
                                m = mm(bank[6][:, j * P:(j + 1) * P], w1[:, i, j * P:(j + 1) * P],
                                       (xT if i < KB else nT)[:, i % KB, :], i == 0, i == 2 * KB - 1)
                        m.then_inc(s["hh_ps"], 1)
                        n_rest, base = rest_table(pe, 0, w)
                    if k == 7:
                        pe.wait_ge(s["xn_in"], 16 * (w + 2))
                        pe.wait_ge(s["mnT_set"], w + 1)
                        flip(5, u1, s["xn1_tp"])
                        pe.wait_ge(s["hr_done"], HBLK * (w + 1))
                        for i in range(HBLK):
                            m = mm(wide(4), hT[0][:, i, :], w2[:, i, :], i == 0, i == HBLK - 1)
                        m.then_inc(s["y1_ps"], 1)
                rest_messages(n_rest, base)
            next_h_turn(W)
            next_h(W)

            pe.sem_inc(s["y_ps"], 2)
            pe.wait_ge(s["ew_low"], W)
            pe.wait_ge(s["h2_done"], W + 1)

            def hidden(w, e):
                pe.wait_ge(s["zc_set"], w + 1)
                pe.wait_ge(s["gelu_done"], HBLK * (NE * w + max(e - 1, 0)))
                for j in range(HBLK):
                    for i in range(KB):
                        for a, b in HALVES:
                            m = mm(bank[(6, 2)[e % 2]][:, j * P:(j + 1) * P], ew1[a][:, e, i, j * P:(j + 1) * P],
                                   nT_part[b][:, i, :], i == 0 and (a, b) == HALVES[0],
                                   i == KB - 1 and (a, b) == HALVES[-1])
                m.then_inc(s["hid_ps"], 1)

            def expert_out(w, e):
                pe.wait_ge(s["h_low"], NE * w + e + 1)
                pe.wait_ge(s["facc"], (NE + 1) * w + (e if e >= 2 else 0))
                for i in range(HBLK):
                    for b, a in HALVES:
                        m = mm(wide((7, 5)[e % 2]), hT_part[e % 2][b][:, i, :], ew2[a][:, e, i, :],
                               i == 0 and (b, a) == HALVES[0], i == HBLK - 1 and (b, a) == HALVES[-1])
                m.then_inc(s["y_ps"], 1)

            def window2(w, msgs=True, epilogue=True):
                if msgs:
                    v = (W + w) * STATIC
                    pe.wait_ge(s["acc2_read"], w)
                for k in range(PIECES):
                    if msgs and k < 7:
                        messages(W + w, v, k, fresh=True)
                    if epilogue and k == 0:
                        pe.wait_ge(s["x2_done"], w + 1)
                        pe.wait_ge(s["zn_set"], w)
                        flip(1, u3, s["x2_tp"])
                    if epilogue and k == 1:
                        pe.wait_ge(s["x2T_set"], w + 1)
                        pe.wait_ge(s["x3b_done"], w)
                        by_rows(4, xT, wp, s["p_ps"])
                    if epilogue and k == 3:
                        pe.wait_ge(s["z3_done"], w + 1)
                        flip(1, u5, s["z3_tp"])
                    if epilogue and k == 4:
                        pe.wait_ge(s["zn_set"], w + 1)
                        pe.wait_ge(s["maskT_set"], w)
                        for i in range(KB):
                            m = mm(bank[3][:, 0:NE], zT[:, i, :], wg[:, i, :], i == 0, i == KB - 1)
                        m.then_inc(s["g_ps"], 1)
                    if epilogue and k == 5:
                        pe.wait_ge(s["mask_done"], w + 1)
                        pe.transpose(bank[3][0:NE, P // 2:P // 2 + P], mask_n[:, :], ident[:, :]).then_inc(s["mt_ps"], 1)
                    if epilogue and k == 6:
                        pe.wait_ge(s["maskT_set"], w + 1)
                        pe.wait_ge(s["x3_done"], w + 1)
                        mm(wide(4), maskT[:, :], eb2r[:, :], True, True).then_inc(s["b2_ps"], 1)
                    hidden(w, k)
                    if msgs and k == 7:
                        messages(W + w, v, k, fresh=True)
                        rest_messages(n_rest, base)
                    if k:
                        expert_out(w, k - 1)
                    if msgs and k == 6:
                        n_rest, base = rest_table(pe, 1, w)
                expert_out(w, NE - 1)

            with pe.Fori(0, W) as w:
                window2(w)
            window2(W, msgs=False)
            window2(W + 1, msgs=False, epilogue=False)


def kernel(**inputs):
    import concourse.bacc as bacc
    from concourse.bass_utils import run_bass_kernel_spmd

    a = {k: np.ascontiguousarray(v) for k, v in inputs.items()}
    src, dst, ew = a["src"], a["dst"], a["edge_weight"]

    def columns(e, **kw):
        return np.ascontiguousarray(np.pad(e, (0, NCOL * P - N_EDGES), **kw).reshape(NCOL, P).T)

    whole = np.pad(dst, (0, NCH * P - N_EDGES), mode="edge")
    dst_rows = np.pad(whole, (0, (RB - NCH // P) * P * P - NCH % P * P), constant_values=-1)
    dst_rows = np.ascontiguousarray(dst_rows.reshape(RB, P, P).transpose(1, 0, 2))

    def col(v):
        return np.ascontiguousarray(v.reshape(-1, P).T)

    g, m, f = "L0_gnn_", "L0_mix_", "L0_ffn_"
    experts = np.concatenate([a[f + n].reshape(NE, -1, P, c).transpose(2, 0, 1, 3).reshape(P, -1)
                              for n, c in (("W1", HID), ("W2", D))], axis=1)
    experts = np.pad(experts, ((0, 0), (0, W * EW_STEP - EW_COLS)))
    arrays = {
        "x": np.pad(a["x"], ((0, (W + 2) * P - N_NODES), (0, 0))),
        "src_cols": columns(src), "dst_cols": columns(dst, mode="edge"), "ew_cols": columns(ew), "dst_rows": dst_rows,
        "vecs": np.stack([a[g + "b6"], a[g + "b7"], a[g + "bp"], a[m + "g2"], a[m + "b2"]]),
        "W6T": np.ascontiguousarray(a[g + "W6"].T), "W7T": np.ascontiguousarray(a[g + "W7"].T),
        "WpT": np.ascontiguousarray(a[g + "Wp"].T),
        "Wq": a[m + "Wq"], "Wk": a[m + "Wk"], "Wv": a[m + "Wv"], "Wm": a[m + "Wm"], "W1": a[m + "W1"], "W2": a[m + "W2"],
        "ln_cols": np.ascontiguousarray(np.stack([col(a[g + n]) for n in ("ln6_g", "ln6_b", "ln7_g", "ln7_b")], 1)),
        "mix_cols": np.ascontiguousarray(np.stack([col(a[m + n]) for n in ("g1", "b1")], 1)),
        "Wg": a[f + "Wg"], "bg": a[f + "bg"].reshape(1, NE), "eW": experts,
        "eb1": np.ascontiguousarray(a[f + "b1"].reshape(NE, HBLK, P).transpose(2, 0, 1)),
        "eb2": a[f + "b2"],
    }
    nc = bacc.Bacc("TRN2", target_bir_lowering=False, num_devices=1)
    args = [nc.dram_tensor(f"in_{n}", v.shape, mybir.dt.from_np(v.dtype), kind="ExternalInput").ap()
            for n, v in arrays.items()]
    out = nc.dram_tensor("out", ((W + 2) * P, D), F32, kind="ExternalOutput").ap()
    gps_kernel(nc, *args, out)
    r = run_bass_kernel_spmd(nc, [{f"in_{n}": v for n, v in arrays.items()}], core_ids=[0])
    return r.results[0]["out"][2 * P:2 * P + N_NODES]
```
